# Optimizing a Trainium2 kernel written in Bass

```python
import numpy as np
import jax
import jax.numpy as jnp

def _softmax(x, axis=-1):
    return jax.nn.softmax(x, axis=axis)

def _gelu(x):
    return jax.nn.gelu(x, approximate=True)

def _silu(x):
    return jax.nn.silu(x)

def _sigmoid(x):
    return jax.nn.sigmoid(x)

def _layernorm(x, axis=-1, eps=1e-05):
    m = jnp.mean(x, axis=axis, keepdims=True)
    v = jnp.var(x, axis=axis, keepdims=True)
    return (x - m) / jnp.sqrt(v + eps)

def _scatter_add(tgt, idx, src, axis=0):
    return tgt.at[idx].add(src)

def _segment_sum(src, seg, n):
    return jax.ops.segment_sum(src, seg, n)
kernel_name = 'mk_vit_tower_cls_d4_tok_img256_r4_59f81b'

def setup_inputs(seed: int=0):
    np.random.seed(seed)
    _w = jnp.asarray

    def _rec_inputs():
        import jax
        import jax.numpy as jnp
        _rk = jax.random.key(seed)
        x = -7.10856e-05 + 0.999911 * jax.random.normal(jax.random.fold_in(_rk, 1), (16, 64, 64, 64), jnp.float32)
        cls_tok = 0.02 * jax.random.normal(jax.random.fold_in(_rk, 5), (1, 1, 64), jnp.float32)
        return (x, cls_tok)
    x, cls_tok = _rec_inputs()

    def _L0_tok_setup():
        import jax, jax.numpy as jnp
        import numpy as np
        GS = 8
        NH = 8
        DM = 64
        B, W, H = (4, 64, 64)
        key = jax.random.key(seed)
        ks = jax.random.split(key, 5)
        s = 0.02
        return {'x': jax.random.normal(ks[0], (B, DM, W, H), dtype=jnp.float32), 'Wq': jax.random.normal(ks[1], (DM, DM), dtype=jnp.float32) * s, 'bq': jnp.zeros((DM,), dtype=jnp.float32), 'Wk': jax.random.normal(ks[2], (DM, DM), dtype=jnp.float32) * s, 'bk': jnp.zeros((DM,), dtype=jnp.float32), 'Wv': jax.random.normal(ks[3], (DM, DM), dtype=jnp.float32) * s, 'bv': jnp.zeros((DM,), dtype=jnp.float32), 'Wo': jax.random.normal(ks[4], (DM, DM), dtype=jnp.float32) * s, 'bo': jnp.zeros((DM,), dtype=jnp.float32)}
    _L0_tok_all = _L0_tok_setup()
    _L0_tok_in = {k: v for k, v in _L0_tok_all.items() if k in ('Wq', 'bq', 'Wk', 'bk', 'Wv', 'bv', 'Wo', 'bo')}
    del _L0_tok_all

    def _L0_attn_setup():
        import jax, jax.numpy as jnp
        import numpy as np
        HEADS, DIM_HEAD = (8, 64)
        EPS = 1e-05

        def instance_norm(t):
            mu = jnp.mean(t, axis=-1, keepdims=True)
            var = jnp.mean((t - mu) ** 2, axis=-1, keepdims=True)
            return (t - mu) * jax.lax.rsqrt(var + EPS)
        key = jax.random.key(seed)
        k1, k2, k3, k4 = jax.random.split(key, 4)
        B, N, D = (8, 2048, 64)
        inner = HEADS * DIM_HEAD
        x = jax.random.normal(k1, (B, N, D), jnp.float32)
        w_qkv = jax.random.normal(k2, (3 * inner, D), jnp.float32) / np.sqrt(D).astype(np.float32)
        w_out = jax.random.normal(k3, (D, inner), jnp.float32) / np.sqrt(inner).astype(np.float32)
        b_out = 0.01 * jax.random.normal(k4, (D,), jnp.float32)
        return {'x': x, 'w_qkv': w_qkv, 'w_out': w_out, 'b_out': b_out}
    _L0_attn_all = _L0_attn_setup()
    _L0_attn_in = {k: v for k, v in _L0_attn_all.items() if k in ('w_qkv', 'w_out', 'b_out')}
    del _L0_attn_all

    def _L0_ffn_setup():
        import jax, jax.numpy as jnp
        import numpy as np
        B, A = (1024, 8)
        IN, OUT = (64, 64)
        SH1, SH2 = (64, 128)
        EH1, EH2 = (128, 64)
        E, TOPK = (4, 2)

        def _shared_mlp(x, W1, b1, W2, b2, W3, b3):
            h = jax.nn.relu(x @ W1 + b1)
            h = jax.nn.relu(h @ W2 + b2)
            return h @ W3 + b3

        def _experts_mlp(x, eW1, eb1, eW2, eb2, eW3, eb3):
            h = jax.nn.relu(jnp.einsum('baf,efh->ebah', x, eW1) + eb1[:, None, None, :])
            h = jax.nn.relu(jnp.einsum('ebah,ehg->ebag', h, eW2) + eb2[:, None, None, :])
            o = jnp.einsum('ebag,ego->ebao', h, eW3) + eb3[:, None, None, :]
            return jnp.moveaxis(o, 0, -1)
        key = jax.random.key(seed)
        ks = jax.random.split(key, 16)
        s = 0.05
        return {'x': jax.random.normal(ks[0], (B, A, IN), jnp.float32), 'sW1': jax.random.normal(ks[1], (IN, SH1), jnp.float32) * s, 'sb1': jnp.zeros((SH1,), jnp.float32), 'sW2': jax.random.normal(ks[2], (SH1, SH2), jnp.float32) * s, 'sb2': jnp.zeros((SH2,), jnp.float32), 'sW3': jax.random.normal(ks[3], (SH2, OUT), jnp.float32) * s, 'sb3': jnp.zeros((OUT,), jnp.float32), 'eW1': jax.random.normal(ks[4], (E, IN, EH1), jnp.float32) * s, 'eb1': jnp.zeros((E, EH1), jnp.float32), 'eW2': jax.random.normal(ks[5], (E, EH1, EH2), jnp.float32) * s, 'eb2': jnp.zeros((E, EH2), jnp.float32), 'eW3': jax.random.normal(ks[6], (E, EH2, OUT), jnp.float32) * s, 'eb3': jnp.zeros((E, OUT), jnp.float32), 'gW': jax.random.normal(ks[7], (IN, E), jnp.float32) * s, 'gb': jnp.zeros((E,), jnp.float32)}
    _L0_ffn_all = _L0_ffn_setup()
    _L0_ffn_in = {k: v for k, v in _L0_ffn_all.items() if k in ('sW1', 'sb1', 'sW2', 'sb2', 'sW3', 'sb3', 'eW1', 'eb1', 'eW2', 'eb2', 'eW3', 'eb3', 'gW', 'gb')}
    del _L0_ffn_all

    def _L1_attn_setup():
        import jax, jax.numpy as jnp
        import numpy as np
        import math
        NUM_HEADS = 8
        HEAD_SIZE = 32

        def get_alibi_slopes(n_heads):

            def pow2_slopes(n):
                start = 2.0 ** (-2.0 ** (-(math.log2(n) - 3)))
                ratio = start
                return [start * ratio ** i for i in range(n)]
            if math.log2(n_heads).is_integer():
                return np.array(pow2_slopes(n_heads), dtype=np.float32)
            cp2 = 2 ** math.floor(math.log2(n_heads))
            extra = pow2_slopes(2 * cp2)[0::2][:n_heads - cp2]
            return np.array(pow2_slopes(cp2) + extra, dtype=np.float32)
        ALIBI_SLOPES = jnp.asarray(get_alibi_slopes(NUM_HEADS))
        key = jax.random.key(seed)
        ks = jax.random.split(key, 6)
        B, T, C = (32, 128, 64)
        s = 1.0 / math.sqrt(C)
        return {'x': jax.random.normal(ks[0], (B, T, C), dtype=jnp.float32), 'Wq': jax.random.normal(ks[1], (C, NUM_HEADS * HEAD_SIZE), dtype=jnp.float32) * s, 'Wk': jax.random.normal(ks[2], (C, NUM_HEADS * HEAD_SIZE), dtype=jnp.float32) * s, 'Wv': jax.random.normal(ks[3], (C, NUM_HEADS * HEAD_SIZE), dtype=jnp.float32) * s, 'Wo': jax.random.normal(ks[4], (NUM_HEADS * HEAD_SIZE, C), dtype=jnp.float32) * s, 'bo': jax.random.normal(ks[5], (C,), dtype=jnp.float32) * 0.01}
    _L1_attn_all = _L1_attn_setup()
    _L1_attn_in = {k: v for k, v in _L1_attn_all.items() if k in ('Wq', 'Wk', 'Wv', 'Wo', 'bo')}
    del _L1_attn_all

    def _L1_ffn_setup():
        import jax, jax.numpy as jnp
        import numpy as np
        DIM = 64
        HEADS = 8
        NUM_KEYS = 64
        NUM_KV = NUM_KEYS ** 2
        PK_TOPK = 16
        FINAL_TOPK = 16
        DIM_KEY = DIM // 2
        P = 2

        def _pk(x, Wq_pk, pk_keys):
            b, n, _ = x.shape
            q = (x @ Wq_pk).reshape(b, n, P, HEADS, DIM_KEY).transpose(2, 0, 1, 3, 4)
            sim = jnp.einsum('pbnhd,pkhd->pbnhk', q, pk_keys)
            scores, idx = jax.lax.top_k(sim, PK_TOPK)
            idx0 = idx[0]
            idx1 = idx[1] * NUM_KEYS
            index = (idx0[..., :, None] + idx1[..., None, :]).reshape(b, n, HEADS, PK_TOPK * PK_TOPK)
            score = (scores[0][..., :, None] + scores[1][..., None, :]).reshape(b, n, HEADS, PK_TOPK * PK_TOPK)
            final_scores, pk_idx = jax.lax.top_k(score, FINAL_TOPK)
            final_indices = jnp.take_along_axis(index, pk_idx, axis=-1)
            final_scores = jax.nn.softmax(final_scores, axis=-1)
            return (final_scores, final_indices)
        key = jax.random.key(seed)
        ks = jax.random.split(key, 7)
        b, n = (2, 256)
        std = 0.02
        x = jax.random.normal(ks[0], (b, n, DIM), dtype=jnp.float32)
        Wq_pk = jax.random.normal(ks[1], (DIM, P * HEADS * DIM_KEY), dtype=jnp.float32) * std
        pk_keys = jax.random.normal(ks[2], (P, NUM_KEYS, HEADS, DIM_KEY), dtype=jnp.float32) * std
        Wq = jax.random.normal(ks[3], (DIM, HEADS * DIM), dtype=jnp.float32) * std
        keys_table = jax.random.normal(ks[4], (NUM_KV * HEADS, DIM), dtype=jnp.float32) * std
        values_table = jax.random.normal(ks[5], (NUM_KV * HEADS, DIM), dtype=jnp.float32) * std
        Wo = jax.random.normal(ks[6], (DIM * HEADS, DIM), dtype=jnp.float32) * std
        return {'x': x, 'Wq_pk': Wq_pk, 'pk_keys': pk_keys, 'Wq': Wq, 'keys_table': keys_table, 'values_table': values_table, 'Wo': Wo}
    _L1_ffn_all = _L1_ffn_setup()
    _L1_ffn_in = {k: v for k, v in _L1_ffn_all.items() if k in ('Wq_pk', 'pk_keys', 'Wq', 'keys_table', 'values_table', 'Wo')}
    del _L1_ffn_all

    def _L2_attn_setup():
        import jax, jax.numpy as jnp
        import numpy as np
        DIM = 64
        WS = 64
        H = 8
        HD = DIM // H
        SCALE = HD ** (-0.5)
        key = jax.random.key(seed)
        k1, k2, k3, k4 = jax.random.split(key, 4)
        B, L = (8, 4096)
        x = jax.random.normal(k1, (B, L, DIM), dtype=jnp.float32)
        w_qkv = jax.random.normal(k2, (3 * DIM, DIM), dtype=jnp.float32) * DIM ** (-0.5)
        w_proj = jax.random.normal(k3, (DIM, DIM), dtype=jnp.float32) * DIM ** (-0.5)
        b_proj = jnp.zeros((DIM,), dtype=jnp.float32)
        rel_bias = jax.random.normal(k4, (2 * WS - 1,), dtype=jnp.float32) * 0.02
        return {'x': x, 'w_qkv': w_qkv, 'w_proj': w_proj, 'b_proj': b_proj, 'rel_bias': rel_bias}
    _L2_attn_all = _L2_attn_setup()
    _L2_attn_in = {k: v for k, v in _L2_attn_all.items() if k in ('w_qkv', 'w_proj', 'b_proj', 'rel_bias')}
    del _L2_attn_all

    def _L2_ffn_setup():
        import jax, jax.numpy as jnp
        import numpy as np
        B, N, D = (16, 1024, 64)
        NUM_EXPERTS, TOP_K, HEADS = (4, 2, 4)
        N_EDGES = 262144
        LN_EPS = 1e-05

        def _layernorm(x, g, b):
            mu = x.mean(-1, keepdims=True)
            var = ((x - mu) ** 2).mean(-1, keepdims=True)
            return (x - mu) * jax.lax.rsqrt(var + LN_EPS) * g + b

        def _forward(x, edge_index, W_gat, att_src, att_dst, b_gat, ln_gamma, ln_beta, W1, b1, W2, b2):
            Bc, Nc, Dc = x.shape
            M = Bc * Nc
            x_flat = x.reshape(M, Dc)
            h = (x_flat @ W_gat).reshape(M, HEADS, NUM_EXPERTS)
            loops = jnp.arange(M, dtype=edge_index.dtype)
            src = jnp.concatenate([edge_index[0], loops])
            dst = jnp.concatenate([edge_index[1], loops])
            a_src = (h * att_src).sum(-1)
            a_dst = (h * att_dst).sum(-1)
            e = jax.nn.leaky_relu(a_src[src] + a_dst[dst], negative_slope=0.2)
            e_max = jax.ops.segment_max(e, dst, num_segments=M)
            ee = jnp.exp(e - e_max[dst])
            denom = jax.ops.segment_sum(ee, dst, num_segments=M)
            alpha = ee / (denom[dst] + 1e-16)
            msg = h[src] * alpha[:, :, None]
            agg = jax.ops.segment_sum(msg, dst, num_segments=M).reshape(M, HEADS * NUM_EXPERTS) + b_gat
            scores = _layernorm(agg, ln_gamma, ln_beta).reshape(M, HEADS, NUM_EXPERTS).mean(1)
            scores = scores.reshape(Bc, Nc, NUM_EXPERTS)
            topk_s, topk_i = jax.lax.top_k(scores, TOP_K)
            w = jax.nn.softmax(topk_s, axis=-1)
            out = jnp.zeros_like(x)
            for ei in range(NUM_EXPERTS):
                g = jnp.where(topk_i == ei, w, 0.0).sum(-1)
                hh = jax.nn.gelu(x @ W1[ei] + b1[ei], approximate=False)
                out = out + g[..., None] * (hh @ W2[ei] + b2[ei])
            return out
        key = jax.random.key(seed)
        ks = jax.random.split(key, 8)
        s = 0.05
        return {'x': jax.random.normal(ks[0], (B, N, D), jnp.float32), 'W_gat': jax.random.normal(ks[1], (D, HEADS * NUM_EXPERTS), jnp.float32) * s, 'att_src': jax.random.normal(ks[2], (HEADS, NUM_EXPERTS), jnp.float32) * s, 'att_dst': jax.random.normal(ks[3], (HEADS, NUM_EXPERTS), jnp.float32) * s, 'b_gat': jnp.zeros((HEADS * NUM_EXPERTS,), jnp.float32), 'ln_gamma': jnp.ones((HEADS * NUM_EXPERTS,), jnp.float32), 'ln_beta': jnp.zeros((HEADS * NUM_EXPERTS,), jnp.float32), 'W1': jax.random.normal(ks[4], (NUM_EXPERTS, D, 2 * D), jnp.float32) * s, 'b1': jnp.zeros((NUM_EXPERTS, 2 * D), jnp.float32), 'W2': jax.random.normal(ks[5], (NUM_EXPERTS, 2 * D, D), jnp.float32) * s, 'b2': jnp.zeros((NUM_EXPERTS, D), jnp.float32), 'edge_index': jax.random.randint(ks[6], (2, N_EDGES), 0, B * N, jnp.int32)}
    _L2_ffn_all = _L2_ffn_setup()
    _L2_ffn_in = {k: v for k, v in _L2_ffn_all.items() if k in ('W_gat', 'att_src', 'att_dst', 'b_gat', 'ln_gamma', 'ln_beta', 'W1', 'b1', 'W2', 'b2', 'edge_index')}
    del _L2_ffn_all

    def _L3_attn_setup():
        import jax, jax.numpy as jnp
        import numpy as np
        H, D = (8, 32)
        EPS = 1e-05
        key = jax.random.key(seed)
        ks = jax.random.split(key, 4)
        B, N, C = (2, 512, 64)
        inner = H * D
        return {'node_features': jax.random.normal(ks[0], (B, N, C), jnp.float32), 'ln_gamma': jnp.ones((C,), jnp.float32), 'ln_beta': jnp.zeros((C,), jnp.float32), 'W_qkv': jax.random.normal(ks[1], (3 * inner, C), jnp.float32) * 0.02, 'W_gate': jax.random.normal(ks[2], (inner, C), jnp.float32) * 0.02, 'b_gate': jnp.ones((inner,), jnp.float32), 'W_final': jax.random.normal(ks[3], (C, inner), jnp.float32) * 0.02, 'b_final': jnp.zeros((C,), jnp.float32)}
    _L3_attn_all = _L3_attn_setup()
    _L3_attn_in = {k: v for k, v in _L3_attn_all.items() if k in ('ln_gamma', 'ln_beta', 'W_qkv', 'W_gate', 'b_gate', 'W_final', 'b_final')}
    del _L3_attn_all

    def _L3_ffn_setup():
        import jax, jax.numpy as jnp
        import numpy as np
        B, T, C = (64, 96, 64)
        NH, NKV = (4, 2)
        HD = C // NH
        NREP = NH // NKV
        NE, TOPK = (8, 2)
        HID = int(8 / 3 * C)
        EPS_RMS = 1e-06

        def _rope_tables(t_len):
            inv_freq = 1.0 / 10000.0 ** (np.arange(0, HD, 2, dtype=np.float32) / HD)
            t = np.arange(t_len, dtype=np.float32)
            freqs = np.outer(t, inv_freq)
            emb = np.concatenate([freqs, freqs], axis=-1)
            return (jnp.asarray(np.cos(emb)), jnp.asarray(np.sin(emb)))

        def _rotate_half(x):
            h = x.shape[-1] // 2
            return jnp.concatenate([-x[..., h:], x[..., :h]], axis=-1)

        def _rmsnorm(v, w):
            return v * jax.lax.rsqrt(jnp.mean(v * v, axis=-1, keepdims=True) + EPS_RMS) * w
        key = jax.random.key(seed)
        ks = jax.random.split(key, 10)
        s = lambda k, shape: jax.random.normal(k, shape, jnp.float32) * 0.02
        return {'x': jax.random.normal(ks[0], (B, T, C), jnp.float32), 'ln1_w': jnp.ones((C,), jnp.float32), 'ln2_w': jnp.ones((C,), jnp.float32), 'wq': s(ks[1], (NH * HD, C)), 'wk': s(ks[2], (NKV * HD, C)), 'wv': s(ks[3], (NKV * HD, C)), 'wo': s(ks[4], (C, C)), 'router_w': s(ks[5], (NE, C)), 'w1': s(ks[6], (NE, HID, C)), 'w2': s(ks[7], (NE, C, HID)), 'w3': s(ks[8], (NE, HID, C))}
    _L3_ffn_all = _L3_ffn_setup()
    _L3_ffn_in = {k: v for k, v in _L3_ffn_all.items() if k in ('ln1_w', 'ln2_w', 'wq', 'wk', 'wv', 'wo', 'router_w', 'w1', 'w2', 'w3')}
    del _L3_ffn_all
    return {'x': x, 'cls_tok': cls_tok, 'L0_tok_Wq': _L0_tok_in['Wq'], 'L0_tok_bq': _L0_tok_in['bq'], 'L0_tok_Wk': _L0_tok_in['Wk'], 'L0_tok_bk': _L0_tok_in['bk'], 'L0_tok_Wv': _L0_tok_in['Wv'], 'L0_tok_bv': _L0_tok_in['bv'], 'L0_tok_Wo': _L0_tok_in['Wo'], 'L0_tok_bo': _L0_tok_in['bo'], 'L0_attn_w_qkv': _L0_attn_in['w_qkv'], 'L0_attn_w_out': _L0_attn_in['w_out'], 'L0_attn_b_out': _L0_attn_in['b_out'], 'L0_ffn_sW1': _L0_ffn_in['sW1'], 'L0_ffn_sb1': _L0_ffn_in['sb1'], 'L0_ffn_sW2': _L0_ffn_in['sW2'], 'L0_ffn_sb2': _L0_ffn_in['sb2'], 'L0_ffn_sW3': _L0_ffn_in['sW3'], 'L0_ffn_sb3': _L0_ffn_in['sb3'], 'L0_ffn_eW1': _L0_ffn_in['eW1'], 'L0_ffn_eb1': _L0_ffn_in['eb1'], 'L0_ffn_eW2': _L0_ffn_in['eW2'], 'L0_ffn_eb2': _L0_ffn_in['eb2'], 'L0_ffn_eW3': _L0_ffn_in['eW3'], 'L0_ffn_eb3': _L0_ffn_in['eb3'], 'L0_ffn_gW': _L0_ffn_in['gW'], 'L0_ffn_gb': _L0_ffn_in['gb'], 'L1_attn_Wq': _L1_attn_in['Wq'], 'L1_attn_Wk': _L1_attn_in['Wk'], 'L1_attn_Wv': _L1_attn_in['Wv'], 'L1_attn_Wo': _L1_attn_in['Wo'], 'L1_attn_bo': _L1_attn_in['bo'], 'L1_ffn_Wq_pk': _L1_ffn_in['Wq_pk'], 'L1_ffn_pk_keys': _L1_ffn_in['pk_keys'], 'L1_ffn_Wq': _L1_ffn_in['Wq'], 'L1_ffn_keys_table': _L1_ffn_in['keys_table'], 'L1_ffn_values_table': _L1_ffn_in['values_table'], 'L1_ffn_Wo': _L1_ffn_in['Wo'], 'L2_attn_w_qkv': _L2_attn_in['w_qkv'], 'L2_attn_w_proj': _L2_attn_in['w_proj'], 'L2_attn_b_proj': _L2_attn_in['b_proj'], 'L2_attn_rel_bias': _L2_attn_in['rel_bias'], 'L2_ffn_W_gat': _L2_ffn_in['W_gat'], 'L2_ffn_att_src': _L2_ffn_in['att_src'], 'L2_ffn_att_dst': _L2_ffn_in['att_dst'], 'L2_ffn_b_gat': _L2_ffn_in['b_gat'], 'L2_ffn_ln_gamma': _L2_ffn_in['ln_gamma'], 'L2_ffn_ln_beta': _L2_ffn_in['ln_beta'], 'L2_ffn_W1': _L2_ffn_in['W1'], 'L2_ffn_b1': _L2_ffn_in['b1'], 'L2_ffn_W2': _L2_ffn_in['W2'], 'L2_ffn_b2': _L2_ffn_in['b2'], 'L2_ffn_edge_index': _L2_ffn_in['edge_index'], 'L3_attn_ln_gamma': _L3_attn_in['ln_gamma'], 'L3_attn_ln_beta': _L3_attn_in['ln_beta'], 'L3_attn_W_qkv': _L3_attn_in['W_qkv'], 'L3_attn_W_gate': _L3_attn_in['W_gate'], 'L3_attn_b_gate': _L3_attn_in['b_gate'], 'L3_attn_W_final': _L3_attn_in['W_final'], 'L3_attn_b_final': _L3_attn_in['b_final'], 'L3_ffn_ln1_w': _L3_ffn_in['ln1_w'], 'L3_ffn_ln2_w': _L3_ffn_in['ln2_w'], 'L3_ffn_wq': _L3_ffn_in['wq'], 'L3_ffn_wk': _L3_ffn_in['wk'], 'L3_ffn_wv': _L3_ffn_in['wv'], 'L3_ffn_wo': _L3_ffn_in['wo'], 'L3_ffn_router_w': _L3_ffn_in['router_w'], 'L3_ffn_w1': _L3_ffn_in['w1'], 'L3_ffn_w2': _L3_ffn_in['w2'], 'L3_ffn_w3': _L3_ffn_in['w3']}

def reference(x, cls_tok, L0_tok_Wq, L0_tok_bq, L0_tok_Wk, L0_tok_bk, L0_tok_Wv, L0_tok_bv, L0_tok_Wo, L0_tok_bo, L0_attn_w_qkv, L0_attn_w_out, L0_attn_b_out, L0_ffn_sW1, L0_ffn_sb1, L0_ffn_sW2, L0_ffn_sb2, L0_ffn_sW3, L0_ffn_sb3, L0_ffn_eW1, L0_ffn_eb1, L0_ffn_eW2, L0_ffn_eb2, L0_ffn_eW3, L0_ffn_eb3, L0_ffn_gW, L0_ffn_gb, L1_attn_Wq, L1_attn_Wk, L1_attn_Wv, L1_attn_Wo, L1_attn_bo, L1_ffn_Wq_pk, L1_ffn_pk_keys, L1_ffn_Wq, L1_ffn_keys_table, L1_ffn_values_table, L1_ffn_Wo, L2_attn_w_qkv, L2_attn_w_proj, L2_attn_b_proj, L2_attn_rel_bias, L2_ffn_W_gat, L2_ffn_att_src, L2_ffn_att_dst, L2_ffn_b_gat, L2_ffn_ln_gamma, L2_ffn_ln_beta, L2_ffn_W1, L2_ffn_b1, L2_ffn_W2, L2_ffn_b2, L2_ffn_edge_index, L3_attn_ln_gamma, L3_attn_ln_beta, L3_attn_W_qkv, L3_attn_W_gate, L3_attn_b_gate, L3_attn_W_final, L3_attn_b_final, L3_ffn_ln1_w, L3_ffn_ln2_w, L3_ffn_wq, L3_ffn_wk, L3_ffn_wv, L3_ffn_wo, L3_ffn_router_w, L3_ffn_w1, L3_ffn_w2, L3_ffn_w3):
    import jax
    import jax.numpy as jnp

    def _L0_tok_ref(x, Wq, bq, Wk, bk, Wv, bv, Wo, bo):
        import jax, jax.numpy as jnp
        import numpy as np
        GS = 8
        NH = 8
        DM = 64
        B, W, H = (4, 64, 64)
        b, d, w, h = x.shape
        gw, gh = (w // GS, h // GS)
        n = gw * gh
        L = GS * GS
        dh = d // NH
        q = x.reshape(b, d, gw, GS, gh, GS).mean(axis=(3, 5))
        q = q.reshape(b, d, n).transpose(0, 2, 1).reshape(b * n, 1, d)
        kv = x.transpose(0, 2, 3, 1)
        kv = kv.reshape(b, gw, GS, gh, GS, d)
        kv = kv.transpose(0, 1, 3, 2, 4, 5).reshape(b * n, L, d)
        qp = (q @ Wq.T + bq).reshape(b * n, 1, NH, dh).transpose(0, 2, 1, 3)
        kp = (kv @ Wk.T + bk).reshape(b * n, L, NH, dh).transpose(0, 2, 1, 3)
        vp = (kv @ Wv.T + bv).reshape(b * n, L, NH, dh).transpose(0, 2, 1, 3)
        scores = jnp.einsum('bhqd,bhkd->bhqk', qp, kp) / jnp.sqrt(jnp.float32(dh))
        attn = jax.nn.softmax(scores, axis=-1)
        ctx = jnp.einsum('bhqk,bhkd->bhqd', attn, vp)
        ctx = ctx.transpose(0, 2, 1, 3).reshape(b * n, 1, d)
        attn_out = ctx @ Wo.T + bo
        out = q + attn_out
        return out.reshape(b, n, d)

    def _L0_attn_ref(x, w_qkv, w_out, b_out):
        import jax, jax.numpy as jnp
        import numpy as np
        HEADS, DIM_HEAD = (8, 64)
        EPS = 1e-05

        def instance_norm(t):
            mu = jnp.mean(t, axis=-1, keepdims=True)
            var = jnp.mean((t - mu) ** 2, axis=-1, keepdims=True)
            return (t - mu) * jax.lax.rsqrt(var + EPS)
        B, N, _ = x.shape
        H, Dh = (HEADS, DIM_HEAD)
        qkv = jnp.einsum('bnd,ed->bne', x, w_qkv)
        q, k, v = jnp.split(qkv, 3, axis=-1)

        def to_heads(t):
            return t.reshape(B, N, H, Dh).transpose(0, 2, 1, 3)
        q, k, v = (to_heads(q), to_heads(k), to_heads(v))
        k = instance_norm(k)
        v = instance_norm(v)
        dots = jnp.einsum('bhnd,bhne->bhde', k, v)
        out = jnp.einsum('bhnd,bhde->bhne', q, dots) / N
        out = out.transpose(0, 2, 1, 3).reshape(B, N, H * Dh)
        return jnp.einsum('bne,de->bnd', out, w_out) + b_out

    def _L0_ffn_ref(x, sW1, sb1, sW2, sb2, sW3, sb3, eW1, eb1, eW2, eb2, eW3, eb3, gW, gb):
        import jax, jax.numpy as jnp
        import numpy as np
        B, A = (1024, 8)
        IN, OUT = (64, 64)
        SH1, SH2 = (64, 128)
        EH1, EH2 = (128, 64)
        E, TOPK = (4, 2)

        def _shared_mlp(x, W1, b1, W2, b2, W3, b3):
            h = jax.nn.relu(x @ W1 + b1)
            h = jax.nn.relu(h @ W2 + b2)
            return h @ W3 + b3

        def _experts_mlp(x, eW1, eb1, eW2, eb2, eW3, eb3):
            h = jax.nn.relu(jnp.einsum('baf,efh->ebah', x, eW1) + eb1[:, None, None, :])
            h = jax.nn.relu(jnp.einsum('ebah,ehg->ebag', h, eW2) + eb2[:, None, None, :])
            o = jnp.einsum('ebag,ego->ebao', h, eW3) + eb3[:, None, None, :]
            return jnp.moveaxis(o, 0, -1)
        all_out = _experts_mlp(x, eW1, eb1, eW2, eb2, eW3, eb3)
        shared = _shared_mlp(x, sW1, sb1, sW2, sb2, sW3, sb3)
        gates = jax.nn.softmax(x @ gW + gb, axis=-1)
        topv, topi = jax.lax.top_k(gates, TOPK)
        topw = jax.nn.softmax(topv, axis=-1)
        sel = jnp.take_along_axis(all_out, topi[:, :, None, :], axis=-1)
        gated = jnp.sum(sel * topw[:, :, None, :], axis=-1)
        return shared + gated

    def _L1_attn_ref(x, Wq, Wk, Wv, Wo, bo):
        import jax, jax.numpy as jnp
        import numpy as np
        import math
        NUM_HEADS = 8
        HEAD_SIZE = 32

        def get_alibi_slopes(n_heads):

            def pow2_slopes(n):
                start = 2.0 ** (-2.0 ** (-(math.log2(n) - 3)))
                ratio = start
                return [start * ratio ** i for i in range(n)]
            if math.log2(n_heads).is_integer():
                return np.array(pow2_slopes(n_heads), dtype=np.float32)
            cp2 = 2 ** math.floor(math.log2(n_heads))
            extra = pow2_slopes(2 * cp2)[0::2][:n_heads - cp2]
            return np.array(pow2_slopes(cp2) + extra, dtype=np.float32)
        ALIBI_SLOPES = jnp.asarray(get_alibi_slopes(NUM_HEADS))
        B, T, C = x.shape
        H, D = (NUM_HEADS, HEAD_SIZE)
        q = (x @ Wq).reshape(B, T, H, D).transpose(0, 2, 1, 3)
        k = (x @ Wk).reshape(B, T, H, D).transpose(0, 2, 1, 3)
        v = (x @ Wv).reshape(B, T, H, D).transpose(0, 2, 1, 3)
        scale = 1.0 / math.sqrt(D)
        wei = jnp.einsum('bhtd,bhsd->bhts', q, k) * scale
        pos = jnp.arange(T)
        rel = (pos[None, :] - pos[:, None]).astype(jnp.float32)
        bias = ALIBI_SLOPES[:, None, None] * rel[None, :, :]
        wei = wei + bias[None]
        causal = pos[None, :] <= pos[:, None]
        wei = jnp.where(causal[None, None], wei, -jnp.inf)
        wei = jax.nn.softmax(wei, axis=-1)
        out = jnp.einsum('bhts,bhsd->bhtd', wei, v)
        out = out.transpose(0, 2, 1, 3).reshape(B, T, H * D)
        return out @ Wo + bo

    def _L1_ffn_ref(x, Wq_pk, pk_keys, Wq, keys_table, values_table, Wo):
        import jax, jax.numpy as jnp
        import numpy as np
        DIM = 64
        HEADS = 8
        NUM_KEYS = 64
        NUM_KV = NUM_KEYS ** 2
        PK_TOPK = 16
        FINAL_TOPK = 16
        DIM_KEY = DIM // 2
        P = 2

        def _pk(x, Wq_pk, pk_keys):
            b, n, _ = x.shape
            q = (x @ Wq_pk).reshape(b, n, P, HEADS, DIM_KEY).transpose(2, 0, 1, 3, 4)
            sim = jnp.einsum('pbnhd,pkhd->pbnhk', q, pk_keys)
            scores, idx = jax.lax.top_k(sim, PK_TOPK)
            idx0 = idx[0]
            idx1 = idx[1] * NUM_KEYS
            index = (idx0[..., :, None] + idx1[..., None, :]).reshape(b, n, HEADS, PK_TOPK * PK_TOPK)
            score = (scores[0][..., :, None] + scores[1][..., None, :]).reshape(b, n, HEADS, PK_TOPK * PK_TOPK)
            final_scores, pk_idx = jax.lax.top_k(score, FINAL_TOPK)
            final_indices = jnp.take_along_axis(index, pk_idx, axis=-1)
            final_scores = jax.nn.softmax(final_scores, axis=-1)
            return (final_scores, final_indices)
        b, n, d = x.shape
        q = (x @ Wq).reshape(b, n, HEADS, DIM) * DIM ** (-0.5)
        kv_scores, indices = _pk(x, Wq_pk, pk_keys)
        offsets = jnp.arange(HEADS, dtype=indices.dtype) * NUM_KV
        ind = indices + offsets[None, None, :, None]
        k = jnp.einsum('bnhk,bnhkd->bnhd', kv_scores, keys_table[ind])
        v = jnp.einsum('bnhk,bnhkd->bnhd', kv_scores, values_table[ind])
        sim = jnp.einsum('bihd,bjhd->bhij', q, k)
        neg = -jnp.finfo(sim.dtype).max
        causal = jnp.tril(jnp.ones((n, n), dtype=bool))
        sim = jnp.where(causal, sim, neg)
        attn = jax.nn.softmax(sim, axis=-1)
        out = jnp.einsum('bhij,bjhd->bhid', attn, v)
        out = out.transpose(0, 2, 1, 3).reshape(b, n, HEADS * DIM)
        return out @ Wo

    def _L2_attn_ref(x, w_qkv, w_proj, b_proj, rel_bias):
        import jax, jax.numpy as jnp
        import numpy as np
        DIM = 64
        WS = 64
        H = 8
        HD = DIM // H
        SCALE = HD ** (-0.5)
        B, L, C = x.shape
        pad_len = (WS - L % WS) % WS
        if pad_len > 0:
            x = jnp.pad(x, ((0, 0), (0, pad_len), (0, 0)))
        padded_L = x.shape[1]
        nw = padded_L // WS
        xw = x.reshape(B, nw, WS, C)
        qkv = jnp.einsum('bnwc,oc->bnwo', xw, w_qkv)
        qkv = qkv.reshape(B, nw, WS, 3, H, HD)
        q = jnp.transpose(qkv[..., 0, :, :], (0, 1, 3, 2, 4))
        k = jnp.transpose(qkv[..., 1, :, :], (0, 1, 3, 2, 4))
        v = jnp.transpose(qkv[..., 2, :, :], (0, 1, 3, 2, 4))
        attn = jnp.einsum('bnhqd,bnhkd->bnhqk', q, k) * SCALE
        pos = jnp.arange(WS)
        rel_idx = pos[None, :] - pos[:, None] + WS - 1
        attn = attn + rel_bias[rel_idx]
        attn = jax.nn.softmax(attn, axis=-1)
        out = jnp.einsum('bnhqk,bnhkd->bnhqd', attn, v)
        out = jnp.transpose(out, (0, 1, 3, 2, 4)).reshape(B, nw, WS, C)
        out = jnp.einsum('bnwc,oc->bnwo', out, w_proj) + b_proj
        out = out.reshape(B, padded_L, C)
        if pad_len > 0:
            out = out[:, :L, :]
        return out

    def _L2_ffn_ref(x, W_gat, att_src, att_dst, b_gat, ln_gamma, ln_beta, W1, b1, W2, b2, edge_index):
        import jax, jax.numpy as jnp
        import numpy as np
        B, N, D = (16, 1024, 64)
        NUM_EXPERTS, TOP_K, HEADS = (4, 2, 4)
        N_EDGES = 262144
        LN_EPS = 1e-05

        def _layernorm(x, g, b):
            mu = x.mean(-1, keepdims=True)
            var = ((x - mu) ** 2).mean(-1, keepdims=True)
            return (x - mu) * jax.lax.rsqrt(var + LN_EPS) * g + b

        def _forward(x, edge_index, W_gat, att_src, att_dst, b_gat, ln_gamma, ln_beta, W1, b1, W2, b2):
            Bc, Nc, Dc = x.shape
            M = Bc * Nc
            x_flat = x.reshape(M, Dc)
            h = (x_flat @ W_gat).reshape(M, HEADS, NUM_EXPERTS)
            loops = jnp.arange(M, dtype=edge_index.dtype)
            src = jnp.concatenate([edge_index[0], loops])
            dst = jnp.concatenate([edge_index[1], loops])
            a_src = (h * att_src).sum(-1)
            a_dst = (h * att_dst).sum(-1)
            e = jax.nn.leaky_relu(a_src[src] + a_dst[dst], negative_slope=0.2)
            e_max = jax.ops.segment_max(e, dst, num_segments=M)
            ee = jnp.exp(e - e_max[dst])
            denom = jax.ops.segment_sum(ee, dst, num_segments=M)
            alpha = ee / (denom[dst] + 1e-16)
            msg = h[src] * alpha[:, :, None]
            agg = jax.ops.segment_sum(msg, dst, num_segments=M).reshape(M, HEADS * NUM_EXPERTS) + b_gat
            scores = _layernorm(agg, ln_gamma, ln_beta).reshape(M, HEADS, NUM_EXPERTS).mean(1)
            scores = scores.reshape(Bc, Nc, NUM_EXPERTS)
            topk_s, topk_i = jax.lax.top_k(scores, TOP_K)
            w = jax.nn.softmax(topk_s, axis=-1)
            out = jnp.zeros_like(x)
            for ei in range(NUM_EXPERTS):
                g = jnp.where(topk_i == ei, w, 0.0).sum(-1)
                hh = jax.nn.gelu(x @ W1[ei] + b1[ei], approximate=False)
                out = out + g[..., None] * (hh @ W2[ei] + b2[ei])
            return out
        return _forward(x, edge_index, W_gat, att_src, att_dst, b_gat, ln_gamma, ln_beta, W1, b1, W2, b2)

    def _L3_attn_ref(node_features, ln_gamma, ln_beta, W_qkv, W_gate, b_gate, W_final, b_final):
        import jax, jax.numpy as jnp
        import numpy as np
        H, D = (8, 32)
        EPS = 1e-05
        x = node_features
        B, N, _ = x.shape
        mu = jnp.mean(x, axis=-1, keepdims=True)
        var = jnp.mean(jnp.square(x - mu), axis=-1, keepdims=True)
        normed = (x - mu) / jnp.sqrt(var + EPS) * ln_gamma + ln_beta
        qkv = normed @ W_qkv.T
        q, k, v = jnp.split(qkv, 3, axis=-1)

        def to_heads(t):
            return t.reshape(B, N, H, D).transpose(0, 2, 1, 3)
        q, k, v = (to_heads(q), to_heads(k), to_heads(v))
        gate = jax.nn.sigmoid(to_heads(x @ W_gate.T + b_gate))
        scores = jnp.einsum('bhid,bhjd->bhij', q, k) * D ** (-0.5)
        attn = jax.nn.softmax(scores, axis=-1)
        out = jnp.einsum('bhij,bhid->bhjd', attn, v) * gate
        out = out.transpose(0, 2, 1, 3).reshape(B, N, H * D)
        return x + out @ W_final.T + b_final

    def _L3_ffn_ref(x, ln1_w, ln2_w, wq, wk, wv, wo, router_w, w1, w2, w3):
        import jax, jax.numpy as jnp
        import numpy as np
        B, T, C = (64, 96, 64)
        NH, NKV = (4, 2)
        HD = C // NH
        NREP = NH // NKV
        NE, TOPK = (8, 2)
        HID = int(8 / 3 * C)
        EPS_RMS = 1e-06

        def _rope_tables(t_len):
            inv_freq = 1.0 / 10000.0 ** (np.arange(0, HD, 2, dtype=np.float32) / HD)
            t = np.arange(t_len, dtype=np.float32)
            freqs = np.outer(t, inv_freq)
            emb = np.concatenate([freqs, freqs], axis=-1)
            return (jnp.asarray(np.cos(emb)), jnp.asarray(np.sin(emb)))

        def _rotate_half(x):
            h = x.shape[-1] // 2
            return jnp.concatenate([-x[..., h:], x[..., :h]], axis=-1)

        def _rmsnorm(v, w):
            return v * jax.lax.rsqrt(jnp.mean(v * v, axis=-1, keepdims=True) + EPS_RMS) * w
        Bx, Tx, Cx = x.shape
        h = _rmsnorm(x, ln1_w)
        q = (h @ wq.T).reshape(Bx, Tx, NH, HD).transpose(0, 2, 1, 3)
        k = (h @ wk.T).reshape(Bx, Tx, NKV, HD).transpose(0, 2, 1, 3)
        v = (h @ wv.T).reshape(Bx, Tx, NKV, HD).transpose(0, 2, 1, 3)
        cos, sin = _rope_tables(Tx)
        cos, sin = (cos[None, None], sin[None, None])
        q = q * cos + _rotate_half(q) * sin
        k = k * cos + _rotate_half(k) * sin
        k = jnp.repeat(k, NREP, axis=1)
        v = jnp.repeat(v, NREP, axis=1)
        scores = jnp.einsum('bhtd,bhsd->bhts', q, k) / jnp.sqrt(jnp.float32(HD))
        causal = jnp.tril(jnp.ones((Tx, Tx), dtype=bool))
        scores = jnp.where(causal[None, None], scores, jnp.float32(-1e+30))
        att = jax.nn.softmax(scores, axis=-1)
        y = jnp.einsum('bhts,bhsd->bhtd', att, v).transpose(0, 2, 1, 3).reshape(Bx, Tx, Cx)
        x = x + y @ wo.T
        flat = _rmsnorm(x, ln2_w).reshape(-1, Cx)
        probs = jax.nn.softmax(flat @ router_w.T, axis=-1)
        tp, ti = jax.lax.top_k(probs, TOPK)
        tp = tp / (jnp.sum(tp, axis=-1, keepdims=True) + 1e-09)
        weights = jnp.sum(tp[..., None] * jax.nn.one_hot(ti, NE, dtype=flat.dtype), axis=1)
        out = jnp.zeros_like(flat)
        for e in range(NE):
            hh = jax.nn.silu(flat @ w1[e].T) * (flat @ w3[e].T)
            out = out + weights[:, e:e + 1] * (hh @ w2[e].T)
        return x + out.reshape(Bx, Tx, Cx)
    h = _L0_tok_ref(x, L0_tok_Wq, L0_tok_bq, L0_tok_Wk, L0_tok_bk, L0_tok_Wv, L0_tok_bv, L0_tok_Wo, L0_tok_bo)
    h = jnp.concatenate([jnp.broadcast_to(cls_tok, (h.shape[0], 1, h.shape[2])), h], axis=1)
    h = h + _L0_attn_ref(_layernorm(h, axis=-1), L0_attn_w_qkv, L0_attn_w_out, L0_attn_b_out)
    h = h + _L0_ffn_ref(_layernorm(h, axis=-1), L0_ffn_sW1, L0_ffn_sb1, L0_ffn_sW2, L0_ffn_sb2, L0_ffn_sW3, L0_ffn_sb3, L0_ffn_eW1, L0_ffn_eb1, L0_ffn_eW2, L0_ffn_eb2, L0_ffn_eW3, L0_ffn_eb3, L0_ffn_gW, L0_ffn_gb)
    h = h + _L1_attn_ref(_layernorm(h, axis=-1), L1_attn_Wq, L1_attn_Wk, L1_attn_Wv, L1_attn_Wo, L1_attn_bo)
    h = h + _L1_ffn_ref(_layernorm(h, axis=-1), L1_ffn_Wq_pk, L1_ffn_pk_keys, L1_ffn_Wq, L1_ffn_keys_table, L1_ffn_values_table, L1_ffn_Wo)
    h = h + _L2_attn_ref(_layernorm(h, axis=-1), L2_attn_w_qkv, L2_attn_w_proj, L2_attn_b_proj, L2_attn_rel_bias)
    h = h + _L2_ffn_ref(_layernorm(h, axis=-1), L2_ffn_W_gat, L2_ffn_att_src, L2_ffn_att_dst, L2_ffn_b_gat, L2_ffn_ln_gamma, L2_ffn_ln_beta, L2_ffn_W1, L2_ffn_b1, L2_ffn_W2, L2_ffn_b2, L2_ffn_edge_index)
    h = h + _L3_attn_ref(_layernorm(h, axis=-1), L3_attn_ln_gamma, L3_attn_ln_beta, L3_attn_W_qkv, L3_attn_W_gate, L3_attn_b_gate, L3_attn_W_final, L3_attn_b_final)
    h = h + _L3_ffn_ref(_layernorm(h, axis=-1), L3_ffn_ln1_w, L3_ffn_ln2_w, L3_ffn_wq, L3_ffn_wk, L3_ffn_wv, L3_ffn_wo, L3_ffn_router_w, L3_ffn_w1, L3_ffn_w2, L3_ffn_w3)
    return h

_drawn_inputs = setup_inputs


def setup_inputs(seed=0):
    import zlib

    import numpy as np

    out = dict(_drawn_inputs(seed))
    spreads = {'L0_tok_bq': (0.0, 0.8),
     'L0_tok_bk': (0.0, 2.0),
     'L0_tok_bv': (0.0, 0.1),
     'L0_tok_bo': (0.0, 0.1),
     'L0_ffn_sb1': (0.0, 0.8),
     'L0_ffn_sb2': (0.0, 0.678),
     'L0_ffn_sb3': (0.0, 0.343),
     'L0_ffn_eb1': (0.0, 0.8),
     'L0_ffn_eb2': (0.0, 0.8),
     'L0_ffn_eb3': (0.0, 0.465),
     'L0_ffn_gb': (0.0, 0.8),
     'L2_attn_b_proj': (0.0, 0.319),
     'L2_ffn_b_gat': (0.0, 0.8),
     'L2_ffn_ln_gamma': (1.0, 0.6),
     'L2_ffn_ln_beta': (0.0, 2.0),
     'L2_ffn_b1': (0.0, 0.8),
     'L2_ffn_b2': (0.0, 0.48),
     'L3_attn_ln_gamma': (1.0, 0.6),
     'L3_attn_ln_beta': (0.0, 0.8),
     'L3_attn_b_gate': (1.0, 0.6),
     'L3_attn_b_final': (0.0, 1.205),
     'L3_ffn_ln1_w': (1.0, 0.6),
     'L3_ffn_ln2_w': (1.0, 0.6)}
    factors = {'L0_tok_Wq': 8.0,
     'L0_tok_Wk': 8.0,
     'L0_attn_b_out': 8.0,
     'L0_ffn_sW1': 6.116,
     'L0_ffn_sW2': 5.079,
     'L0_ffn_sW3': 3.324,
     'L0_ffn_eW1': 8.0,
     'L0_ffn_eW2': 8.0,
     'L0_ffn_eW3': 6.687,
     'L0_ffn_gW': 4.244,
     'L1_attn_bo': 22.905,
     'L1_ffn_Wq_pk': 32.496,
     'L1_ffn_pk_keys': 31.808,
     'L1_ffn_Wq': 64.0,
     'L1_ffn_keys_table': 64.0,
     'L1_ffn_values_table': 35.174,
     'L1_ffn_Wo': 33.071,
     'L2_attn_rel_bias': 64.0,
     'L2_ffn_W_gat': 2.958,
     'L2_ffn_att_src': 39.811,
     'L2_ffn_att_dst': 200.0,
     'L2_ffn_W1': 2.757,
     'L2_ffn_W2': 2.709,
     'L3_attn_W_qkv': 8.0,
     'L3_attn_W_gate': 8.0,
     'L3_attn_W_final': 8.0,
     'L3_ffn_wq': 8.0,
     'L3_ffn_wk': 8.0,
     'L3_ffn_wv': 8.0,
     'L3_ffn_wo': 8.0,
     'L3_ffn_router_w': 8.0,
     'L3_ffn_w1': 8.0,
     'L3_ffn_w2': 8.0,
     'L3_ffn_w3': 8.0}
    for name, (base, spread) in spreads.items():
        noise = np.random.default_rng([zlib.crc32(name.encode()), seed]).standard_normal(out[name].shape)
        drawn = base * np.exp(spread * noise) if base else spread * noise
        out[name] = jnp.asarray(drawn.astype(out[name].dtype))
    for name, factor in factors.items():
        out[name] = (out[name] * factor).astype(out[name].dtype)
    return out
```

```python
from contextlib import ExitStack, contextmanager

import numpy as np
import concourse.bass as bass
from concourse import mybir

F32 = mybir.dt.float32
BF16 = mybir.dt.bfloat16
U32 = mybir.dt.uint32
I32 = mybir.dt.int32
ALU = mybir.AluOpType
ACT = mybir.ActivationFunctionType
X = mybir.AxisListType.X

B, N, D = 16, 65, 64
T = B * N
IPC = 4
CH = IPC * N
NC = T // CH
NEG = -1.0e30


@contextmanager
def stage(nc, tag, *signals):
    sems = {s: nc.alloc_semaphore(f"{tag}_{s}") for s in signals}
    with ExitStack() as stack:
        def sb(name, shape, dt=F32):
            return stack.enter_context(nc.sbuf_tensor(f"{tag}_{name}", shape, dt))

        def ps(name, shape, dt=F32):
            return stack.enter_context(nc.psum_tensor(f"{tag}_{name}", shape, dt))

        yield sems, sb, ps
    nc.clear_and_free_semaphores(list(sems.values()))
    nc.all_engine_barrier()


def wait_alone(engine, signal, value, passed):
    engine.wait_ge(signal, value)
    engine.sem_inc(passed, 1)


def layer_norm(nc, tag, src, dst, ones, eps=1e-5, center=True, gain=None, shift=None):
    with stage(nc, tag, "mean", "centered", "squared", "var", "std", "rstd", "normed", "gained", "eps") as (s, sb, ps):
        mean_ps = ps("mean", [D, NC, 512]) if center else None
        var_ps = ps("var", [D, NC, 512])
        cent = sb("cent", [D, T])
        sq = sb("sq", [D, T])
        rstd = sb("rstd", [D, T])
        std = sb("std", [D, T])
        eps_col = sb("eps", [D, 1])
        tok = lambda t, c: t[:, c * CH:(c + 1) * CH]
        base = cent if center else src
        with nc.Block() as block:
            @block.tensor
            def _(pe):
                if center:
                    for c in range(NC):
                        nc.tensor.matmul(mean_ps[:, c, 0:CH], ones[:, :], tok(src, c), start=True, stop=True).then_inc(s["mean"], 1)
                for c in range(NC):
                    pe.wait_ge(s["squared"], c + 1)
                    nc.tensor.matmul(var_ps[:, c, 0:CH], ones[:, :], tok(sq, c), start=True, stop=True).then_inc(s["var"], 1)

            @block.gpsimd
            def _(pool):
                nc.gpsimd.memset(eps_col[:, :], eps).then_inc(s["eps"], 1)

            @block.scalar
            def _(act):
                act.wait_ge(s["eps"], 1)
                for c in range(NC):
                    if center:
                        act.wait_ge(s["centered"], c + 1)
                    nc.scalar.activation(tok(sq, c), tok(base, c), ACT.Square).then_inc(s["squared"], 1)
                for c in range(NC):
                    act.wait_ge(s["var"], c + 1)
                    nc.scalar.activation(tok(std, c), var_ps[:, c, 0:CH], ACT.Sqrt, bias=eps_col[:, 0:1]).then_inc(s["std"], 1)

            @block.vector
            def _(dve):
                if center:
                    for c in range(NC):
                        dve.wait_ge(s["mean"], c + 1)
                        nc.vector.tensor_tensor(tok(cent, c), tok(src, c), mean_ps[:, c, 0:CH], ALU.subtract).then_inc(s["centered"], 1)
                for c in range(NC):
                    dve.wait_ge(s["std"], c + 1)
                    nc.vector.reciprocal(tok(rstd, c), tok(std, c)).then_inc(s["rstd"], 1)
                for c in range(NC):
                    dve.wait_ge(s["rstd"], c + 1)
                    nc.vector.tensor_tensor(tok(dst, c), tok(base, c), tok(rstd, c), ALU.mult).then_inc(s["normed"], 1)
                if gain is not None:
                    for c in range(NC):
                        dve.wait_ge(s["normed"], c + 1)
                        if shift is not None:
                            nc.vector.tensor_scalar(tok(dst, c), tok(dst, c), gain, shift, ALU.mult, ALU.add).then_inc(s["gained"], 1)
                        else:
                            nc.vector.tensor_scalar(tok(dst, c), tok(dst, c), gain, None, ALU.mult).then_inc(s["gained"], 1)


def attention(nc, tag, x, h, wqk, wv, wo, ident, *, heads, hp, scale, bias=None, bo=None, keys=N, vd=None,
              kv=None, rope=None, gate=None, over_queries=False):
    per = 128 // hp
    nb = heads // per
    nq = wqk.shape[1]
    two = 2
    slot = lambda hd: (hp * (hd % per), hd // per)
    row = lambda hd: (hd % per) * nb + hd // per
    with stage(nc, tag, "x_copied", "qk_made", "v_made", "qk_saved", "v_saved", "scores", "masked", "maxed",
               "shifted", "exped", "summed", "inverted", "probs", "turned", "turned_saved", "summed_v",
               "out_saved", "projected", "added", "roped", "kv_copied", "pads") as (s, sb, ps):
        xb = sb("xb", [D, two, N])
        nblk = nb if kv is not None else 2 * nb
        qk = sb("qk", [128, two, nblk, max(N, keys)])
        vt = sb("vt", [N, two, heads * hp])
        kvb = sb("kvb", [128, two, heads, N]) if kv is not None else None
        rp = sb("rp", [128, two, 2, 2, N]) if rope is not None else None
        z = sb("z", [N, two, heads, keys])
        stat = sb("stat", [N, two, 3, heads])
        pt = sb("pt", [N, two, heads, N])
        ot = sb("ot", [128, two, nb, N])
        psA = [ps(f"a{u}", [128, 512]) for u in range(two)]
        psB = [ps(f"b{u}", [128, 512]) for u in range(two)]
        psS = ps("s", [128, per, 2048 // per])
        s_of = lambda u, hd: psS[:, hd % per, (u * nb + hd // per) * 128:(u * nb + hd // per + 1) * 128]
        s_all = lambda u: psS[0:N, :, u * nb * 128:(u + 1) * nb * 128].rearrange("p r (j c) -> p r j c", c=128)
        by_slot = lambda t: t.rearrange("n (r j) c -> n r j c", r=per)
        steps = B // two
        copy_inc = 2 if kv is None else 3

        with nc.Block() as block:
            @block.gpsimd
            def _(pool):
                if keys > N:
                    nc.gpsimd.memset(qk[:, :, :, N:keys], 0.0).then_inc(s["pads"], 1)
                with pool.Fori(0, steps) as i:
                    for u in range(two):
                        nc.gpsimd.tensor_copy(xb[:, u, :], x[:, bass.ds(i * (two * N) + u * N, N)]).then_inc(s["x_copied"], 1)
                    if kv is not None:
                        for u in range(two):
                            nc.gpsimd.tensor_copy(kvb[:, u, :, :], kv[:, :, bass.ds(i * (two * N) + u * N, N)]).then_inc(s["kv_copied"], 1)
                    pool.wait_ge(s["added"], i * two + two)

            @block.tensor
            def _(pe):
                if keys > N:
                    pe.wait_ge(s["pads"], 1)
                with pe.Fori(0, steps) as i:
                    for u in range(two):
                        pe.wait_ge(s["x_copied"], i * two + (u + 1))
                        for j in range(nq):
                            mm = nc.tensor.matmul(psA[u][:, j * N:(j + 1) * N], wqk[:, j, :], xb[:, u, :], start=True, stop=True)
                        mm.then_inc(s["qk_made"], 1)
                        if kv is None:
                            nc.tensor.matmul(psB[u][0:N, 0:heads * hp], xb[:, u, :], wv, start=True, stop=True).then_inc(s["v_made"], 1)
                        else:
                            pe.wait_ge(s["kv_copied"], i * two + (u + 1))
                            for hd in range(heads):
                                mm = nc.tensor.transpose(s_of(u, hd)[0:N, :], kvb[:, u, hd, :], ident[:, :])
                            mm.then_inc(s["v_made"], 1)
                    for u in range(two):
                        pe.wait_ge(s["qk_saved"], i * two + (u + 1))
                        if kv is not None:
                            pe.wait_ge(s["v_saved"], i * two + (u + 1))
                        for hd in range(heads):
                            p, j = slot(hd)
                            k_of = kvb[p:p + hp, u, hd, :] if kv is not None else qk[p:p + hp, u, nb + j, 0:keys]
                            mm = nc.tensor.matmul(s_of(u, hd)[0:N, 0:keys], qk[p:p + hp, u, j, 0:N], k_of, start=True, stop=True)
                        mm.then_inc(s["scores"], 1)
                    for u in range(two):
                        pe.wait_ge(s["probs"], i * two + (u + 1))
                        if not over_queries:
                            for hd in range(heads):
                                mm = nc.tensor.transpose(s_of(u, hd)[0:N, 0:N], z[:, u, row(hd), 0:N], ident[0:N, 0:N])
                            mm.then_inc(s["turned"], 1)
                    for u in range(two):
                        if not over_queries:
                            pe.wait_ge(s["turned_saved"], i * two + (u + 1))
                        pe.wait_ge(s["v_saved"], i * two + (u + 1))
                        for hd in range(heads):
                            p, j = slot(hd)
                            probs = z[:, u, row(hd), 0:N] if over_queries else pt[:, u, row(hd), :]
                            mm = nc.tensor.matmul(psA[u][p:p + hp, j * N:(j + 1) * N], vt[:, u, hd * hp:(hd + 1) * hp], probs, start=True, stop=True)
                        mm.then_inc(s["summed_v"], 1)
                    for u in range(two):
                        pe.wait_ge(s["out_saved"], i * two + (u + 1))
                        for j in range(nb):
                            mm = nc.tensor.matmul(psB[u][0:D, 0:N], wo[:, j, :], ot[:, u, j, :], start=(j == 0), stop=(j == nb - 1))
                        mm.then_inc(s["projected"], 1)
                    pe.wait_ge(s["added"], i * two + two)

            @block.scalar
            def _(act):
                with act.Fori(0, steps) as i:
                    for u in range(two):
                        act.wait_ge(s["qk_made"], i * two + (u + 1))
                        if rope is None:
                            nc.scalar.copy(qk[:, u, :, 0:N], psA[u][:, 0:nq * N].rearrange("p (j n) -> p j n", n=N)).then_inc(s["qk_saved"], 1)
                        act.wait_ge(s["v_made"], i * two + (u + 1))
                        if kv is None:
                            nc.scalar.copy(vt[:, u, :], psB[u][0:N, 0:heads * hp]).then_inc(s["v_saved"], 1)
                        else:
                            v_of = vt[:, u, :].rearrange("n (h two d) -> n h two d", two=2, d=hp)
                            nc.scalar.copy(v_of[:, :, 0, :], s_all(u)[:, 0, :, hp:2 * hp])
                            nc.scalar.copy(v_of[:, :, 1, :], s_all(u)[:, 1, :, 0:hp]).then_inc(s["v_saved"], 1)
                    for u in range(two):
                        act.wait_ge(s["shifted"], i * two + (u + 1))
                        nc.scalar.activation(z[:, u, :, :], z[:, u, :, :], ACT.Exp, scale=scale).then_inc(s["exped"], 1)
                    for u in range(two):
                        if not over_queries:
                            act.wait_ge(s["turned"], i * two + two)
                            nc.scalar.copy(by_slot(pt[:, u, :, :]), s_all(u)[:, :, :, 0:N]).then_inc(s["turned_saved"], 1)
                    for u in range(two):
                        act.wait_ge(s["summed_v"], i * two + (u + 1))
                        if gate is None:
                            nc.scalar.copy(ot[:, u, :, :], psA[u][:, 0:nb * N].rearrange("p (j n) -> p j n", n=N)).then_inc(s["out_saved"], 1)
                    act.wait_ge(s["added"], i * two + two)

            @block.vector
            def _(dve):
                with dve.Fori(0, steps) as i:
                    if rope is not None:
                        for u in range(two):
                            made = psA[u][:, 0:nq * N].rearrange("p (a j n) -> p a j n", a=2, n=N)
                            dve.wait_ge(s["qk_made"], i * two + (u + 1))
                            nc.vector.tensor_tensor(rp[:, u, 0, :, :], made[:, 0, :, :], rope[:, 0:1, :].to_broadcast([128, 2, N]), ALU.mult).then_inc(s["roped"], 1)
                            nc.vector.tensor_tensor(rp[:, u, 1, :, :], made[:, 1, :, :], rope[:, 1:2, :].to_broadcast([128, 2, N]), ALU.mult).then_inc(s["roped"], 1)
                            dve.wait_ge(s["roped"], i * (2 * two) + 2 * (u + 1))
                            nc.vector.tensor_tensor(qk[:, u, :, 0:N], rp[:, u, 0, :, :], rp[:, u, 1, :, :], ALU.add).then_inc(s["qk_saved"], 1)
                    for u in range(two):
                        dve.wait_ge(s["scores"], i * two + two)
                        of, zz = s_all(u)[:, :, :, 0:keys], by_slot(z[:, u, :, :])
                        if bias is not None:
                            nc.vector.tensor_tensor(zz, of, bias, ALU.add).then_inc(s["masked"], 1)
                            dve.wait_ge(s["masked"], i * two + (u + 1))
                            of = zz
                        mx = stat[:, u, 0, :].rearrange("n (r j) -> n r j", r=per)
                        nc.vector.tensor_reduce(mx, of, X, ALU.max).then_inc(s["maxed"], 1)
                        dve.wait_ge(s["maxed"], i * two + (u + 1))
                        nc.vector.tensor_tensor(zz, of, mx.unsqueeze(3).to_broadcast([N, per, nb, keys]), ALU.subtract).then_inc(s["shifted"], 1)
                    for u in range(two):
                        dve.wait_ge(s["exped"], i * two + (u + 1))
                        nc.vector.tensor_reduce(stat[:, u, 1, :], z[:, u, :, :], X, ALU.add).then_inc(s["summed"], 1)
                        dve.wait_ge(s["summed"], i * two + (u + 1))
                        nc.vector.reciprocal(stat[:, u, 2, :], stat[:, u, 1, :]).then_inc(s["inverted"], 1)
                        dve.wait_ge(s["inverted"], i * two + (u + 1))
                        nc.vector.tensor_tensor(z[:, u, :, :], z[:, u, :, :], stat[:, u, 2, :].unsqueeze(2).to_broadcast([N, heads, keys]), ALU.mult).then_inc(s["probs"], 1)
                    for u in range(two):
                        if gate is not None:
                            dve.wait_ge(s["summed_v"], i * two + (u + 1))
                            nc.vector.tensor_tensor(ot[:, u, :, :], psA[u][:, 0:nb * N].rearrange("p (j n) -> p j n", n=N),
                                                    gate[:, :, bass.ds(i * (two * N) + u * N, N)], ALU.mult).then_inc(s["out_saved"], 1)
                    for u in range(two):
                        dve.wait_ge(s["projected"], i * two + (u + 1))
                        mine = h[:, bass.ds(i * (two * N) + u * N, N)]
                        if bo is not None:
                            nc.vector.scalar_tensor_tensor(mine, psB[u][0:D, 0:N], bo, mine, ALU.add, ALU.add).then_inc(s["added"], 1)
                        else:
                            nc.vector.tensor_tensor(mine, psB[u][0:D, 0:N], mine, ALU.add).then_inc(s["added"], 1)


def linear_attention(nc, tag, x, h, wq, wkv, wo, bo):
    H, dh, two, nb = 8, 64, 2, 4
    with stage(nc, tag, "wsum", "wmean", "wcentered", "x_copied", "q_made", "kv_made", "q_saved", "squared", "sums",
               "eps", "root", "inverted", "kv_saved", "dots", "dots_saved", "out", "out_saved", "projected", "added") as (s, sb, ps):
        wmean = sb("wmean", [D, 2, 2 * H])
        eps_col = sb("eps", [N, 1])
        xb = sb("xb", [D, two, N])
        q = sb("q", [128, two, nb, N])
        sq = sb("sq", [N, two, 2 * H, dh])
        kv = sb("kv", [N, two, 2 * H, dh])
        stat = sb("stat", [N, two, 3, 2 * H])
        dots = sb("dots", [128, two, nb, 128])
        ot = sb("ot", [128, two, nb, N])
        psQ = [ps(f"q{u}", [128, 512]) for u in range(two)]
        psKV = [ps(f"kv{u}", [128, 2, 512]) for u in range(two)]
        psD = [ps(f"d{u}", [128, 512]) for u in range(two)]
        steps = B // two
        img = lambda t, i, u: t[:, bass.ds(i * (two * N) + u * N, N)]
        with nc.Block() as block:
            @block.gpsimd
            def _(pool):
                nc.gpsimd.memset(eps_col[:, :], 1e-5).then_inc(s["eps"], 1)
                nc.gpsimd.memset(dots[:, :, :, :], 0.0).then_inc(s["eps"], 1)
                with pool.Fori(0, steps) as i:
                    for u in range(two):
                        nc.gpsimd.tensor_copy(xb[:, u, :], img(x, i, u)).then_inc(s["x_copied"], 1)
                    pool.wait_ge(s["added"], i * two + two)

            @block.tensor
            def _(pe):
                pe.wait_ge(s["wcentered"], 1)
                with pe.Fori(0, steps) as i:
                    for u in range(two):
                        pe.wait_ge(s["x_copied"], i * two + (u + 1))
                        for part in range(2):
                            mm = nc.tensor.matmul(psKV[u][0:N, part, :], xb[:, u, :], wkv[:, part * H:(part + 1) * H, :], start=True, stop=True)
                        mm.then_inc(s["kv_made"], 1)
                        for j in range(nb):
                            mm = nc.tensor.matmul(psQ[u][:, j * N:(j + 1) * N], wq[:, j, :], xb[:, u, :], start=True, stop=True)
                        mm.then_inc(s["q_made"], 1)
                    for u in range(two):
                        pe.wait_ge(s["kv_saved"], i * two + (u + 1))
                        for hd in range(H):
                            p = dh * (hd % 2)
                            mm = nc.tensor.matmul(psD[u][p:p + dh, (hd // 2) * dh:(hd // 2 + 1) * dh], kv[:, u, hd, :], kv[:, u, H + hd, :], start=True, stop=True)
                        mm.then_inc(s["dots"], 1)
                    for u in range(two):
                        pe.wait_ge(s["q_saved"], i * two + (u + 1))
                        pe.wait_ge(s["dots_saved"], i * (2 * two) + 2 * (u + 1))
                        for j in range(nb):
                            mm = nc.tensor.matmul(psQ[u][:, j * N:(j + 1) * N], dots[:, u, j, :], q[:, u, j, :], start=True, stop=True)
                        mm.then_inc(s["out"], 1)
                    for u in range(two):
                        pe.wait_ge(s["out_saved"], i * two + (u + 1))
                        for j in range(nb):
                            mm = nc.tensor.matmul(psKV[u][0:D, 1, 0:N], wo[:, j, :], ot[:, u, j, :], start=(j == 0), stop=(j == nb - 1))
                        mm.then_inc(s["projected"], 1)
                    pe.wait_ge(s["added"], i * two + two)

            @block.scalar
            def _(act):
                act.wait_ge(s["eps"], 2)
                with act.Fori(0, steps) as i:
                    for u in range(two):
                        act.wait_ge(s["kv_made"], i * two + (u + 1))
                        nc.scalar.activation(sq[:, u, :, :], psKV[u][0:N, :, :].rearrange("n a (h d) -> n (a h) d", d=dh), ACT.Square).then_inc(s["squared"], 1)
                        act.wait_ge(s["q_made"], i * two + (u + 1))
                        nc.scalar.activation(q[:, u, :, :], psQ[u][:, 0:nb * N].rearrange("p (j n) -> p j n", n=N), ACT.Copy).then_inc(s["q_saved"], 1)
                    for u in range(two):
                        act.wait_ge(s["sums"], i * two + (u + 1))
                        nc.scalar.activation(stat[:, u, 1, :], stat[:, u, 0, :], ACT.Sqrt, bias=eps_col[:, 0:1], scale=1.0 / dh).then_inc(s["root"], 1)
                    for u in range(two):
                        act.wait_ge(s["dots"], i * two + (u + 1))
                        for p in (0, dh):
                            nc.scalar.activation(dots[p:p + dh, u, :, p:p + dh], psD[u][p:p + dh, 0:nb * dh].rearrange("p (j d) -> p j d", d=dh), ACT.Copy, scale=1.0 / N).then_inc(s["dots_saved"], 1)
                    for u in range(two):
                        act.wait_ge(s["out"], i * two + (u + 1))
                        nc.scalar.activation(ot[:, u, :, :], psQ[u][:, 0:nb * N].rearrange("p (j n) -> p j n", n=N), ACT.Copy).then_inc(s["out_saved"], 1)
                    act.wait_ge(s["added"], i * two + two)

            @block.vector
            def _(dve):
                nc.vector.tensor_reduce(wmean[:, 0, :], wkv[:, :, :], X, ALU.add).then_inc(s["wsum"], 1)
                dve.wait_ge(s["wsum"], 1)
                nc.vector.tensor_scalar(wmean[:, 1, :], wmean[:, 0, :], 1.0 / dh, None, ALU.mult).then_inc(s["wmean"], 1)
                dve.wait_ge(s["wmean"], 1)
                nc.vector.tensor_tensor(wkv[:, :, :], wkv[:, :, :], wmean[:, 1, :].unsqueeze(2).to_broadcast([D, 2 * H, dh]), ALU.subtract).then_inc(s["wcentered"], 1)
                with dve.Fori(0, steps) as i:
                    for u in range(two):
                        dve.wait_ge(s["squared"], i * two + (u + 1))
                        nc.vector.tensor_reduce(stat[:, u, 0, :], sq[:, u, :, :], X, ALU.add).then_inc(s["sums"], 1)
                    for u in range(two):
                        dve.wait_ge(s["root"], i * two + (u + 1))
                        nc.vector.reciprocal(stat[:, u, 2, :], stat[:, u, 1, :]).then_inc(s["inverted"], 1)
                        dve.wait_ge(s["inverted"], i * two + (u + 1))
                        nc.vector.tensor_tensor(kv[:, u, :, :], psKV[u][0:N, :, :].rearrange("n a (h d) -> n (a h) d", d=dh),
                                                stat[:, u, 2, :].unsqueeze(2).to_broadcast([N, 2 * H, dh]), ALU.mult).then_inc(s["kv_saved"], 1)
                    for u in range(two):
                        dve.wait_ge(s["projected"], i * two + (u + 1))
                        nc.vector.scalar_tensor_tensor(img(h, i, u), psKV[u][0:D, 1, 0:N], bo, img(h, i, u), ALU.add, ALU.add).then_inc(s["added"], 1)


def top2(nc, tag, wT, ident, E, mode, x=None, gw=None, gb=None, scores=None):
    gated = scores is None
    with stage(nc, tag, "logits", "chain", "ones", "tri", "shifted", "exped", "weights", "turned", "saved") as (s, sb, ps):
        g = sb("g", [N, B, E]) if gated else scores
        z = sb("z", [N, B, E])
        gt = sb("gt", [N, B, E, E])
        eq = sb("eq", [N, B, E, E])
        tri = sb("tri", [N, E, E])
        st = sb("st", [N, 2, B])
        rank = sb("rank", [N, B, E])
        logits_ps = ps("logits", [N, B, E])
        wT_ps = ps("wT", [E, NC, 512])
        wide = lambda t: t.unsqueeze(2).to_broadcast([N, B, E])
        every = [N, B, E, E]
        n_exp = 2 if mode == "softmax of gates" else 1
        with nc.Block() as block:
            @block.gpsimd
            def _(pool):
                nc.gpsimd.memset(tri[:, :, :], 1.0).then_inc(s["ones"], 1)
                pool.wait_ge(s["ones"], 1)
                nc.gpsimd.affine_select(out=tri[:, :, :], in_=tri[:, :, :], compare_op=ALU.is_ge, fill=0.0, base=-1,
                                        pattern=[[1, E], [-1, E]], channel_multiplier=0).then_inc(s["tri"], 1)

            @block.tensor
            def _(pe):
                if gated:
                    for b in range(B):
                        mm = nc.tensor.matmul(logits_ps[:, b, :], x[:, b * N:(b + 1) * N], gw, start=True, stop=True)
                    mm.then_inc(s["logits"], 1)
                pe.wait_ge(s["weights"], 1)
                for b in range(B):
                    mm = nc.tensor.transpose(wT_ps[:, b // IPC, (b % IPC) * N:(b % IPC + 1) * N], z[:, b, :], ident[0:N, 0:N])
                mm.then_inc(s["turned"], 1)

            @block.scalar
            def _(act):
                for n in range(n_exp):
                    act.wait_ge(s["shifted"], n + 1)
                    if mode != "share" and n == n_exp - 1:
                        nc.scalar.activation(z[:, :, :], z[:, :, :], ACT.Exp).then_inc(s["exped"], 1)
                    else:
                        nc.scalar.activation(g[:, :, :], g[:, :, :], ACT.Exp).then_inc(s["exped"], 1)
                act.wait_ge(s["turned"], 1)
                nc.scalar.activation(wT[:, :].rearrange("e (c t) -> e c t", c=NC), wT_ps[:, :, 0:CH], ACT.Copy).then_inc(s["saved"], 1)

            @block.vector
            def _(dve):
                links = [0]

                def link(ins):
                    links[0] += 1
                    ins.then_inc(s["chain"], 1)
                    dve.wait_ge(s["chain"], links[0])

                V = nc.vector
                if gated:
                    dve.wait_ge(s["logits"], 1)
                    if gb is not None:
                        link(V.tensor_tensor(g[:, :, :], logits_ps[:, :, :], gb.unsqueeze(1).to_broadcast([N, B, E]), ALU.add))
                    else:
                        link(V.tensor_copy(g[:, :, :], logits_ps[:, :, :]))
                    link(V.tensor_reduce(st[:, 0, :], g[:, :, :], X, ALU.max))
                    V.tensor_tensor(g[:, :, :], g[:, :, :], wide(st[:, 0, :]), ALU.subtract).then_inc(s["shifted"], 1)
                    dve.wait_ge(s["exped"], 1)
                    link(V.tensor_reduce(st[:, 0, :], g[:, :, :], X, ALU.add))
                    link(V.reciprocal(st[:, 1, :], st[:, 0, :]))
                    link(V.tensor_tensor(g[:, :, :], g[:, :, :], wide(st[:, 1, :]), ALU.mult))
                dve.wait_ge(s["tri"], 1)
                mine, other = g[:, :, :].unsqueeze(3).to_broadcast(every), g[:, :, :].unsqueeze(2).to_broadcast(every)
                V.tensor_tensor(gt[:, :, :, :], other, mine, ALU.is_gt)
                link(V.tensor_tensor(eq[:, :, :, :], other, mine, ALU.is_equal))
                link(V.tensor_tensor(eq[:, :, :, :], eq[:, :, :, :], tri[:, :, :].unsqueeze(1).to_broadcast(every), ALU.mult))
                link(V.tensor_tensor(gt[:, :, :, :], gt[:, :, :, :], eq[:, :, :, :], ALU.add))
                link(V.tensor_reduce(rank[:, :, :], gt[:, :, :, :], X, ALU.add))
                if mode == "share":
                    link(V.scalar_tensor_tensor(z[:, :, :], rank[:, :, :], 2.0, g[:, :, :], ALU.is_lt, ALU.mult))
                    link(V.tensor_reduce(st[:, 0, :], z[:, :, :], X, ALU.add))
                    link(V.tensor_scalar(st[:, 0, :], st[:, 0, :], 1e-9, None, ALU.add))
                else:
                    link(V.tensor_reduce(st[:, 0, :], g[:, :, :], X, ALU.max))
                    V.tensor_tensor(z[:, :, :], g[:, :, :], wide(st[:, 0, :]), ALU.subtract).then_inc(s["shifted"], 1)
                    dve.wait_ge(s["exped"], n_exp)
                    link(V.scalar_tensor_tensor(z[:, :, :], rank[:, :, :], 2.0, z[:, :, :], ALU.is_lt, ALU.mult))
                    link(V.tensor_reduce(st[:, 0, :], z[:, :, :], X, ALU.add))
                link(V.reciprocal(st[:, 1, :], st[:, 0, :]))
                V.tensor_tensor(z[:, :, :], z[:, :, :], wide(st[:, 1, :]), ALU.mult).then_inc(s["weights"], 1)


def chunk(t, i):
    return t[:, i * CH:(i + 1) * CH]


def relu_experts(nc, tag, x, h, wT, pick, W1, b1, W2, b2, W3, sb3, eb3):
    M = len(W1)
    with stage(nc, tag, "first", "first_saved", "second", "second_saved", "weight", "weighted", "sum", "added") as (s, sb, ps):
        h1 = sb("h1", [128, 2, CH])
        h2 = sb("h2", [128, 2, CH])
        hw = sb("hw", [128, 2, CH])
        p1 = [ps(f"p1{k}", [128, 512]) for k in range(2)]
        p2 = [ps(f"p2{k}", [128, 512]) for k in range(2)]
        pw = [ps(f"pw{k}", [128, 512]) for k in range(2)]
        acc = ps("acc", [D, 512])
        n1 = [w.shape[1] for w in W1]
        n2 = [w.shape[1] for w in W2]
        place = [(i, m) for i in range(NC) for m in range(M)]
        gated = lambda i, m: i * (M - 1) + m
        with nc.Block() as block:
            @block.tensor
            def _(pe):
                def first(n):
                    if n >= len(place):
                        return
                    i, m = place[n]
                    if n >= 2:
                        pe.wait_ge(s["first_saved"], n - 1)
                    nc.tensor.matmul(p1[n % 2][0:n1[m], 0:CH], W1[m], chunk(x, i), start=True, stop=True).then_inc(s["first"], 1)

                def last(n):
                    i, m = place[n]
                    if m == 0:
                        if i:
                            pe.wait_ge(s["added"], i)
                        nc.tensor.matmul(acc[:, 0:CH], eb3, chunk(wT, i), start=True, stop=False)
                        pe.wait_ge(s["second_saved"], n + 1)
                    else:
                        pe.wait_ge(s["weighted"], gated(i, m))
                    src = (hw[0:n2[m], gated(i, m) % 2, :] if m else h2[0:n2[m], n % 2, :])
                    mm = nc.tensor.matmul(acc[:, 0:CH], W3[m], src, start=False, stop=(m == M - 1))
                    if m == M - 1:
                        mm.then_inc(s["sum"], 1)

                first(0)
                for n, (i, m) in enumerate(place):
                    first(n + 1)
                    pe.wait_ge(s["first_saved"], n + 1)
                    if n >= 2:
                        pe.wait_ge(s["second_saved"], n - 1)
                    nc.tensor.matmul(p2[n % 2][0:n2[m], 0:CH], W2[m], h1[0:n1[m], n % 2, :], start=True, stop=True).then_inc(s["second"], 1)
                    if m:
                        if gated(i, m) >= 3:
                            pe.wait_ge(s["weighted"], gated(i, m) - 2)
                        nc.tensor.matmul(pw[gated(i, m) % 2][0:n2[m], 0:CH], pick[0:M - 1, m - 1, 0:n2[m]], chunk(wT, i), start=True, stop=True).then_inc(s["weight"], 1)
                    if n:
                        last(n - 1)
                last(len(place) - 1)

            @block.scalar
            def _(act):
                for n, (i, m) in enumerate(place):
                    act.wait_ge(s["first"], n + 1)
                    if n >= 2:
                        act.wait_ge(s["second"], n - 1)
                    nc.scalar.activation(h1[0:n1[m], n % 2, :], p1[n % 2][0:n1[m], 0:CH], ACT.Relu, bias=b1[m]).then_inc(s["first_saved"], 1)
                    act.wait_ge(s["second"], n + 1)
                    if n >= 2 and place[n - 2][1]:
                        act.wait_ge(s["weighted"], gated(*place[n - 2]))
                    nc.scalar.activation(h2[0:n2[m], n % 2, :], p2[n % 2][0:n2[m], 0:CH], ACT.Relu, bias=b2[m]).then_inc(s["second_saved"], 1)

            @block.vector
            def _(dve):
                for n, (i, m) in enumerate(place):
                    if m:
                        k = gated(i, m)
                        dve.wait_ge(s["second_saved"], n + 1)
                        dve.wait_ge(s["weight"], k)
                        nc.vector.tensor_tensor(hw[0:n2[m], k % 2, :], h2[0:n2[m], n % 2, :], pw[k % 2][0:n2[m], 0:CH], ALU.mult).then_inc(s["weighted"], 1)
                    if m == M - 1:
                        dve.wait_ge(s["sum"], i + 1)
                        nc.vector.scalar_tensor_tensor(chunk(h, i), acc[:, 0:CH], sb3, chunk(h, i), ALU.add, ALU.add).then_inc(s["added"], 1)


PK = 16
NKEY = 64
TT = 104
NT = T // TT
TG = 8
HG = TG // 2


def product_keys(nc, tag, x, wq, keys, table, kv, ident):
    H, G2, SL = 8, 16, slice(None)
    LINKS = 21
    rounds = TT // TG
    early = 8
    with stage(nc, tag, "q", "q_saved", "iota_i", "consts", "q_tile", "sim", "sim_saved", "chain", "shifted", "exped", "rows_ready",
               "turned", "index_saved", "spread", "staged", "gathered0", "gathered1", "weighed", "kv_saved", "passed") as (s, sb, ps):
        qT = sb("qT", [128, 4, T])
        qb = sb("qb", [128, 4, TT])
        sim = sb("sim", [TT, G2, NKEY])
        sim2 = sb("sim2", [TT, G2, NKEY])
        top = sb("top", [TT, G2, PK])
        topi = sb("topi", [TT, G2, PK], U32)
        topf = sb("topf", [TT, G2, PK])
        sums = sb("sums", [TT, H, PK * PK])
        sums2 = sb("sums2", [TT, H, PK * PK])
        best = sb("best", [TT, H, PK])
        besti = sb("besti", [TT, H, PK], U32)
        part_u = sb("part_u", [TT, 2, H * PK], U32)
        part = sb("part", [TT, 2, H, PK])
        half_i = sb("half_i", [TT, 2, H, PK])
        row = sb("row", [TT, H, PK])
        wt = sb("wt", [TT, H, PK])
        st = sb("st", [TT, 2, H])
        head0 = sb("head0", [TT, H, PK])
        count = sb("count", [TT, PK])
        own = sb("own", [128, H])
        idxT = sb("idxT", [128, T + TG], U32)
        spread = sb("spread", [128, T, H])
        idx = [sb(f"idx{a}", [128, HG], U32) for a in range(2)]
        got = [sb(f"got{n}", [128, 128]) for n in range(TG)]
        psQ = ps("s", [128, 4, 512])
        psS = psQ[0:TT, :, :]
        psT = ps("t", [128, 2, 512])
        psG = [ps(f"g{a}", [128, 512]) for a in range(2)]
        full = [TT, H, PK, PK]
        with nc.Block() as block:
            def gather_at(t, g):
                return t * TT + g * TG

            @block.gpsimd
            def _(pool):
                P = nc.gpsimd
                P.iota(head0[:, :, :], [[NKEY * NKEY, H], [0, PK]], base=0, channel_multiplier=0, allow_small_or_imprecise_dtypes=True)
                P.iota(count[:, :], [[1, PK]], base=0, channel_multiplier=0, allow_small_or_imprecise_dtypes=True)
                P.memset(own[:, :], 1.0).then_inc(s["iota_i"], 1)
                pool.wait_ge(s["iota_i"], 1)
                P.memset(idxT[:, T:T + TG], 0)
                P.affine_select(out=own[:, :], in_=own[:, :], compare_op=ALU.is_ge, fill=0.0, base=0, pattern=[[-PK, H]], channel_multiplier=1).then_inc(s["iota_i"], 1)
                pool.wait_ge(s["iota_i"], 2)
                P.affine_select(out=own[:, :], in_=own[:, :], compare_op=ALU.is_ge, fill=0.0, base=PK - 1, pattern=[[PK, H]], channel_multiplier=-1).then_inc(s["consts"], 1)
                pool.wait_ge(s["consts"], 1)
                with pool.Fori(0, T // TG) as n:
                    for a in range(2):
                        wait_alone(pool, s["staged"], n * 2 + (a + 1), s["passed"])
                        for k in range(HG):
                            P.indirect_dma_start(out=got[a * HG + k][:, :], out_offset=None, in_=table,
                                                 in_offset=bass.IndirectOffsetOnAxis(ap=idx[a][:, k:k + 1], axis=0)).then_inc(s[f"gathered{a}"], 16)

            @block.tensor
            def _(pe):
                M = nc.tensor.matmul
                for j in range(4):
                    for c in range(NC):
                        if j * NC + c >= 4:
                            pe.wait_ge(s["q_saved"], j * NC + c - 3)
                        M(psQ[:, (j * NC + c) % 4, 0:CH], wq[:, j, :], chunk(x, c), start=True, stop=True).then_inc(s["q"], 1)
                pe.wait_ge(s["q_saved"], 4 * NC)

                def score(t):
                    pe.wait_ge(s["q_tile"], t + 1)
                    for f in range(G2):
                        r, j = f % 4, f // 4
                        mm = M(psS[:, r, j * NKEY:(j + 1) * NKEY], qb[32 * r:32 * r + 32, j, :], keys[32 * r:32 * r + 32, j, :], start=True, stop=True)
                    mm.then_inc(s["sim"], 1)

                def turn(t):
                    pe.wait_ge(s["rows_ready"], t + 1)
                    nc.tensor.transpose(psT[:, 0, 0:TT], row[:, :, :].rearrange("n h k -> n (h k)"), ident[0:TT, 0:TT])
                    nc.tensor.transpose(psT[:, 1, 0:TT], wt[:, :, :].rearrange("n h k -> n (h k)"), ident[0:TT, 0:TT]).then_inc(s["turned"], 1)

                def weigh(t, first, steps):
                    wait_alone(pe, s["spread"], t + 1, s["passed"])
                    with pe.Fori(0, steps) as k_:
                        g = k_ + first
                        for a in range(2):
                            pe.wait_ge(s[f"gathered{a}"], (t * rounds + g) * (16 * HG) + 16 * HG)
                            for k in range(HG):
                                mm = M(psG[a][:, k * H:(k + 1) * H], got[a * HG + k][:, :],
                                       spread[:, bass.ds(gather_at(t, g) + (a * HG + k), 1), :].rearrange("p o h -> p (o h)"), start=True, stop=True)
                            mm.then_inc(s["weighed"], 1)
                        pe.wait_ge(s["kv_saved"], (t * rounds + g) * 2 + 2)

                score(0)
                turn(0)
                with pe.Fori(0, NT - 1) as t:
                    score(t + 1)
                    weigh(t, 0, early)
                    turn(t + 1)
                    weigh(t, early, rounds - early)
                weigh(NT - 1, 0, rounds)

            @block.scalar
            def _(act):
                C = lambda out, in_: nc.scalar.activation(out, in_, ACT.Copy)
                for j in range(4):
                    for c in range(NC):
                        n = j * NC + c
                        act.wait_ge(s["q"], n + 1)
                        C(chunk(qT[:, j, :], c), psQ[:, n % 4, 0:CH]).then_inc(s["q_saved"], 1)
                act.wait_ge(s["q_saved"], 4 * NC)

                def score(t):
                    C(qb[:, :, :], qT[:, :, bass.ds(t * TT, TT)]).then_inc(s["q_tile"], 1)
                    act.wait_ge(s["sim"], t + 1)
                    C(sim[:, :, :].rearrange("n (j r) k -> n r j k", r=4), psS[:, :, 0:4 * NKEY].rearrange("n r (j k) -> n r j k", j=4)).then_inc(s["sim_saved"], 1)

                def soften(t):
                    act.wait_ge(s["shifted"], t + 1)
                    nc.scalar.activation(wt[:, :, :], wt[:, :, :], ACT.Exp).then_inc(s["exped"], 1)
                    act.wait_ge(s["turned"], t + 1)
                    C(idxT[:, bass.ds(t * TT, TT)], psT[:, 0, 0:TT]).then_inc(s["index_saved"], 1)

                def stage_index(t, g, a):
                    C(idx[a][:, :], idxT[:, bass.ds(gather_at(t, g) + a * HG, HG)]).then_inc(s["staged"], 1)

                def gathers(t, first, steps, tiles):
                    wait_alone(act, s["index_saved"], tiles, s["passed"])
                    with act.Fori(0, steps) as k_:
                        g = k_ + first
                        for a in range(2):
                            act.wait_ge(s["weighed"], (t * rounds + g) * 2 + (a + 1))
                            stage_index(t, g + 1, a)
                            C(kv[:, :, bass.ds(gather_at(t, g) + a * HG, HG)], psG[a][:, 0:HG * H].rearrange("p (n h) -> p h n", h=H)).then_inc(s["kv_saved"], 1)

                score(0)
                soften(0)
                act.wait_ge(s["index_saved"], 1)
                act.wait_ge(s["consts"], 1)
                for a in range(2):
                    stage_index(0, 0, a)
                with act.Fori(0, NT - 1) as t:
                    score(t + 1)
                    gathers(t, 0, early, t + 1)
                    soften(t + 1)
                    gathers(t, early, rounds - early, t + 2)
                gathers(NT - 1, 0, rounds, NT)

            @block.vector
            def _(dve):
                V = nc.vector
                dve.wait_ge(s["consts"], 1)

                def score(t):
                    links = [0]

                    def link(ins):
                        links[0] += 1
                        ins.then_inc(s["chain"], 1)
                        wait_alone(dve, s["chain"], t * LINKS + links[0], s["passed"])

                    def top16(n, val, ind, src, src2):
                        for f in range(n):
                            last = V.max(val[:, f, 0:8], src[:, f, :])
                        link(last)
                        for f in range(n):
                            V.max_index(ind[:, f, 0:8], val[:, f, 0:8], src[:, f, :])
                        for f in range(n):
                            last = V.match_replace(src2[:, f, :], val[:, f, 0:8], src[:, f, :], NEG)
                        link(last)
                        for f in range(n):
                            last = V.max(val[:, f, 8:16], src2[:, f, :])
                        link(last)
                        for f in range(n):
                            last = V.max_index(ind[:, f, 8:16], val[:, f, 8:16], src2[:, f, :])
                        link(last)

                    wait_alone(dve, s["sim_saved"], t + 1, s["passed"])
                    top16(G2, top, topi, sim, sim2)
                    link(V.tensor_copy(topf[:, :, :], topi[:, :, :]))
                    for hd in range(H):
                        last = V.tensor_tensor(sums[:, hd, :].rearrange("n (a b) -> n a b", a=PK), top[:, hd, :].unsqueeze(2).to_broadcast([TT, PK, PK]),
                                               top[:, H + hd, :].unsqueeze(1).to_broadcast([TT, PK, PK]), ALU.add)
                    link(last)
                    top16(H, best, besti, sums, sums2)
                    flat = besti[:, :, :].rearrange("n h k -> n (h k)")
                    V.tensor_scalar(part_u[:, 0, :], flat, 4, None, ALU.logical_shift_right)
                    link(V.tensor_scalar(part_u[:, 1, :], flat, PK - 1, None, ALU.bitwise_and))
                    link(V.tensor_copy(part[:, :, :, :].rearrange("n a h k -> n a (h k)"), part_u[:, :, :]))
                    for a in range(2):
                        eq = sums[:, :, :].rearrange("n h (k m) -> n h k m", k=PK)
                        link(V.tensor_tensor(eq, part[:, a, :, :].unsqueeze(3).to_broadcast(full), count[:, :].unsqueeze(1).unsqueeze(1).to_broadcast(full), ALU.is_equal))
                        link(V.tensor_tensor(eq, eq, topf[:, a * H:(a + 1) * H, :].unsqueeze(2).to_broadcast(full), ALU.mult))
                        link(V.tensor_reduce(half_i[:, a, :, :], eq, X, ALU.add))
                    if not isinstance(t, int) or t:
                        dve.wait_ge(s["turned"], t)
                    link(V.scalar_tensor_tensor(row[:, :, :], half_i[:, 1, :, :], float(NKEY), half_i[:, 0, :, :], ALU.mult, ALU.add))
                    V.tensor_tensor(row[:, :, :], row[:, :, :], head0[:, :, :], ALU.add)
                    V.tensor_tensor(wt[:, :, :], best[:, :, :], best[:, :, 0:1].to_broadcast([TT, H, PK]), ALU.subtract).then_inc(s["shifted"], 1)
                    dve.wait_ge(s["exped"], t + 1)
                    link(V.tensor_reduce(st[:, 0, :], wt[:, :, :], X, ALU.add))
                    link(V.reciprocal(st[:, 1, :], st[:, 0, :]))
                    V.tensor_tensor(wt[:, :, :], wt[:, :, :], st[:, 1, :].unsqueeze(2).to_broadcast([TT, H, PK]), ALU.mult).then_inc(s["rows_ready"], 1)
                    dve.wait_ge(s["index_saved"], t + 1)
                    V.tensor_tensor(spread[:, bass.ds(t * TT, TT), :], psT[:, 1, 0:TT].unsqueeze(2).to_broadcast([128, TT, H]),
                                    own[:, :].unsqueeze(1).to_broadcast([128, TT, H]), ALU.mult).then_inc(s["spread"], 1)
                    assert links[0] <= LINKS, links
                    while links[0] < LINKS:
                        link(V.tensor_copy(st[:, 0, 0:1], st[:, 1, 0:1]))

                score(0)
                with dve.Fori(0, NT - 1) as t:
                    score(t + 1)



def gate_values(nc, tag, x, h, wg, bg, gate):
    with stage(nc, tag, "made", "saved", "added") as (s, sb, ps):
        made = [ps(f"g{k}", [128, 512]) for k in range(4)]
        with nc.Block() as block:
            @block.tensor
            def _(pe):
                for n in range(2 * NC):
                    if n >= 4:
                        pe.wait_ge(s["saved"], n - 3)
                    nc.tensor.matmul(made[n % 4][:, 0:CH], wg[:, n // NC, :], chunk(x, n % NC), start=True, stop=True).then_inc(s["made"], 1)

            @block.scalar
            def _(act):
                for n in range(2 * NC):
                    act.wait_ge(s["made"], n + 1)
                    nc.scalar.activation(chunk(gate[:, n // NC, :], n % NC), made[n % 4][:, 0:CH], ACT.Sigmoid, bias=bg[:, n // NC:n // NC + 1]).then_inc(s["saved"], 1)

            @block.vector
            def _(dve):
                nc.vector.tensor_tensor(h[:, :], h[:, :], x[:, :], ALU.add).then_inc(s["added"], 1)


def silu_experts(nc, tag, x, h, rest, wT, pick, w1, w3, w2, experts, hid):
    place = [(i, e) for i in range(NC) for e in range(experts)]
    with stage(nc, tag, "weight", "weighted", "up", "silu", "linear", "product", "sum", "rested", "added") as (s, sb, ps):
        xw = sb("xw", [D, 2, CH])
        act_sb = sb("act", [hid, 2, 2, CH])
        hw = sb("hw", [hid, 2, 2, CH])
        p1 = [ps(f"p1{k}", [hid, 2, 512]) for k in range(2)]
        p3 = ps("p3", [hid, 2, 512])
        pw = ps("pw", [D, 512])
        acc = ps("acc", [D, 512])
        with nc.Block() as block:
            @block.tensor
            def _(pe):
                M = nc.tensor.matmul

                def up(n):
                    i, e = place[n]
                    if n:
                        pe.wait_ge(s["weighted"], n)
                    M(pw[:, 0:CH], pick[0:experts, e, 0:D], chunk(wT, i), start=True, stop=True).then_inc(s["weight"], 1)
                    if n >= 2:
                        pe.wait_ge(s["silu"], n - 1)
                    for k in range(2):
                        mm = M(p1[n % 2][:, k, 0:CH], w1[:, e, k, :], chunk(x, i), start=True, stop=True)
                    mm.then_inc(s["up"], 1)

                def down(n):
                    i, e = place[n]
                    pe.wait_ge(s["product"], n + 1)
                    if e == 0 and i:
                        pe.wait_ge(s["added"], i)
                    for k in range(2):
                        mm = M(acc[:, 0:CH], w2[:, e, k, :], hw[:, n % 2, k, :], start=(e == 0 and k == 0), stop=(e == experts - 1 and k == 1))
                    if e == experts - 1:
                        mm.then_inc(s["sum"], 1)

                up(0)
                for n, (i, e) in enumerate(place):
                    if n + 1 < len(place):
                        up(n + 1)
                    pe.wait_ge(s["weighted"], n + 1)
                    if n:
                        pe.wait_ge(s["product"], n)
                    for k in range(2):
                        mm = M(p3[:, k, 0:CH], w3[:, e, k, :], xw[:, n % 2, :], start=True, stop=True)
                    mm.then_inc(s["linear"], 1)
                    if n:
                        down(n - 1)
                down(len(place) - 1)

            @block.scalar
            def _(act):
                for n in range(len(place)):
                    act.wait_ge(s["up"], n + 1)
                    if n >= 2:
                        act.wait_ge(s["product"], n - 1)
                    nc.scalar.activation(act_sb[:, n % 2, :, :], p1[n % 2][:, :, 0:CH], ACT.Silu).then_inc(s["silu"], 1)

            @block.vector
            def _(dve):
                V = nc.vector
                V.tensor_tensor(h[:, :], h[:, :], rest[:, :], ALU.add).then_inc(s["rested"], 1)

                def weight(n):
                    i, e = place[n]
                    dve.wait_ge(s["weight"], n + 1)
                    if n >= 2:
                        dve.wait_ge(s["linear"], n - 1)
                    V.tensor_tensor(xw[:, n % 2, :], chunk(x, i), pw[:, 0:CH], ALU.mult).then_inc(s["weighted"], 1)

                weight(0)
                for n, (i, e) in enumerate(place):
                    if n + 1 < len(place):
                        weight(n + 1)
                    dve.wait_ge(s["silu"], n + 1)
                    dve.wait_ge(s["linear"], n + 1)
                    if n == 0:
                        dve.wait_ge(s["rested"], 1)
                    V.tensor_tensor(hw[:, n % 2, :, :], act_sb[:, n % 2, :, :], p3[:, :, 0:CH], ALU.mult).then_inc(s["product"], 1)
                    if e == experts - 1:
                        dve.wait_ge(s["sum"], i + 1)
                        V.tensor_tensor(chunk(h, i), chunk(h, i), acc[:, 0:CH], ALU.add).then_inc(s["added"], 1)


def gelu_experts(nc, tag, x, h, wT, pick, w1, b1, w2, b2, experts, hid):
    place = [(i, e) for i in range(NC) for e in range(experts)]
    with stage(nc, tag, "weight", "up", "gelu", "weighted", "sum", "added") as (s, sb, ps):
        act_sb = sb("act", [hid, 2, CH])
        hw = sb("hw", [hid, 2, CH])
        p1 = [ps(f"p1{k}", [hid, 512]) for k in range(2)]
        pw = [ps(f"pw{k}", [hid, 512]) for k in range(2)]
        acc = ps("acc", [D, 512])
        with nc.Block() as block:
            @block.tensor
            def _(pe):
                M = nc.tensor.matmul

                def up(n):
                    i, e = place[n]
                    if n >= 2:
                        pe.wait_ge(s["weighted"], n - 1)
                    M(pw[n % 2][:, 0:CH], pick[0:experts, e, 0:hid], chunk(wT, i), start=True, stop=True).then_inc(s["weight"], 1)
                    M(p1[n % 2][:, 0:CH], w1[:, e, :], chunk(x, i), start=True, stop=True).then_inc(s["up"], 1)

                up(0)
                for n, (i, e) in enumerate(place):
                    if n + 1 < len(place):
                        up(n + 1)
                    if e == 0:
                        if i:
                            pe.wait_ge(s["added"], i)
                        M(acc[:, 0:CH], b2, chunk(wT, i), start=True, stop=False)
                    pe.wait_ge(s["weighted"], n + 1)
                    mm = M(acc[:, 0:CH], w2[:, e, :], hw[:, n % 2, :], start=False, stop=(e == experts - 1))
                    if e == experts - 1:
                        mm.then_inc(s["sum"], 1)

            @block.scalar
            def _(act):
                for n, (i, e) in enumerate(place):
                    act.wait_ge(s["up"], n + 1)
                    if n >= 2:
                        act.wait_ge(s["weighted"], n - 1)
                    nc.scalar.activation(act_sb[:, n % 2, :], p1[n % 2][:, 0:CH], ACT.Gelu, bias=b1[:, e:e + 1]).then_inc(s["gelu"], 1)

            @block.vector
            def _(dve):
                for n, (i, e) in enumerate(place):
                    dve.wait_ge(s["gelu"], n + 1)
                    dve.wait_ge(s["weight"], n + 1)
                    nc.vector.tensor_tensor(hw[:, n % 2, :], act_sb[:, n % 2, :], pw[n % 2][:, 0:CH], ALU.mult).then_inc(s["weighted"], 1)
                    if e == experts - 1:
                        dve.wait_ge(s["sum"], i + 1)
                        nc.vector.tensor_tensor(chunk(h, i), chunk(h, i), acc[:, 0:CH], ALU.add).then_inc(s["added"], 1)


M_ALL = 16 * 1024
ROUND = 8
ROUNDS = 3


def edge_counts(nc, tag, src_ap, dst_ap, ident, countT, absent):
    E = src_ap.shape[0]
    L = E // 128
    LOW = 32
    HIGH = T // LOW + 1
    CK = 32
    steps = L // (2 * CK)
    KEY = 2048
    with stage(nc, tag, "loaded", "chain", "iota", "hot", "hot_used", "zeros", "hist", "hist_saved", "hist_out", "hist_in", "rchain",
               "round_hot", "counted", "added", "flag", "flag_int", "rounds_done", "loops", "turned", "made", "passed") as (s, sb, ps):
        src = sb("src", [128, L], I32)
        dst = sb("dst", [128, L], I32)
        key = sb("key", [128, L])
        srcf = sb("srcf", [128, L])
        dig = sb("dig", [128, 2, L], BF16)
        count = sb("count", [128, HIGH + 1], BF16)
        hot_hi = sb("hot_hi", [128, 2, CK, HIGH], BF16)
        hot_lo = sb("hot_lo", [128, 2, CK, LOW], BF16)
        place = sb("place", [128, T])
        zero = sb("zero", [128, T], BF16)
        hot = sb("hot", [128, 2, ROUND, T], BF16)
        top = sb("top", [128, ROUND])
        top_u = sb("top_u", [128, 3, ROUND], U32)
        top_f = sb("top_f", [128, 2, ROUND])
        flag = sb("flag", [128, 1])
        flag_i = sb("flag_i", [128, 1], I32)
        hist = sb("hist", [HIGH, LOW])
        hist_dram = nc.dram_tensor(f"{tag}_hist_dram", (HIGH * LOW,), F32).ap()
        psC = ps("c", [128, 2, 4, 512])
        psH = psC[0:HIGH, 0, 0, 0:LOW]
        V = nc.vector
        with nc.Block() as block:
            @block.sync
            def _(sp):
                sp.dma_start(src[:, :], src_ap.rearrange("(p l) -> p l", p=128)).then_inc(s["loaded"], 16)
                sp.dma_start(dst[:, :], dst_ap.rearrange("(p l) -> p l", p=128)).then_inc(s["loaded"], 16)
                sp.wait_ge(s["hist_saved"], 1)
                sp.dma_start(hist_dram.rearrange("(a b) -> a b", b=LOW), hist[:, :]).then_inc(s["hist_out"], 16)
                sp.wait_ge(s["hist_out"], 16)
                sp.wait_ge(s["rounds_done"], 1)
                sp.dma_start(countT[TT - 1:TT, NT - 1, :], hist_dram[0:T].rearrange("(a n) -> a n", a=1)).then_inc(s["hist_in"], 16)

            @block.gpsimd
            def _(pool):
                P = nc.gpsimd
                P.iota(count[:, :], [[1, HIGH + 1]], base=0, channel_multiplier=0, allow_small_or_imprecise_dtypes=True)
                P.iota(place[:, :], [[1, T]], base=0, channel_multiplier=0, allow_small_or_imprecise_dtypes=True).then_inc(s["iota"], 1)
                P.memset(zero[:, :], 0.0).then_inc(s["zeros"], 1)
                P.memset(countT[:, :, :], 0.0).then_inc(s["zeros"], 1)
                pool.wait_ge(s["flag"], 1)
                P.partition_all_reduce(flag[:, :], flag[:, :], 128, bass.bass_isa.ReduceOp.max).then_inc(s["flag"], 1)

            @block.tensor
            def _(pe):
                M = nc.tensor.matmul
                pe.wait_ge(s["zeros"], 1)
                M(psH, zero[:, 0:HIGH], zero[:, 0:LOW], start=True, stop=False)
                with pe.Fori(0, steps) as i:
                    for a in range(2):
                        pe.wait_ge(s["hot"], i * 2 + (a + 1))
                        for k in range(CK):
                            mm = M(psH, hot_hi[:, a, k, :], hot_lo[:, a, k, :], start=False, stop=False, skip_group_check=True)
                        mm.then_inc(s["hot_used"], 1)
                M(psH, zero[:, 0:HIGH], zero[:, 0:LOW], start=False, stop=True).then_inc(s["hist"], 1)
                pe.wait_ge(s["hist_saved"], 1)

                def round_(r):
                    pe.wait_ge(s["round_hot"], r + 1)
                    for t in range(NT):
                        if t >= 2:
                            pe.wait_ge(s["added"], r * NT + (t - 1))
                        for c in range(NC):
                            for k in range(ROUND):
                                mm = M(psC[0:TT, t % 2, c, 0:CH], hot[:, 0, k, t * TT:(t + 1) * TT], hot[:, 1, k, c * CH:(c + 1) * CH],
                                       start=(k == 0), stop=(k == ROUND - 1))
                        mm.then_inc(s["counted"], 1)
                    pe.wait_ge(s["added"], r * NT + NT)

                with pe.Fori(0, ROUNDS) as r:
                    round_(r)
                pe.wait_ge(s["flag_int"], 1)
                left = pe.value_load(flag_i[0:1, 0:1], min_val=0, max_val=1)
                with pe.If(left > 0):
                    with pe.Fori(ROUNDS, L // ROUND) as r:
                        round_(r)
                for t in range(NT):
                    pe.wait_ge(s["loops"], NT)
                    if t >= 2:
                        pe.wait_ge(s["made"], t - 1)
                    for o in range(NT):
                        mm = nc.tensor.transpose(psC[0:TT, t % 2, o // 4, (o % 4) * TT:(o % 4 + 1) * TT], countT[:, o, t * TT:(t + 1) * TT], ident[0:TT, 0:TT])
                    mm.then_inc(s["turned"], 1)

            @block.vector
            def _(dve):
                links = [0]

                def link(ins):
                    links[0] += 1
                    ins.then_inc(s["chain"], 1)
                    dve.wait_ge(s["chain"], links[0])

                dve.wait_ge(s["loaded"], 32)
                dve.wait_ge(s["iota"], 1)
                link(V.tensor_copy(srcf[:, :], src[:, :]))
                link(V.tensor_copy(key[:, :], dst[:, :]))
                link(V.tensor_scalar(src[:, :], dst[:, :], 5, None, ALU.logical_shift_right))
                link(V.tensor_copy(dig[:, 0, :], src[:, :]))
                link(V.tensor_scalar(src[:, :], dst[:, :], LOW - 1, None, ALU.bitwise_and))
                link(V.tensor_copy(dig[:, 1, :], src[:, :]))
                true = src[:, :].bitcast(F32)
                link(V.tensor_scalar(true, srcf[:, :], float(T - 1), None, ALU.is_lt))
                link(V.scalar_tensor_tensor(dig[:, 1, :], true, 2.0 * LOW, dig[:, 1, :], ALU.mult, ALU.add))
                link(V.scalar_tensor_tensor(true, key[:, :], float(T), true, ALU.is_lt, ALU.mult))
                link(V.scalar_tensor_tensor(key[:, :], key[:, :], float(KEY), srcf[:, :], ALU.mult, ALU.add))
                link(V.scalar_tensor_tensor(key[:, :], key[:, :], 1.0, true, ALU.add, ALU.mult))

                def hist_half(i, a):
                    cols = lambda d: dig[:, d, bass.ds(i * (2 * CK) + a * CK, CK)]
                    for d, (to, n) in enumerate(((hot_hi, HIGH), (hot_lo, LOW))):
                        last = V.tensor_tensor(to[:, a, :, :], cols(d).unsqueeze(2).to_broadcast([128, CK, n]),
                                               count[:, 0:n].unsqueeze(1).to_broadcast([128, CK, n]), ALU.is_equal)
                    last.then_inc(s["hot"], 1)

                hist_half(0, 0)
                hist_half(0, 1)
                with dve.Fori(0, steps - 1) as i:
                    for a in range(2):
                        dve.wait_ge(s["hot_used"], i * 2 + (a + 1))
                        hist_half(i + 1, a)
                dve.wait_ge(s["hist"], 1)
                V.tensor_copy(hist[:, :], psH).then_inc(s["hist_saved"], 1)

                RLINKS = 6

                def rlink(r, n, ins):
                    ins.then_inc(s["rchain"], 1)
                    wait_alone(dve, s["rchain"], r * RLINKS + n, s["passed"])

                def round_(r):
                    rlink(r, 1, V.max(top[:, :], key[:, :]))
                    V.match_replace(key[:, :], top[:, :], key[:, :], 0.0)
                    rlink(r, 2, V.tensor_copy(top_u[:, 0, :], top[:, :]))
                    V.tensor_scalar(top_u[:, 1, :], top_u[:, 0, :], KEY - 1, None, ALU.bitwise_and)
                    rlink(r, 3, V.tensor_scalar(top_u[:, 2, :], top_u[:, 0, :], 11, None, ALU.logical_shift_right))
                    rlink(r, 4, V.tensor_copy(top_f[:, :, :], top_u[:, 1:3, :]))
                    rlink(r, 5, V.tensor_scalar(top_f[:, 0, :], top_f[:, 0, :], -1.0, None, ALU.add))
                    for k in range(ROUND):
                        V.tensor_scalar(hot[:, 0, k, :], place[:, :], top_f[:, 0, k:k + 1], None, ALU.is_equal)
                        last = V.tensor_scalar(hot[:, 1, k, :], place[:, :], top_f[:, 1, k:k + 1], None, ALU.is_equal)
                    last.then_inc(s["round_hot"], 1)
                    for t in range(NT):
                        dve.wait_ge(s["counted"], r * NT + (t + 1))
                        V.tensor_tensor(countT[:, t, :].rearrange("p (c n) -> p c n", c=NC), countT[:, t, :].rearrange("p (c n) -> p c n", c=NC),
                                        psC[0:TT, t % 2, :, 0:CH], ALU.add).then_inc(s["added"], 1)
                    rlink(r, 6, V.tensor_copy(top_u[:, 0, 0:1], top_u[:, 1, 0:1]))

                dve.wait_ge(s["zeros"], 2)
                with dve.Fori(0, ROUNDS) as r:
                    round_(r)
                link(V.tensor_reduce(flag[:, :], key[:, :], X, ALU.max))
                V.tensor_scalar(flag[:, :], flag[:, :], 1.0, None, ALU.min).then_inc(s["flag"], 1)
                dve.wait_ge(s["flag_int"], 1)
                left = dve.value_load(flag_i[0:1, 0:1], min_val=0, max_val=1)
                with dve.If(left > 0):
                    with dve.Fori(ROUNDS, L // ROUND) as r:
                        round_(r)
                V.tensor_copy(top[:, 0:1], flag[:, :]).then_inc(s["rounds_done"], 1)
                dve.wait_ge(s["hist_in"], 16)
                for t in range(NT):
                    V.tensor_tensor(countT[:, t, t * TT:(t + 1) * TT], countT[:, t, t * TT:(t + 1) * TT], ident[0:TT, 0:TT], ALU.add).then_inc(s["loops"], 1)
                for t in range(NT):
                    dve.wait_ge(s["turned"], t + 1)
                    for lo, hi in ((0, 8), (8, NT)):
                        last = V.tensor_scalar(absent[:, t, lo * TT:hi * TT].rearrange("p (c n) -> p c n", n=min(4, hi - lo) * TT),
                                               psC[0:TT, t % 2, lo // 4:(hi + 3) // 4, 0:min(4, hi - lo) * TT], 0.5, NEG, ALU.is_lt, ALU.mult)
                    last.then_inc(s["made"], 1)

            @block.scalar
            def _(act):
                act.wait_ge(s["flag"], 2)
                nc.scalar.activation(flag_i[:, :], flag[:, :], ACT.Copy).then_inc(s["flag_int"], 1)


def graph_scores(nc, tag, x, wgat, att, att_col, rows, ident, pick, countT, absent, scores):
    K, E = 4, 4
    W = 32
    two = 2
    with stage(nc, tag, "zeros", "ones", "sel", "made", "saved", "chain", "spread", "maxed", "parts", "turned", "turned_saved",
               "wide", "wide_saved", "copied", "low", "high", "below", "exped", "edges", "summed", "agg", "agg_saved",
               "back", "root", "eps", "passed") as (s, sb, ps):
        hT = sb("hT", [K * E, T])
        hp = sb("hp", [TT, NT, K, W])
        hb = sb("hb", [TT, two, K, W])
        sel = sb("sel", [K * E, K, TT])
        zero = sb("zero", [TT, CH])
        tmp = sb("tmp", [TT, NT, K, E])
        a = sb("a", [TT, 2, NT, K])
        junk = sb("junk", [TT, two, T])
        M = sb("m", [TT, NT, K])
        U = sb("u", [TT, NT, 2 * K])
        UT = sb("ut", [2 * K, T])
        UB = sb("ub", [TT, 2 * K, T])
        low = sb("low", [TT, two, T])
        z = sb("z", [TT, two, T])
        p = sb("p", [TT, two, T])
        aggT = sb("aggt", [128, T])
        g = sb("g", [N, B, K * E])
        sq = sb("sq", [N, B, K * E])
        st = sb("st", [N, 4, B])
        den = sb("den", [N, B, K])
        eps_col = sb("eps", [N, 1])
        psA = ps("banks", [128, 2, NC, 512])
        by_chunk = lambda t: t.rearrange("p (c n) -> p c n", c=NC)
        V = nc.vector
        with nc.Block() as block:
            @block.gpsimd
            def _(pool):
                P = nc.gpsimd
                P.memset(sel[:, :, :], 1.0).then_inc(s["ones"], 1)
                P.memset(zero[:, :], 0.0).then_inc(s["zeros"], 1)
                P.memset(eps_col[:, :], 1e-5).then_inc(s["eps"], 1)
                P.memset(hp[:, :, :, :], 0.0).then_inc(s["ones"], 1)
                pool.wait_ge(s["ones"], 1)
                P.affine_select(out=sel[:, :, :], in_=sel[:, :, :], compare_op=ALU.is_ge, fill=0.0, base=0,
                                pattern=[[-E, K], [0, TT]], channel_multiplier=1).then_inc(s["ones"], 1)
                pool.wait_ge(s["ones"], 3)
                P.affine_select(out=sel[:, :, :], in_=sel[:, :, :], compare_op=ALU.is_ge, fill=0.0, base=E - 1,
                                pattern=[[E, K], [0, TT]], channel_multiplier=-1).then_inc(s["ones"], 1)
                P.memset(hp[:, :, :, E:E + 1], 1.0).then_inc(s["ones"], 1)
                pool.wait_ge(s["ones"], 5)
                P.tensor_scalar(sel[:, :, :], sel[:, :, :], att_col, None, ALU.mult).then_inc(s["sel"], 1)
                pool.wait_ge(s["parts"], 1)
                with pool.Fori(0, NT // two) as i:
                    for u in range(two):
                        P.tensor_copy(hb[:, u, :, :], hp[:, bass.ds(i * two + u, 1), :, :].rearrange("p a k w -> p (a k) w")).then_inc(s["copied"], 1)
                    for u in range(two):
                        for k in range(K):
                            n = u * K + k + 1
                            wait_alone(pool, s["high"], i * (two * K) + n, s["passed"])
                            P.tensor_scalar(z[:, k % 2, :], z[:, k % 2, :], 0.0, None, ALU.min).then_inc(s["below"], 1)
                    pool.wait_ge(s["summed"], i * (two * K) + two * K)

            @block.tensor
            def _(pe):
                MM = nc.tensor.matmul
                for c in range(NC):
                    mm = MM(psA[0:K * E, 0, c, 0:CH], wgat, chunk(x, c), start=True, stop=True)
                mm.then_inc(s["made"], 1)
                for t in range(NT):
                    mm = MM(psA[0:TT, 1, 0, t * K * E:(t + 1) * K * E], x[:, t * TT:(t + 1) * TT], wgat, start=True, stop=True)
                mm.then_inc(s["made"], 1)
                pe.wait_ge(s["saved"], 2)
                pe.wait_ge(s["sel"], 1)
                for k in range(K):
                    if k >= 2:
                        pe.wait_ge(s["maxed"], (k - 1) * NT)
                    for c in range(NC):
                        mm = MM(psA[0:TT, k % 2, c, 0:CH], sel[:, k, :], chunk(hT, c), start=True, stop=True)
                    mm.then_inc(s["spread"], 1)
                pe.wait_ge(s["parts"], 1)
                for t in range(NT):
                    mm = nc.tensor.transpose(psA[0:2 * K, 0, t // 4, (t % 4) * TT:(t % 4 + 1) * TT], U[:, t, :], ident[0:TT, 0:TT])
                mm.then_inc(s["turned"], 1)
                pe.wait_ge(s["turned_saved"], 2)
                for j in range(2 * K):
                    if j >= 2:
                        pe.wait_ge(s["wide_saved"], j - 1)
                    for c in range(NC):
                        mm = MM(psA[0:TT, j % 2, c, 0:CH], pick[0:2 * K, j, 0:TT], chunk(UT, c), start=True, stop=True)
                    mm.then_inc(s["wide"], 1)
                pe.wait_ge(s["wide_saved"], 2 * K)
                for c in range(NC):
                    MM(psA[:, 0, c, 0:CH], zero[:, 0:128], zero[:, :], start=True, stop=False)
                with pe.Fori(0, NT // two) as i:
                    for u in range(two):
                        for k in range(K):
                            pe.wait_ge(s["edges"], i * (two * K) + (u * K + k + 1))
                            for c in range(NC):
                                mm = MM(psA[k * W:(k + 1) * W, 0, c, 0:CH], hb[:, u, k, :], p[:, k % 2, c * CH:(c + 1) * CH],
                                        start=False, stop=False, skip_group_check=True, tile_position=(0, k * W))
                            mm.then_inc(s["summed"], 1)
                for c in range(NC):
                    mm = MM(psA[:, 0, c, 0:CH], zero[:, 0:128], zero[:, :], start=False, stop=True)
                mm.then_inc(s["agg"], 1)
                pe.wait_ge(s["agg_saved"], 1)
                for b in range(B):
                    mm = nc.tensor.transpose(psA[0:N, 1, b // IPC, (b % IPC) * 128:(b % IPC + 1) * 128], aggT[:, b * N:(b + 1) * N], ident[:, :])
                mm.then_inc(s["back"], 1)

            @block.scalar
            def _(act):
                act.wait_ge(s["made"], 1)
                nc.scalar.copy(by_chunk(hT[:, :]), psA[0:K * E, 0, :, 0:CH]).then_inc(s["saved"], 1)
                act.wait_ge(s["turned"], 1)
                nc.scalar.copy(UT[:, 0:8 * TT].rearrange("p (c n) -> p c n", c=2), psA[0:2 * K, 0, 0:2, 0:4 * TT]).then_inc(s["turned_saved"], 1)
                nc.scalar.copy(UT[:, 8 * TT:T], psA[0:2 * K, 0, 2, 0:2 * TT]).then_inc(s["turned_saved"], 1)
                for j in range(2 * K):
                    act.wait_ge(s["wide"], j + 1)
                    nc.scalar.copy(by_chunk(UB[:, j, :]), psA[0:TT, j % 2, :, 0:CH]).then_inc(s["wide_saved"], 1)
                act.wait_ge(s["wide_saved"], 2 * K)
                with act.Fori(0, NT // two) as i:
                    act.wait_ge(s["copied"], i * two + two)

                    def lower(u, k):
                        n = u * K + k
                        if n >= 2:
                            act.wait_ge(s["high"], i * (two * K) + (n - 1))
                        nc.scalar.activation(low[:, k % 2, :], UB[:, K + k, :], ACT.Identity, bias=hb[:, u, k, E + 2:E + 3]).then_inc(s["low"], 1)

                    lower(0, 0)
                    for n in range(two * K):
                        u, k = divmod(n, K)
                        if n + 1 < two * K:
                            lower(*divmod(n + 1, K))
                        act.wait_ge(s["below"], i * (two * K) + (n + 1))
                        nc.scalar.activation(z[:, k % 2, :], z[:, k % 2, :], ACT.Exp).then_inc(s["exped"], 1)
                act.wait_ge(s["agg"], 1)
                nc.scalar.copy(by_chunk(aggT[:, :]), psA[:, 0, :, 0:CH]).then_inc(s["agg_saved"], 1)
                act.wait_ge(s["eps"], 1)
                act.wait_ge(s["back"], 2)
                nc.scalar.activation(st[:, 2, :], st[:, 1, :], ACT.Sqrt, bias=eps_col[:, 0:1], scale=1.0 / (K * E)).then_inc(s["root"], 1)

            @block.vector
            def _(dve):
                links = [0]

                def link(ins):
                    links[0] += 1
                    ins.then_inc(s["chain"], 1)
                    dve.wait_ge(s["chain"], links[0])

                heads_of = lambda t: t.rearrange("p t (k e) -> p t k e", k=K)
                dve.wait_ge(s["ones"], 5)
                dve.wait_ge(s["made"], 2)
                made = psA[0:TT, 1, 0, 0:NT * K * E].rearrange("p (t k e) -> p t k e", k=K, e=E)
                link(V.tensor_copy(hp[:, :, :, 0:E], made))
                for side in range(2):
                    row = att[:, side, :].rearrange("p (k e) -> p k e", k=K).unsqueeze(1).to_broadcast([TT, NT, K, E])
                    link(V.tensor_tensor(tmp[:, :, :, :], hp[:, :, :, 0:E], row, ALU.mult))
                    link(V.tensor_reduce(a[:, side, :, :], tmp[:, :, :, :], X, ALU.add))
                V.tensor_scalar(hp[:, :, :, E + 1], a[:, 0, :, :], 1.0, None, ALU.mult)
                V.tensor_scalar(hp[:, :, :, E + 2], a[:, 0, :, :], 0.2, None, ALU.mult).then_inc(s["saved"], 1)
                for k in range(K):
                    dve.wait_ge(s["spread"], k + 1)
                    for t in range(NT):
                        n = k * NT + t
                        if n >= two:
                            dve.wait_ge(s["maxed"], n - 1)
                        V.tensor_tensor_reduce(out=by_chunk(junk[:, n % two, :]), in0=by_chunk(absent[:, t, :]), in1=psA[0:TT, k % 2, :, 0:CH],
                                               scale=1.0, scalar=-3.0e38, op0=ALU.add, op1=ALU.max, accum_out=M[:, t, k:k + 1]).then_inc(s["maxed"], 1)
                dve.wait_ge(s["maxed"], K * NT)
                ad = a[:, 1, :, :]
                link(V.tensor_tensor(M[:, :, :], M[:, :, :], ad, ALU.add))
                link(V.scalar_tensor_tensor(M[:, :, :], M[:, :, :], 0.2, M[:, :, :], ALU.mult, ALU.max))
                V.tensor_tensor(U[:, :, 0:K], ad, M[:, :, :], ALU.subtract)
                V.scalar_tensor_tensor(U[:, :, K:2 * K], ad, 0.2, M[:, :, :], ALU.mult, ALU.subtract).then_inc(s["parts"], 1)
                dve.wait_ge(s["wide_saved"], 2 * K)
                with dve.Fori(0, NT // two) as i:
                    dve.wait_ge(s["copied"], i * two + two)
                    last = two * K

                    def top(n):
                        u, k = divmod(n, K)
                        dve.wait_ge(s["low"], i * last + (n + 1))
                        V.scalar_tensor_tensor(z[:, k % 2, :], UB[:, k, :], hb[:, u, k, E + 1:E + 2], low[:, k % 2, :], ALU.add, ALU.max).then_inc(s["high"], 1)

                    top(0)
                    for n in range(last):
                        u, k = divmod(n, K)
                        if n + 1 < last:
                            if n >= 1:
                                dve.wait_ge(s["edges"], i * last + n)
                            top(n + 1)
                        dve.wait_ge(s["exped"], i * last + (n + 1))
                        if n >= 2:
                            dve.wait_ge(s["summed"], i * last + (n - 1))
                        V.tensor_tensor(p[:, k % 2, :], z[:, k % 2, :], countT[:, bass.ds(i * two + u, 1), :].rearrange("p a t -> p (a t)"), ALU.mult).then_inc(s["edges"], 1)
                    dve.wait_ge(s["summed"], i * last + last)
                dve.wait_ge(s["back"], 1)
                agg = psA[0:N, 1, :, :].rearrange("n c (i k w) -> n (c i) k w", k=K, w=W)
                g4 = heads_of(g[:, :, :])
                wide = lambda t: t.unsqueeze(2).to_broadcast([N, B, K * E])
                all_of = lambda r: rows[:, r:r + 1, :].to_broadcast([N, B, K * E])
                link(V.tensor_scalar(den[:, :, :], agg[:, :, :, E], 1e-16, None, ALU.add))
                link(V.reciprocal(den[:, :, :], den[:, :, :]))
                link(V.tensor_tensor(g4, agg[:, :, :, 0:E], den[:, :, :].unsqueeze(3).to_broadcast([N, B, K, E]), ALU.mult))
                link(V.tensor_tensor(g[:, :, :], g[:, :, :], all_of(0), ALU.add))
                link(V.tensor_reduce(st[:, 0, :], g[:, :, :], X, ALU.add))
                link(V.tensor_scalar(st[:, 0, :], st[:, 0, :], 1.0 / (K * E), None, ALU.mult))
                link(V.tensor_tensor(g[:, :, :], g[:, :, :], wide(st[:, 0, :]), ALU.subtract))
                link(V.tensor_tensor(sq[:, :, :], g[:, :, :], g[:, :, :], ALU.mult))
                V.tensor_reduce(st[:, 1, :], sq[:, :, :], X, ALU.add).then_inc(s["back"], 1)
                dve.wait_ge(s["root"], 1)
                link(V.reciprocal(st[:, 3, :], st[:, 2, :]))
                link(V.tensor_tensor(g[:, :, :], g[:, :, :], wide(st[:, 3, :]), ALU.mult))
                link(V.tensor_tensor(g[:, :, :], g[:, :, :], all_of(1), ALU.mult))
                link(V.tensor_tensor(g[:, :, :], g[:, :, :], all_of(2), ALU.add))
                link(V.tensor_reduce(scores[:, :, :], g4.rearrange("n b k e -> n b e k"), X, ALU.add))
                V.tensor_scalar(scores[:, :, :], scores[:, :, :], 1.0 / K, None, ALU.mult)


def pool_tokens(nc, tag, x_dram, h, wq, wk, wv, wo, cols, cls, ident):
    H, L, G, R, PAIRS = 8, 64, 64, 4, B // 2
    IH = 2 * H
    with stage(nc, tag, "loaded_even", "loaded_odd", "ones", "masks", "summed", "sums", "regrouped", "meaned", "q_made", "q_saved", "spread", "qk_made", "qk_saved",
               "qb_made", "qb_saved", "scores", "scored", "maxed", "shifted", "exped", "totals", "inverted", "probs",
               "x_turned", "x_saved", "p_turned", "p_saved", "ctx", "ctx_saved", "v_made", "v_saved", "o_made", "out", "passed") as (s, sb, ps):
        x = sb("x", [128, 2, 4096])
        xr = sb("xr", [128, 2, G, L])
        xT = sb("xt", [128, 2, 8, R, 128])
        q = sb("q", [128, PAIRS, G])
        qp = sb("qp", [128, 2, G])
        qb = sb("qb", [128, 2, 16])
        mask = sb("mask", [128, 32])
        bmask = sb("bmask", [128, 32])
        qm = sb("qm", [128, G, IH])
        A = sb("a", [128, 2, G, 32])
        z = sb("z", [128, 16, L])
        stat = sb("stat", [128, 3, 16])
        pT = sb("pt", [128, 8, 128])
        ctx = sb("ctx", [128, PAIRS, H, G])
        v = sb("v", [128, PAIRS * G])
        psC = [ps(f"c{p}", [128, 512]) for p in range(2)]
        psA = ps("ka", [128, 2, 512])
        psS = ps("s", [128, 2, 512])
        psT = [ps(f"t{p}", [128, 512]) for p in range(2)]
        V = nc.vector

        def pipeline(engine, front, mid, back):
            front(0, 0)
            with engine.Fori(0, PAIRS // 2 - 1) as i:
                for u in range(2):
                    mid(i * 2 + u, u)
                    front(i * 2 + (u + 1), 1 - u)
                    back(i * 2 + u, u)
            n = PAIRS - 2
            mid(n, 0)
            front(n + 1, 1)
            back(n, 0)
            mid(n + 1, 1)
            back(n + 1, 1)

        with nc.Block() as block:
            @block.sync
            def _(sp):
                for n in range(PAIRS):
                    if n >= 2:
                        sp.wait_ge(s["regrouped"], (n - 1) * 8)
                    sp.dma_start(x[:, n % 2, :], x_dram[2 * n:2 * n + 2].rearrange("i d w h -> (i d) (w h)")).then_inc(s["loaded_odd" if n % 2 else "loaded_even"], 16)

            @block.gpsimd
            def _(pool):
                P = nc.gpsimd
                P.memset(mask[:, :], 1.0).then_inc(s["ones"], 1)
                P.memset(A[:, :, :, :], 0.0).then_inc(s["ones"], 1)
                pool.wait_ge(s["ones"], 1)
                P.affine_select(out=mask[:, :], in_=mask[:, :], compare_op=ALU.is_ge, fill=0.0, base=0,
                                pattern=[[-8, 32]], channel_multiplier=1).then_inc(s["ones"], 1)
                pool.wait_ge(s["ones"], 3)
                P.affine_select(out=mask[:, :], in_=mask[:, :], compare_op=ALU.is_ge, fill=0.0, base=7,
                                pattern=[[8, 32]], channel_multiplier=-1).then_inc(s["ones"], 1)
                pool.wait_ge(s["ones"], 4)
                P.tensor_scalar(bmask[:, :], mask[:, :], cols[:, 1:2], None, ALU.mult).then_inc(s["masks"], 1)

                def regroup(i, u):
                    wait_alone(pool, s["loaded_odd" if u else "loaded_even"], i * 16 + 16, s["passed"])
                    for w in range(8):
                        P.tensor_copy(xr[:, u, w * 8:(w + 1) * 8, :].rearrange("p h (a b) -> p h a b", b=8),
                                      x[:, u, w * 512:(w + 1) * 512].rearrange("p (a h b) -> p h a b", a=8, h=8)).then_inc(s["regrouped"], 1)

                regroup(0, 0)
                regroup(0, 1)
                with pool.Fori(1, PAIRS // 2) as i:
                    for u in range(2):
                        wait_alone(pool, s["scores"], i * 2 + (u - 1), s["passed"])
                        regroup(i, u)

            @block.tensor
            def _(pe):
                M = nc.tensor.matmul

                def front(n, u):
                    for w in range(8):
                        pe.wait_ge(s["regrouped"], n * 8 + (w + 1))
                        if isinstance(n, int):
                            if n * 8 + w >= 2:
                                pe.wait_ge(s["x_saved"], n * 8 + w - 1)
                        else:
                            pe.wait_ge(s["x_saved"], n * 8 + w - 1)
                        for r in range(R):
                            g = w * 8 + 2 * r
                            mm = nc.tensor.transpose(psT[w % 2][:, r * 128:(r + 1) * 128], xr[:, u, g:g + 2, :], ident[:, :])
                        mm.then_inc(s["x_turned"], 1)
                    pe.wait_ge(s["meaned"], n + 1)
                    M(psC[0][:, 0:G], wq, q_at(n), start=True, stop=True).then_inc(s["q_made"], 1)
                    pe.wait_ge(s["q_saved"], n + 1)
                    for r in range(R):
                        mm = M(psC[0][r * 32:(r + 1) * 32, G:G + 16], bmask[:, :], qp[:, u, :].rearrange("d (w r p) -> d r w p", r=R, p=2)[:, r, :, :],
                               start=True, stop=True, tile_position=(0, r * 32))
                    mm.then_inc(s["qb_made"], 1)
                    pe.wait_ge(s["spread"], n + 1)
                    for c in range(2):
                        mm = M(psA[:, c, :], wk, qm[:, c * 32:(c + 1) * 32, :], start=True, stop=True)
                    mm.then_inc(s["qk_made"], 1)

                def mid(n, u):
                    pe.wait_ge(s["qk_saved"], n + 1)
                    for g in range(G):
                        r, j = g % 8 // 2, g // 8 * 2 + g % 2
                        mm = M(psS[r * 32:(r + 1) * 32, j // 8, (j % 8) * L:(j % 8 + 1) * L], A[:, u, g, :], xr[:, u, g, :],
                               start=True, stop=True, tile_position=(0, r * 32))
                    mm.then_inc(s["scores"], 1)

                def back(n, u):
                    pe.wait_ge(s["probs"], n + 1)
                    pe.wait_ge(s["qk_saved"], later(n))
                    for w in range(8):
                        mm = nc.tensor.transpose(psA[:, w // 4, (w % 4) * 128:(w % 4 + 1) * 128], z[:, 2 * w:2 * w + 2, :], ident[:, :])
                    mm.then_inc(s["p_turned"], 1)
                    pe.wait_ge(s["p_saved"], n + 1)
                    pe.wait_ge(s["qb_saved"], later(n))
                    for p in range(2):
                        for w in range(8):
                            for r in range(R):
                                mm = M(psC[p][:, (w * R + r) * IH:(w * R + r + 1) * IH], xT[p * 64:(p + 1) * 64, u, w, r, :],
                                       pT[p * 64:(p + 1) * 64, w, r * 32:r * 32 + IH], start=True, stop=True)
                    mm.then_inc(s["ctx"], 1)
                    pe.wait_ge(s["ctx_saved"], n + 1)

                later = lambda n: n + 2 if not isinstance(n, int) else min(n + 2, PAIRS)
                q_at = lambda n: q[:, n, :] if isinstance(n, int) else q[:, bass.ds(n, 1), :].rearrange("p a g -> p (a g)")
                pe.wait_ge(s["masks"], 1)
                pipeline(pe, front, mid, back)
                for hd in range(H):
                    mm = M(psT[0][:, :].rearrange("p (n g) -> p n g", g=G), wv[:, hd, :], ctx[:, :, hd, :], start=(hd == 0), stop=(hd == H - 1))
                mm.then_inc(s["v_made"], 1)
                pe.wait_ge(s["v_saved"], 1)
                for i in range(2):
                    M(psC[i][0:D, :], wo[:, i * D:(i + 1) * D], v[:, :], start=True, stop=False)
                    M(psC[i][0:D, :], ident[:, i * D:(i + 1) * D], q[:, :, :], start=False, stop=True).then_inc(s["o_made"], 1)

            @block.scalar
            def _(act):
                def front(n, u):
                    for w in range(8):
                        act.wait_ge(s["x_turned"], n * 8 + (w + 1))
                        nc.scalar.copy(xT[:, u, w, :, :], psT[w % 2][:, :].rearrange("p (r d) -> p r d", r=R)).then_inc(s["x_saved"], 1)
                    act.wait_ge(s["qk_made"], n + 1)
                    nc.scalar.copy(A[:, u, :, 0:IH], psA[:, :, :].rearrange("p c (g h) -> p (c g) h", h=IH)).then_inc(s["qk_saved"], 1)

                def mid(n, u):
                    act.wait_ge(s["shifted"], n + 1)
                    nc.scalar.activation(z[:, :, :], z[:, :, :], ACT.Exp, scale=8.0 ** -0.5).then_inc(s["exped"], 1)

                def back(n, u):
                    act.wait_ge(s["p_turned"], n + 1)
                    nc.scalar.copy(pT[:, :, :], psA[:, :, :].rearrange("p c (w r) -> p (c w) r", r=128)).then_inc(s["p_saved"], 1)

                act.wait_ge(s["ones"], 2)
                pipeline(act, front, mid, back)
                act.wait_ge(s["v_made"], 1)
                nc.scalar.activation(v[:, :], psT[0][:, :], ACT.Identity, bias=cols[:, 2:3]).then_inc(s["v_saved"], 1)

            @block.vector
            def _(dve):
                def front(n, u):
                    dve.wait_ge(s["regrouped"], n * 8 + 8)
                    V.tensor_reduce(q_of(n), xr[:, u, :, :], X, ALU.add).then_inc(s["sums"], 1)
                    dve.wait_ge(s["sums"], n + 1)
                    V.tensor_scalar(q_of(n), q_of(n), 1.0 / L, None, ALU.mult).then_inc(s["meaned"], 1)
                    dve.wait_ge(s["q_made"], n + 1)
                    V.tensor_scalar(qp[:, u, :], psC[0][:, 0:G], cols[:, 0:1], None, ALU.add).then_inc(s["q_saved"], 1)
                    dve.wait_ge(s["q_saved"], n + 1)
                    V.tensor_tensor(qm[:, :, :], qp[:, u, :].unsqueeze(2).to_broadcast([128, G, IH]),
                                    mask[:, 0:IH].unsqueeze(1).to_broadcast([128, G, IH]), ALU.mult).then_inc(s["spread"], 1)
                    dve.wait_ge(s["qb_made"], n + 1)
                    V.tensor_copy(qb[:, u, :], psC[0][:, G:G + 16]).then_inc(s["qb_saved"], 1)

                wide = lambda t: t.unsqueeze(2).to_broadcast([128, 16, L])

                def mid(n, u):
                    dve.wait_ge(s["qb_saved"], n + 1)
                    dve.wait_ge(s["scores"], n + 1)
                    if not (isinstance(n, int) and n == 0):
                        dve.wait_ge(s["p_turned"], n)
                    V.tensor_tensor(z[:, :, :], psS[:, :, :].rearrange("p c (j l) -> p (c j) l", l=L), wide(qb[:, u, :]), ALU.add).then_inc(s["scored"], 1)
                    dve.wait_ge(s["scored"], n + 1)
                    V.tensor_reduce(stat[:, 0, :], z[:, :, :], X, ALU.max).then_inc(s["maxed"], 1)
                    dve.wait_ge(s["maxed"], n + 1)
                    V.tensor_tensor(z[:, :, :], z[:, :, :], wide(stat[:, 0, :]), ALU.subtract).then_inc(s["shifted"], 1)

                def back(n, u):
                    dve.wait_ge(s["exped"], n + 1)
                    V.tensor_reduce(stat[:, 1, :], z[:, :, :], X, ALU.add).then_inc(s["totals"], 1)
                    dve.wait_ge(s["totals"], n + 1)
                    V.reciprocal(stat[:, 2, :], stat[:, 1, :]).then_inc(s["inverted"], 1)
                    dve.wait_ge(s["inverted"], n + 1)
                    V.tensor_tensor(z[:, :, :], z[:, :, :], wide(stat[:, 2, :]), ALU.mult).then_inc(s["probs"], 1)
                    dve.wait_ge(s["ctx"], n + 1)
                    for i in range(2):
                        for p in range(2):
                            mine = ctx_of(n, i).rearrange("d h (w r p) -> d p h w r", w=8, p=2)[:, p, :, :, :]
                            made = psC[p][i * 64:(i + 1) * 64, :].rearrange("d (w r i h) -> d i h w r", w=8, r=R, i=2)[:, i, :, :, :]
                            last = V.tensor_copy(mine, made)
                    last.then_inc(s["ctx_saved"], 1)

                q_of = lambda n: q[:, n, :] if isinstance(n, int) else q[:, bass.ds(n, 1), :].rearrange("p a g -> p (a g)")
                ctx_of = lambda n, i: (ctx[i * 64:(i + 1) * 64, n, :, :] if isinstance(n, int) else
                                       ctx[i * 64:(i + 1) * 64, bass.ds(n, 1), :, :].rearrange("p a h g -> p (a h) g"))
                dve.wait_ge(s["masks"], 1)
                pipeline(dve, front, mid, back)
                V.tensor_copy(h[:, :].rearrange("d (b n) -> d b n", n=N)[:, :, 0], cls.to_broadcast([D, B])).then_inc(s["out"], 1)
                for i in range(2):
                    dve.wait_ge(s["o_made"], i + 1)
                    V.tensor_scalar(h[:, :].rearrange("d (m i n) -> d i m n", i=2, n=N)[:, i, :, 1:N], psC[i][0:D, :].rearrange("d (m g) -> d m g", g=G),
                                    cols[0:D, 3:4], None, ALU.add).then_inc(s["out"], 1)


def constants(nc, ones, ident, pick, causal, alibi):
    EXPERTS = pick.shape[0]
    with stage(nc, "const", "filled", "cut", "chain") as (s, sb, ps):
        with nc.Block() as block:
            @block.gpsimd
            def _(pool):
                P = nc.gpsimd
                P.memset(ones[:, :], 1.0 / D).then_inc(s["filled"], 1)
                P.memset(ident[:, :], 0.0).then_inc(s["filled"], 1)
                P.memset(pick[:, :, :], 0.0).then_inc(s["filled"], 1)
                P.memset(causal[:, :], 0.0).then_inc(s["filled"], 1)
                P.iota(alibi[:, :, :], [[0, 8], [1, N]], base=0, channel_multiplier=-1, allow_small_or_imprecise_dtypes=True).then_inc(s["filled"], 1)
                pool.wait_ge(s["filled"], 5)
                P.affine_select(out=ident[:, :], in_=ident[:, :], compare_op=ALU.not_equal, fill=1.0, base=0,
                                pattern=[[-1, 128]], channel_multiplier=1).then_inc(s["cut"], 1)
                P.affine_select(out=pick[:, :, :], in_=pick[:, :, :], compare_op=ALU.not_equal, fill=1.0, base=0,
                                pattern=[[-1, EXPERTS], [0, 128]], channel_multiplier=1).then_inc(s["cut"], 1)
                P.affine_select(out=causal[:, :], in_=causal[:, :], compare_op=ALU.is_ge, fill=NEG, base=0,
                                pattern=[[-1, N]], channel_multiplier=1).then_inc(s["cut"], 1)
                for place in range(8):
                    head = place % 2 * 4 + place // 2
                    P.tensor_scalar(alibi[:, place, :], alibi[:, place, :], 0.5 ** (head + 1) * 32.0 ** 0.5, None, ALU.mult).then_inc(s["chain"], 1)
                pool.wait_ge(s["chain"], 8)
                P.affine_select(out=alibi[:, :, :], in_=alibi[:, :, :], compare_op=ALU.is_ge, fill=NEG, base=0,
                                pattern=[[0, 8], [-1, N]], channel_multiplier=1).then_inc(s["cut"], 1)
                pool.wait_ge(s["cut"], 4)


def window_bias(nc, window, toeplitz, last):
    WS = toeplitz.shape[0]
    with stage(nc, "window", "filled", "loaded", "scaled") as (s, sb, ps):
        with nc.Block() as block:
            @block.gpsimd
            def _(pool):
                nc.gpsimd.memset(window[:, :], NEG).then_inc(s["filled"], 1)
                pool.wait_ge(s["loaded"], 32)
                nc.gpsimd.tensor_scalar(window[:, :], window[:, :], 8.0 ** 0.5, None, ALU.mult).then_inc(s["scaled"], 1)

            @block.sync
            def _(sp):
                sp.wait_ge(s["filled"], 1)
                sp.dma_start(window[0:WS, 0:WS], toeplitz).then_inc(s["loaded"], 16)
                sp.dma_start(window[WS:N, WS:2 * WS], last).then_inc(s["loaded"], 16)


def load(nc, tag, pairs):
    with stage(nc, tag, "loaded") as (s, sb, ps):
        with nc.Block() as block:
            @block.sync
            def _(sp):
                for to, source in pairs[0::2]:
                    sp.dma_start(to, source).then_inc(s["loaded"], 16)
                sp.wait_ge(s["loaded"], 16 * len(pairs))

            @block.scalar
            def _(act):
                for to, source in pairs[1::2]:
                    act.dma_start(to, source).then_inc(s["loaded"], 16)


def store(nc, h, out):
    with stage(nc, "store", "stored") as (s, sb, ps):
        with nc.Block() as block:
            @block.sync
            def _(sp):
                sp.dma_start(out, h[:, :]).then_inc(s["stored"], 16)
                sp.wait_ge(s["stored"], 16)


def weights(nc, stack, dram, *names):
    to = {n: stack.enter_context(nc.sbuf_tensor(f"w_{n}", list(dram[n].shape), F32)) for n in names}
    load(nc, "load_" + names[0], [(to[n][tuple(slice(None) for _ in dram[n].shape)], dram[n]) for n in names])
    return to


def tower(nc, dram, out):
    E = 4
    with stage(nc, "tower") as (_, sb, _ps), ExitStack() as stack:
        h, x = sb("h", [D, T]), sb("x", [D, T])
        ones, ident = sb("ones", [D, D]), sb("ident", [128, 128])
        pick = sb("pick", [8, 8, 128])
        causal, window = sb("causal", [N, N]), sb("window", [N, 2 * 64])
        wT = sb("wt", [8, T])
        with ExitStack() as early:
            alibi = early.enter_context(nc.sbuf_tensor("alibi", [N, 8, N], F32))
            constants(nc, ones, ident, pick, causal, alibi)
            window_bias(nc, window, dram["a2_toeplitz"], dram["a2_last"])

            with ExitStack() as own:
                w = weights(nc, own, dram, "tok_wq", "tok_wk", "tok_wv", "tok_wo", "tok_cols", "cls")
                pool_tokens(nc, "tok", dram["x"], h, w["tok_wq"][:, :], w["tok_wk"][:, :], w["tok_wv"], w["tok_wo"], w["tok_cols"], w["cls"][:, 0:1], ident)

            w = weights(nc, early, dram, "a0_wq", "a0_wkv", "a0_wo", "a0_bo", "f0_gw", "f0_gb", "f0_sW1", "f0_sW2", "f0_sW3", "f0_sb",
                        "f0_eW1", "f0_eW2", "f0_eW3", "f0_eb1", "f0_eb2", "f0_eb3", "a1_wqk", "a1_wv", "a1_wo", "a1_bo")
            layer_norm(nc, "a0_ln", h, x, ones)
            linear_attention(nc, "a0", x, h, w["a0_wq"], w["a0_wkv"], w["a0_wo"], w["a0_bo"][:, 0:1])
            layer_norm(nc, "f0_ln", h, x, ones)
            top2(nc, "f0_top", wT[0:E], ident, E, "softmax of gates", x=x, gw=w["f0_gw"][:, :], gb=w["f0_gb"][:, :])
            each = lambda name: [w[name][:, e, :] for e in range(E)]
            column = lambda name: [w[name][:, e:e + 1] for e in range(E)]
            relu_experts(nc, "f0", x, h, wT[0:E], pick[0:E], [w["f0_sW1"][:, :]] + each("f0_eW1"), [w["f0_sb"][0:D, 0:1]] + column("f0_eb1"),
                         [w["f0_sW2"][:, :]] + each("f0_eW2"), [w["f0_sb"][:, 1:2]] + column("f0_eb2"),
                         [w["f0_sW3"][:, :]] + each("f0_eW3"), w["f0_sb"][0:D, 2:3], w["f0_eb3"][:, :])
            layer_norm(nc, "a1_ln", h, x, ones)
            attention(nc, "a1", x, h, w["a1_wqk"], w["a1_wv"][:, :], w["a1_wo"], ident, heads=8, hp=32, scale=32.0 ** -0.5,
                      bias=alibi[:, :, :].rearrange("n (r j) c -> n r j c", r=4), bo=w["a1_bo"][:, 0:1])
        with ExitStack() as own:
            w = weights(nc, own, dram, "f1_wqpk", "f1_keys", "f1_wq", "f1_wo")
            layer_norm(nc, "f1_ln", h, x, ones)
            kv = own.enter_context(nc.sbuf_tensor("f1_kv", [128, 8, T], F32))
            product_keys(nc, "f1_keys", x, w["f1_wqpk"], w["f1_keys"], dram["f1_table"], kv, ident)
            attention(nc, "f1", x, h, w["f1_wq"], None, w["f1_wo"], ident, heads=8, hp=64, scale=64.0 ** -0.5, kv=kv,
                      bias=causal[:, :].unsqueeze(1).unsqueeze(1).to_broadcast([N, 2, 4, N]))
        with ExitStack() as own:
            w = weights(nc, own, dram, "a2_wqk", "a2_wv", "a2_wo", "a2_bo", "f2_wgat", "f2_att", "f2_att_col", "f2_rows", "f2_w1", "f2_b1", "f2_w2", "f2_b2")
            layer_norm(nc, "a2_ln", h, x, ones)
            attention(nc, "a2", x, h, w["a2_wqk"], w["a2_wv"][:, :], w["a2_wo"], ident, heads=8, hp=32, scale=8.0 ** -0.5, keys=128,
                      bo=w["a2_bo"][:, 0:1], bias=window[:, :].unsqueeze(1).unsqueeze(1).to_broadcast([N, 4, 2, 128]))
            layer_norm(nc, "f2_ln", h, x, ones)
            scores = own.enter_context(nc.sbuf_tensor("f2_scores", [N, B, E], F32))
            with ExitStack() as graph:
                countT = graph.enter_context(nc.sbuf_tensor("f2_count", [TT, NT, T], F32))
                absent = graph.enter_context(nc.sbuf_tensor("f2_absent", [TT, NT, T], F32))
                edge_counts(nc, "f2_edges", dram["f2_src"], dram["f2_dst"], ident, countT, absent)
                graph_scores(nc, "f2_gat", x, w["f2_wgat"][:, :], w["f2_att"], w["f2_att_col"][:, 0:1], w["f2_rows"], ident, pick, countT, absent, scores)
            top2(nc, "f2_top", wT[0:E], ident, E, "softmax", scores=scores)
            gelu_experts(nc, "f2", x, h, wT[0:E], pick[0:E], w["f2_w1"], w["f2_b1"], w["f2_w2"], w["f2_b2"][:, :], E, 2 * D)
        with ExitStack() as own:
            w = weights(nc, own, dram, "a3_wqk", "a3_wv", "a3_wo", "a3_wg", "a3_bg", "a3_cols", "f3_wqk", "f3_wv", "f3_wo", "f3_rope", "f3_cols",
                        "f3_router", "f3_w1", "f3_w3", "f3_w2")
            xn = own.enter_context(nc.sbuf_tensor("xn", [D, T], F32))
            gate = own.enter_context(nc.sbuf_tensor("a3_gate", [128, 2, T], F32))
            layer_norm(nc, "a3_ln", h, x, ones)
            layer_norm(nc, "a3_ln2", x, xn, ones, gain=w["a3_cols"][:, 1:2], shift=w["a3_cols"][:, 2:3])
            gate_values(nc, "a3_gate", x, h, w["a3_wg"], w["a3_bg"], gate)
            attention(nc, "a3", xn, h, w["a3_wqk"], w["a3_wv"][:, :], w["a3_wo"], ident, heads=8, hp=32, scale=32.0 ** -0.5,
                      bo=w["a3_cols"][:, 0:1], gate=gate, over_queries=True)
            layer_norm(nc, "f3_ln", h, x, ones)
            layer_norm(nc, "f3_ln1", x, xn, ones, eps=1e-6, center=False, gain=w["f3_cols"][:, 0:1])
            attention(nc, "f3_att", xn, x, w["f3_wqk"], w["f3_wv"][:, :], w["f3_wo"], ident, heads=4, hp=32, scale=16.0 ** -0.5, rope=w["f3_rope"],
                      bias=causal[:, :].unsqueeze(1).unsqueeze(1).to_broadcast([N, 4, 1, N]))
            layer_norm(nc, "f3_ln2", x, xn, ones, eps=1e-6, center=False, gain=w["f3_cols"][:, 1:2])
            top2(nc, "f3_top", wT, ident, 8, "share", x=xn, gw=w["f3_router"][:, :])
            silu_experts(nc, "f3", xn, h, x, wT, pick, w["f3_w1"], w["f3_w3"], w["f3_w2"], 8, 85)
        store(nc, h, out)


def blocks(w):
    z = np.zeros((2, D, 2, D), w.dtype)
    z[0, :, 0], z[1, :, 1] = w, w
    return z.reshape(2 * D, 2 * D)


def padded_heads(w, of, size, swap=False):
    z = np.zeros((w.shape[0], len(of), 32), w.dtype)
    for place, head in enumerate(of):
        part = w[:, head * size:(head + 1) * size]
        z[:, place, :size] = np.roll(part, size // 2, axis=1) if swap else part
    return z.reshape(w.shape[0], -1)


def lay_out(inputs):
    g = {n: np.asarray(a) for n, a in inputs.items()}
    out = {"x": g["x"]}
    t = lambda n: g["L0_tok_" + n]
    wv = np.zeros((8, D, D), np.float32)
    for head in range(8):
        wv[head][:, head * 8:head * 8 + 8] = t("Wv").T[:, head * 8:head * 8 + 8]
    out.update(tok_wq=blocks(t("Wq").T), tok_wk=blocks(t("Wk")), tok_wv=np.stack([blocks(w) for w in wv], 1), tok_wo=blocks(t("Wo").T),
               tok_cols=np.tile(np.stack([t(n) for n in ("bq", "bk", "bv", "bo")], 1), (2, 1)), cls=g["cls_tok"].reshape(D, 1))
    w = g["L0_attn_w_qkv"].T
    out.update(a0_wq=w[:, :512].reshape(D, 4, 128), a0_wkv=w[:, 512:].reshape(D, 16, 64), a0_bo=g["L0_attn_b_out"].reshape(D, 1),
               a0_wo=g["L0_attn_w_out"].T.reshape(4, 128, D).transpose(1, 0, 2))
    t = lambda n: g["L0_ffn_" + n]
    sb = np.zeros((128, 3), np.float32)
    sb[:D, 0], sb[:, 1], sb[:D, 2] = t("sb1"), t("sb2"), t("sb3")
    out.update(f0_gw=t("gW"), f0_gb=np.broadcast_to(t("gb"), (N, 4)), f0_sW1=t("sW1"), f0_sW2=t("sW2"), f0_sW3=t("sW3"), f0_sb=sb,
               f0_eW1=t("eW1").transpose(1, 0, 2), f0_eW2=t("eW2").transpose(1, 0, 2), f0_eW3=t("eW3").transpose(1, 0, 2),
               f0_eb1=t("eb1").T, f0_eb2=t("eb2").T, f0_eb3=t("eb3"))
    t = lambda n: g["L1_attn_" + n]
    out.update(a1_wqk=np.stack([t("Wq")[:, :128], t("Wq")[:, 128:], t("Wk")[:, :128], t("Wk")[:, 128:]], 1), a1_wv=t("Wv"),
               a1_wo=t("Wo").reshape(2, 128, D).transpose(1, 0, 2), a1_bo=t("bo").reshape(D, 1))
    t = lambda n: g["L1_ffn_" + n]
    keys, values = t("keys_table").reshape(8, 4096, D), t("values_table").reshape(8, 4096, D)
    table = np.empty((8, 4096, 2 * D), np.float32)
    table[0::2, :, :D], table[0::2, :, D:] = keys[0::2], values[0::2]
    table[1::2, :, :D], table[1::2, :, D:] = values[1::2], keys[1::2]
    out.update(f1_wqpk=t("Wq_pk").reshape(D, 4, 128), f1_keys=t("pk_keys").transpose(0, 2, 3, 1).reshape(4, 128, 64).transpose(1, 0, 2),
               f1_table=table.reshape(-1, 2 * D), f1_wq=t("Wq").reshape(D, 4, 128), f1_wo=t("Wo").reshape(4, 128, D).transpose(1, 0, 2))
    t = lambda n: g["L2_attn_" + n]
    w = t("w_qkv").T
    first, second = range(0, 4), range(4, 8)
    q, k, v = (w[:, n * D:(n + 1) * D] for n in range(3))
    toeplitz = t("rel_bias")[np.arange(64)[None] - np.arange(64)[:, None] + 63]
    wo = np.zeros((4, 32, 2, D), np.float32)
    wo[:, :8] = t("w_proj").T.reshape(2, 4, 8, D).transpose(1, 2, 0, 3)
    out.update(a2_wqk=np.stack([padded_heads(m, heads, 8) for m in (q, k) for heads in (first, second)], 1), a2_wv=padded_heads(v, range(8), 8),
               a2_wo=wo.reshape(128, 2, D), a2_bo=t("b_proj").reshape(D, 1), a2_toeplitz=toeplitz, a2_last=t("rel_bias")[63:].reshape(1, 64))
    t = lambda n: g["L2_ffn_" + n]
    out.update(f2_wgat=t("W_gat"), f2_att=np.broadcast_to(np.stack([t("att_src").reshape(16), t("att_dst").reshape(16)]), (TT, 2, 16)),
               f2_att_col=t("att_src").reshape(16, 1), f2_rows=np.broadcast_to(np.stack([t("b_gat"), t("ln_gamma"), t("ln_beta")]), (N, 3, 16)),
               f2_w1=t("W1").transpose(1, 0, 2), f2_b1=t("b1").T, f2_w2=t("W2").transpose(1, 0, 2), f2_b2=t("b2"),
               f2_src=t("edge_index")[0], f2_dst=t("edge_index")[1])
    t = lambda n: g["L3_attn_" + n]
    w = t("W_qkv").T
    out.update(a3_wqk=w[:, :512].reshape(D, 4, 128), a3_wv=w[:, 512:], a3_wo=t("W_final").T.reshape(2, 128, D).transpose(1, 0, 2),
               a3_wg=t("W_gate").T.reshape(D, 2, 128), a3_bg=t("b_gate").reshape(2, 128).T,
               a3_cols=np.stack([t("b_final"), t("ln_gamma"), t("ln_beta")], 1))
    t = lambda n: g["L3_ffn_" + n]
    own, shared = range(4), (0, 0, 1, 1)
    q, k, v = t("wq").T, t("wk").T, t("wv").T
    wo = np.zeros((4, 32, D), np.float32)
    wo[:, :16] = t("wo").T.reshape(4, 16, D)
    angle = np.outer(np.arange(N, dtype=np.float32), 1.0 / 10000.0 ** (np.arange(0, 16, 2, dtype=np.float32) / 16))
    rope = np.zeros((4, 32, 2, N), np.float32)
    rope[:, 0:8, 0] = rope[:, 8:16, 0] = np.cos(angle).T
    rope[:, 0:8, 1], rope[:, 8:16, 1] = -np.sin(angle).T, np.sin(angle).T
    out.update(f3_wqk=np.stack([padded_heads(q, own, 16), padded_heads(k, shared, 16), padded_heads(q, own, 16, True), padded_heads(k, shared, 16, True)], 1),
               f3_wv=padded_heads(v, shared, 16), f3_wo=wo.reshape(128, 1, D), f3_rope=rope.reshape(128, 2, N),
               f3_cols=np.stack([t("ln1_w"), t("ln2_w")], 1), f3_router=t("router_w").T,
               f3_w1=t("w1").transpose(2, 0, 1).reshape(D, 8, 2, 85), f3_w3=t("w3").transpose(2, 0, 1).reshape(D, 8, 2, 85),
               f3_w2=t("w2").transpose(2, 0, 1).reshape(2, 85, 8, D).transpose(1, 2, 0, 3))
    return {n: np.ascontiguousarray(a) for n, a in out.items()}


def kernel(**inputs):
    import concourse.bacc as _bacc
    from concourse.bass_utils import run_bass_kernel_spmd as _run

    nc = _bacc.Bacc("TRN2", target_bir_lowering=False, num_devices=1)
    arrays = {f"in_{n}": a for n, a in lay_out(inputs).items()}
    dram = {n[3:]: nc.dram_tensor(n, a.shape, mybir.dt.from_np(a.dtype), kind="ExternalInput").ap() for n, a in arrays.items()}
    out = nc.dram_tensor("tokens_out", (D, T), F32, kind="ExternalOutput").ap()
    tower(nc, dram, out)
    r = _run(nc, [arrays], core_ids=[0])
    return r.results[0]["tokens_out"].T.reshape(B, N, D)
```

```python
from contextlib import ExitStack, contextmanager

import numpy as np
import concourse.bass as bass
from concourse import mybir

F32 = mybir.dt.float32
BF16 = mybir.dt.bfloat16
U32 = mybir.dt.uint32
I32 = mybir.dt.int32
ALU = mybir.AluOpType
ACT = mybir.ActivationFunctionType
X = mybir.AxisListType.X

B, N, D = 16, 65, 64
T = B * N
IPC = 4
CH = IPC * N
NC = T // CH
NEG = -1.0e30


@contextmanager
def stage(nc, tag, *signals):
    sems = {s: nc.alloc_semaphore(f"{tag}_{s}") for s in signals}
    with ExitStack() as stack:
        def sb(name, shape, dt=F32):
            return stack.enter_context(nc.sbuf_tensor(f"{tag}_{name}", shape, dt))

        def ps(name, shape, dt=F32):
            return stack.enter_context(nc.psum_tensor(f"{tag}_{name}", shape, dt))

        yield sems, sb, ps
    nc.clear_and_free_semaphores(list(sems.values()))
    nc.all_engine_barrier()


def wait_alone(engine, signal, value, passed):
    engine.wait_ge(signal, value)
    engine.sem_inc(passed, 1)


def layer_norm(nc, tag, src, dst, ones, eps=1e-5, center=True, gain=None, shift=None):
    with stage(nc, tag, "mean", "centered", "squared", "var", "std", "rstd", "normed", "gained", "eps") as (s, sb, ps):
        mean_ps = ps("mean", [2 * D, 2, 512]) if center else None
        var_ps = ps("var", [2 * D, 2, 512])
        cent = sb("cent", [2 * D, 2, CH])
        sq = sb("sq", [2 * D, 2, CH])
        rstd = sb("rstd", [2 * D, 2, CH])
        std = sb("std", [2 * D, 2, CH])
        eps_col = sb("eps", [2 * D, 1])
        unused = sb("unused", [2 * D, 1])
        tok = lambda t, c: t[:, c * CH:(c + 1) * CH]
        place = [(a, b, 2 * a + b) for b in range(2) for a in range(2)]
        half = lambda t, a, b: t[a * D:(a + 1) * D, b, 0:CH]
        with nc.Block() as block:
            @block.tensor
            def _(pe):
                if center:
                    for a, b, c in place:
                        nc.tensor.matmul(half(mean_ps, a, b), ones[0:D, 0:D], tok(src, c), start=True, stop=True).then_inc(s["mean"], 1)
                for b in range(2):
                    pe.wait_ge(s["squared"], b + 1)
                    nc.tensor.matmul(var_ps[:, b, 0:CH], ones[:, :], sq[:, b, :], start=True, stop=True).then_inc(s["var"], 1)

            @block.gpsimd
            def _(pool):
                nc.gpsimd.memset(eps_col[:, :], eps).then_inc(s["eps"], 1)

            @block.scalar
            def _(act):
                act.wait_ge(s["eps"], 1)
                nc.scalar.activation(unused[:, :], eps_col[:, :], ACT.Sqrt)
                for b in range(2):
                    act.wait_ge(s["var"], b + 1)
                    nc.scalar.activation(std[:, b, :], var_ps[:, b, 0:CH], ACT.Sqrt, bias=eps_col[:, 0:1]).then_inc(s["std"], 1)

            @block.vector
            def _(dve):
                V = nc.vector
                for n, (a, b, c) in enumerate(place):
                    if center:
                        dve.wait_ge(s["mean"], 2 * b + 2)
                        V.tensor_tensor(half(cent, a, b), tok(src, c), half(mean_ps, a, b), ALU.subtract).then_inc(s["centered"], 1)
                    else:
                        V.tensor_copy(half(cent, a, b), tok(src, c)).then_inc(s["centered"], 1)
                    if a == 1:
                        dve.wait_ge(s["centered"], n + 1)
                        V.tensor_tensor(sq[:, b, :], cent[:, b, :], cent[:, b, :], ALU.mult).then_inc(s["squared"], 1)
                for b in range(2):
                    dve.wait_ge(s["std"], b + 1)
                    V.reciprocal(rstd[:, b, :], std[:, b, :]).then_inc(s["rstd"], 1)
                for n, (a, b, c) in enumerate(place):
                    dve.wait_ge(s["rstd"], b + 1)
                    V.tensor_tensor(tok(dst, c), half(cent, a, b), half(rstd, a, b), ALU.mult).then_inc(s["normed"], 1)
                if gain is not None:
                    for n, (a, b, c) in enumerate(place):
                        dve.wait_ge(s["normed"], n + 1)
                        if shift is not None:
                            V.tensor_scalar(tok(dst, c), tok(dst, c), gain, shift, ALU.mult, ALU.add).then_inc(s["gained"], 1)
                        else:
                            V.tensor_scalar(tok(dst, c), tok(dst, c), gain, None, ALU.mult).then_inc(s["gained"], 1)


def attention(nc, tag, x, h, wqk, wv, wo, ident, *, heads, hp, scale, bias=None, bo=None, keys=N,
              kv=None, rope=None, gate=None, over_queries=False):
    per = 128 // hp
    nb = heads // per
    nq = wqk.shape[1]
    banks = heads // 4
    PROJ = 5 * N
    img = lambda t, m: t[:, m * N:(m + 1) * N] if isinstance(m, int) else t[:, bass.ds(m * N, N)]
    imgs = lambda t, m: t[:, :, m * N:(m + 1) * N] if isinstance(m, int) else t[:, :, bass.ds(m * N, N)]
    with stage(nc, tag, "x_copied", "kv_copied", "pads", "qk_made", "qk_saved", "v_made", "v_saved", "scores", "masked", "maxed",
               "shifted", "exped", "summed", "inverted", "probs", "turned", "turned_saved", "summed_v",
               "out_saved", "projected", "added", "roped", "passed") as (s, sb, ps):
        xb = sb("xb", [D, 2, N])
        spread_q = kv is not None
        qx = sb("qx", [128, 2, nb, per if spread_q else 1, N])
        kx = None if spread_q else sb("kx", [128, 2, nb, per, keys])
        vt = sb("vt", [N, 2, heads * hp])
        kvb = sb("kvb", [128, 2, heads, N]) if spread_q else None
        rp = sb("rp", [128, 2, 2, 2, N]) if rope is not None else None
        z = sb("z", [N, 2, heads, keys])
        stat = sb("stat", [N, 2, 3, heads])
        pt = sb("pt", [N, 2, heads, N])
        ot = sb("ot", [128, 2, nb, N])
        psA = [ps(f"a{u}", [128, 512]) for u in range(2)]
        psB = [ps(f"b{u}", [128, 512]) for u in range(2)]
        psS = ps("s", [128, 2, 2, 512])
        at = lambda u, hd, n: psS[0:N, u, hd // 4, hd % 4 * keys:hd % 4 * keys + n]
        all_at = lambda u, n: psS[0:N, u, 0:banks, 0:4 * keys].rearrange("n b (r c) -> n b r c", r=4)[:, :, :, 0:n]
        by_bank = lambda t: t.rearrange("n (b r) c -> n b r c", r=4)

        with nc.Block() as block:
            @block.gpsimd
            def _(pool):
                def take(m, u):
                    nc.gpsimd.tensor_copy(xb[:, u, :], img(x, m)).then_inc(s["x_copied"], 1)
                    if spread_q:
                        nc.gpsimd.tensor_copy(kvb[:, u, :, :], imgs(kv, m)).then_inc(s["kv_copied"], 1)

                nc.gpsimd.memset(qx[:, :, :, :, :] if spread_q else kx[:, :, :, :, :], 0.0).then_inc(s["pads"], 1)
                for u in range(2):
                    take(u, u)
                with pool.Fori(1, B // 2) as i:
                    for u in range(2):
                        wait_alone(pool, s["v_made"], i * 2 + (u - 1), s["passed"])
                        if spread_q:
                            wait_alone(pool, s["scores"], i * 2 + (u - 1), s["passed"])
                        take(i * 2 + u, u)

            @block.tensor
            def _(pe):
                M = nc.tensor.matmul

                def make_qk(m, u):
                    pe.wait_ge(s["x_copied"], m + 1)
                    for j in range(nq):
                        mm = M(psA[u][:, j * N:(j + 1) * N], wqk[:, j, :], xb[:, u, :], start=True, stop=True)
                    mm.then_inc(s["qk_made"], 1)

                def make_v(m, u):
                    if spread_q:
                        pe.wait_ge(s["kv_copied"], m + 1)
                        for hd in range(heads):
                            mm = nc.tensor.transpose(psS[0:N, u, hd // 4, hd % 4 * 128:hd % 4 * 128 + 128], kvb[:, u, hd, :], ident[:, :])
                        mm.then_inc(s["v_made"], 1)
                    else:
                        M(psB[u][0:N, 0:heads * hp], xb[:, u, :], wv, start=True, stop=True).then_inc(s["v_made"], 1)

                def score(m, u):
                    pe.wait_ge(s["qk_saved"], m + 1)
                    if spread_q:
                        pe.wait_ge(s["v_saved"], m + 1)
                        for hd in range(heads):
                            mm = M(at(u, hd, N), qx[:, u, hd // per, hd % per, :], kvb[:, u, hd, :], start=True, stop=True)
                    else:
                        for j in range(nb):
                            mm = M(psS[0:N, u, j, 0:per * keys], qx[:, u, j, 0, :], kx[:, u, j, :, :], start=True, stop=True)
                    mm.then_inc(s["scores"], 1)

                def turn(m, u):
                    pe.wait_ge(s["probs"], m + 1)
                    if not over_queries:
                        for hd in range(heads):
                            mm = nc.tensor.transpose(at(u, hd, N), z[:, u, hd, 0:N], ident[0:N, 0:N])
                        mm.then_inc(s["turned"], 1)

                def finish(m, u, last):
                    if not over_queries:
                        pe.wait_ge(s["turned_saved"], m + 1)
                    pe.wait_ge(s["v_saved"], m + 1)
                    if not last:
                        pe.wait_ge(s["qk_saved"], m + 3)
                    for hd in range(heads):
                        p, j = hp * (hd % per), hd // per
                        probs = z[:, u, hd, 0:N] if over_queries else pt[:, u, hd, :]
                        mm = M(psA[u][p:p + hp, j * N:(j + 1) * N], vt[:, u, hd * hp:(hd + 1) * hp], probs, start=True, stop=True)
                    mm.then_inc(s["summed_v"], 1)
                    pe.wait_ge(s["out_saved"], m + 1)
                    for j in range(nb):
                        mm = M(psA[u][0:D, PROJ:PROJ + N], wo[:, j, :], ot[:, u, j, :], start=(j == 0), stop=(j == nb - 1))
                    mm.then_inc(s["projected"], 1)

                def step(m, u):
                    score(m, u)
                    turn(m - 1, 1 - u)
                    if not isinstance(m, int) or m > 1:
                        pe.wait_ge(s["added"], m - 1)
                    make_qk(m + 1, 1 - u)
                    if spread_q:
                        pe.wait_ge(s["turned_saved"], m)
                    make_v(m + 1, 1 - u)
                    finish(m - 1, 1 - u, False)

                pe.wait_ge(s["pads"], 1)
                make_qk(0, 0)
                make_v(0, 0)
                score(0, 0)
                make_qk(1, 1)
                make_v(1, 1)
                step(1, 1)
                with pe.Fori(1, B // 2 - 1) as i:
                    step(i * 2, 0)
                    step(i * 2 + 1, 1)
                step(B - 2, 0)
                score(B - 1, 1)
                for m in (B - 2, B - 1):
                    turn(m, m % 2)
                    finish(m, m % 2, True)

            @block.scalar
            def _(act):
                C = nc.scalar.copy

                def save_qk(m, u):
                    if rope is None:
                        act.wait_ge(s["qk_made"], m + 1)
                        made = psA[u][:, 0:nq * N].rearrange("p (j n) -> p j n", n=N)
                        if not spread_q:
                            C(qx[:, u, :, 0, :], made[:, 0:nb, :])
                        for r in range(per):
                            rows = slice(r * hp, (r + 1) * hp)
                            to = qx[rows, u, :, r, :] if spread_q else kx[rows, u, :, r, 0:N]
                            last = C(to, made[rows, nq - nb:nq, :])
                        last.then_inc(s["qk_saved"], 1)

                def save_v(m, u):
                    act.wait_ge(s["v_made"], m + 1)
                    if spread_q:
                        v_of = vt[:, u, :].rearrange("n (b r two d) -> n b r two d", b=banks, two=2, d=hp)
                        turned = psS[0:N, u, :, :].rearrange("n b (r two c) -> n b r two c", two=2, c=128)
                        C(v_of[:, :, :, 0, :], turned[:, :, :, 0, hp:2 * hp])
                        C(v_of[:, :, :, 1, :], turned[:, :, :, 1, 0:hp]).then_inc(s["v_saved"], 1)
                    else:
                        C(vt[:, u, :], psB[u][0:N, 0:heads * hp]).then_inc(s["v_saved"], 1)

                def save_turned(m, u):
                    if not over_queries:
                        act.wait_ge(s["turned"], m + 1)
                        C(by_bank(pt[:, u, :, :]), all_at(u, N)).then_inc(s["turned_saved"], 1)

                def exp(m, u):
                    act.wait_ge(s["shifted"], m + 1)
                    nc.scalar.activation(z[:, u, :, :], z[:, u, :, :], ACT.Exp, scale=scale).then_inc(s["exped"], 1)

                def save_out(m, u):
                    if gate is None:
                        act.wait_ge(s["summed_v"], m + 1)
                        C(ot[:, u, :, :], psA[u][:, 0:nb * N].rearrange("p (j n) -> p j n", n=N)).then_inc(s["out_saved"], 1)

                def step(m, u):
                    save_turned(m - 1, 1 - u)
                    save_qk(m + 1, 1 - u)
                    exp(m, u)
                    save_out(m - 1, 1 - u)
                    act.wait_ge(s["summed_v"], m)
                    save_v(m + 1, 1 - u)

                act.wait_ge(s["pads"], 1)
                save_qk(0, 0)
                save_v(0, 0)
                save_qk(1, 1)
                exp(0, 0)
                save_v(1, 1)
                with act.Fori(0, B // 2 - 1) as i:
                    step(i * 2 + 1, 1)
                    step(i * 2 + 2, 0)
                save_turned(B - 2, 0)
                exp(B - 1, 1)
                save_out(B - 2, 0)
                save_turned(B - 1, 1)
                save_out(B - 1, 1)

            @block.vector
            def _(dve):
                V = nc.vector

                def rotate(m, u):
                    if rope is not None:
                        made = psA[u][:, 0:nq * N].rearrange("p (a j n) -> p a j n", a=2, n=N)
                        dve.wait_ge(s["qk_made"], m + 1)
                        for a in range(2):
                            last = V.tensor_tensor(rp[:, u, a, :, :], made[:, a, :, :], rope[:, a:a + 1, :].to_broadcast([128, 2, N]), ALU.mult)
                        last.then_inc(s["roped"], 1)
                        dve.wait_ge(s["roped"], m + 1)
                        V.tensor_tensor(qx[:, u, 0, 0, :], rp[:, u, 0, 0, :], rp[:, u, 1, 0, :], ALU.add)
                        for r in range(per):
                            rows = slice(r * hp, (r + 1) * hp)
                            last = V.tensor_tensor(kx[rows, u, 0, r, 0:N], rp[rows, u, 0, 1, :], rp[rows, u, 1, 1, :], ALU.add)
                        last.then_inc(s["qk_saved"], 1)

                def shift(m, u):
                    dve.wait_ge(s["scores"], m + 1)
                    of, zz = all_at(u, keys), by_bank(z[:, u, :, :])
                    if bias is not None:
                        V.tensor_tensor(zz, of, bias, ALU.add).then_inc(s["masked"], 1)
                        dve.wait_ge(s["masked"], m + 1)
                        of = zz
                    mx = stat[:, u, 0, :].rearrange("n (b r) -> n b r", r=4)
                    V.tensor_reduce(mx, of, X, ALU.max).then_inc(s["maxed"], 1)
                    dve.wait_ge(s["maxed"], m + 1)
                    V.tensor_tensor(zz, of, mx.unsqueeze(3).to_broadcast([N, banks, 4, keys]), ALU.subtract).then_inc(s["shifted"], 1)

                def norm(m, u):
                    dve.wait_ge(s["exped"], m + 1)
                    V.tensor_reduce(stat[:, u, 1, :], z[:, u, :, :], X, ALU.add).then_inc(s["summed"], 1)
                    dve.wait_ge(s["summed"], m + 1)
                    V.reciprocal(stat[:, u, 2, :], stat[:, u, 1, :]).then_inc(s["inverted"], 1)
                    dve.wait_ge(s["inverted"], m + 1)
                    V.tensor_tensor(z[:, u, :, 0:N], z[:, u, :, 0:N], stat[:, u, 2, :].unsqueeze(2).to_broadcast([N, heads, N]), ALU.mult).then_inc(s["probs"], 1)

                def add(m, u):
                    if gate is not None:
                        dve.wait_ge(s["summed_v"], m + 1)
                        V.tensor_tensor(ot[:, u, :, :], psA[u][:, 0:nb * N].rearrange("p (j n) -> p j n", n=N), imgs(gate, m), ALU.mult).then_inc(s["out_saved"], 1)
                    dve.wait_ge(s["projected"], m + 1)
                    mine, made = img(h, m), psA[u][0:D, PROJ:PROJ + N]
                    if bo is not None:
                        V.scalar_tensor_tensor(mine, made, bo, mine, ALU.add, ALU.add).then_inc(s["added"], 1)
                    else:
                        V.tensor_tensor(mine, made, mine, ALU.add).then_inc(s["added"], 1)

                def step(m, u):
                    shift(m, u)
                    rotate(m + 1, 1 - u)
                    norm(m, u)
                    add(m - 1, 1 - u)

                dve.wait_ge(s["pads"], 1)
                rotate(0, 0)
                shift(0, 0)
                rotate(1, 1)
                norm(0, 0)
                with dve.Fori(0, B // 2 - 1) as i:
                    step(i * 2 + 1, 1)
                    step(i * 2 + 2, 0)
                shift(B - 1, 1)
                norm(B - 1, 1)
                add(B - 2, 0)
                add(B - 1, 1)


def linear_attention(nc, tag, x, h, wq, wkv, wo, bo):
    H, dh, two, nb = 8, 64, 2, 4
    with stage(nc, tag, "wsum", "wmean", "wcentered", "x_copied", "q_made", "kv_made", "q_saved", "squared", "sums",
               "eps", "root", "inverted", "kv_saved", "dots", "dots_saved", "out", "out_saved", "projected", "added") as (s, sb, ps):
        wmean = sb("wmean", [D, 2, 2 * H])
        eps_col = sb("eps", [N, 1])
        xb = sb("xb", [D, two, N])
        q = sb("q", [128, two, nb, N])
        sq = sb("sq", [N, two, 2 * H, dh])
        kv = sb("kv", [N, two, 2 * H, dh])
        stat = sb("stat", [N, two, 3, 2 * H])
        dots = sb("dots", [128, two, nb, 128])
        ot = sb("ot", [128, two, nb, N])
        psQ = [ps(f"q{u}", [128, 512]) for u in range(two)]
        psKV = [ps(f"kv{u}", [128, 2, 512]) for u in range(two)]
        psD = [ps(f"d{u}", [128, 512]) for u in range(two)]
        steps = B // two
        img = lambda t, i, u: t[:, bass.ds(i * (two * N) + u * N, N)]
        with nc.Block() as block:
            @block.gpsimd
            def _(pool):
                nc.gpsimd.memset(eps_col[:, :], 1e-5).then_inc(s["eps"], 1)
                nc.gpsimd.memset(dots[:, :, :, :], 0.0).then_inc(s["eps"], 1)
                with pool.Fori(0, steps) as i:
                    for u in range(two):
                        nc.gpsimd.tensor_copy(xb[:, u, :], img(x, i, u)).then_inc(s["x_copied"], 1)
                    pool.wait_ge(s["added"], i * two + two)

            @block.tensor
            def _(pe):
                pe.wait_ge(s["wcentered"], 1)
                with pe.Fori(0, steps) as i:
                    for u in range(two):
                        pe.wait_ge(s["x_copied"], i * two + (u + 1))
                        for part in range(2):
                            mm = nc.tensor.matmul(psKV[u][0:N, part, :], xb[:, u, :], wkv[:, part * H:(part + 1) * H, :], start=True, stop=True)
                        mm.then_inc(s["kv_made"], 1)
                        for j in range(nb):
                            mm = nc.tensor.matmul(psQ[u][:, j * N:(j + 1) * N], wq[:, j, :], xb[:, u, :], start=True, stop=True)
                        mm.then_inc(s["q_made"], 1)
                    for u in range(two):
                        pe.wait_ge(s["kv_saved"], i * two + (u + 1))
                        for hd in range(H):
                            p = dh * (hd % 2)
                            mm = nc.tensor.matmul(psD[u][p:p + dh, (hd // 2) * dh:(hd // 2 + 1) * dh], kv[:, u, hd, :], kv[:, u, H + hd, :], start=True, stop=True)
                        mm.then_inc(s["dots"], 1)
                    for u in range(two):
                        pe.wait_ge(s["q_saved"], i * two + (u + 1))
                        pe.wait_ge(s["dots_saved"], i * (2 * two) + 2 * (u + 1))
                        for j in range(nb):
                            mm = nc.tensor.matmul(psQ[u][:, j * N:(j + 1) * N], dots[:, u, j, :], q[:, u, j, :], start=True, stop=True)
                        mm.then_inc(s["out"], 1)
                    for u in range(two):
                        pe.wait_ge(s["out_saved"], i * two + (u + 1))
                        for j in range(nb):
                            mm = nc.tensor.matmul(psKV[u][0:D, 1, 0:N], wo[:, j, :], ot[:, u, j, :], start=(j == 0), stop=(j == nb - 1))
                        mm.then_inc(s["projected"], 1)
                    pe.wait_ge(s["added"], i * two + two)

            @block.scalar
            def _(act):
                act.wait_ge(s["eps"], 2)
                with act.Fori(0, steps) as i:
                    for u in range(two):
                        act.wait_ge(s["kv_made"], i * two + (u + 1))
                        nc.scalar.activation(sq[:, u, :, :], psKV[u][0:N, :, :].rearrange("n a (h d) -> n (a h) d", d=dh), ACT.Square).then_inc(s["squared"], 1)
                        act.wait_ge(s["q_made"], i * two + (u + 1))
                        nc.scalar.activation(q[:, u, :, :], psQ[u][:, 0:nb * N].rearrange("p (j n) -> p j n", n=N), ACT.Copy).then_inc(s["q_saved"], 1)
                    for u in range(two):
                        act.wait_ge(s["sums"], i * two + (u + 1))
                        nc.scalar.activation(stat[:, u, 1, :], stat[:, u, 0, :], ACT.Sqrt, bias=eps_col[:, 0:1], scale=1.0 / dh).then_inc(s["root"], 1)
                    for u in range(two):
                        act.wait_ge(s["dots"], i * two + (u + 1))
                        for p in (0, dh):
                            nc.scalar.activation(dots[p:p + dh, u, :, p:p + dh], psD[u][p:p + dh, 0:nb * dh].rearrange("p (j d) -> p j d", d=dh), ACT.Copy, scale=1.0 / N).then_inc(s["dots_saved"], 1)
                    for u in range(two):
                        act.wait_ge(s["out"], i * two + (u + 1))
                        nc.scalar.activation(ot[:, u, :, :], psQ[u][:, 0:nb * N].rearrange("p (j n) -> p j n", n=N), ACT.Copy).then_inc(s["out_saved"], 1)
                    act.wait_ge(s["added"], i * two + two)

            @block.vector
            def _(dve):
                nc.vector.tensor_reduce(wmean[:, 0, :], wkv[:, :, :], X, ALU.add).then_inc(s["wsum"], 1)
                dve.wait_ge(s["wsum"], 1)
                nc.vector.tensor_scalar(wmean[:, 1, :], wmean[:, 0, :], 1.0 / dh, None, ALU.mult).then_inc(s["wmean"], 1)
                dve.wait_ge(s["wmean"], 1)
                nc.vector.tensor_tensor(wkv[:, :, :], wkv[:, :, :], wmean[:, 1, :].unsqueeze(2).to_broadcast([D, 2 * H, dh]), ALU.subtract).then_inc(s["wcentered"], 1)
                with dve.Fori(0, steps) as i:
                    for u in range(two):
                        dve.wait_ge(s["squared"], i * two + (u + 1))
                        nc.vector.tensor_reduce(stat[:, u, 0, :], sq[:, u, :, :], X, ALU.add).then_inc(s["sums"], 1)
                    for u in range(two):
                        dve.wait_ge(s["root"], i * two + (u + 1))
                        nc.vector.reciprocal(stat[:, u, 2, :], stat[:, u, 1, :]).then_inc(s["inverted"], 1)
                        dve.wait_ge(s["inverted"], i * two + (u + 1))
                        nc.vector.tensor_tensor(kv[:, u, :, :], psKV[u][0:N, :, :].rearrange("n a (h d) -> n (a h) d", d=dh),
                                                stat[:, u, 2, :].unsqueeze(2).to_broadcast([N, 2 * H, dh]), ALU.mult).then_inc(s["kv_saved"], 1)
                    for u in range(two):
                        dve.wait_ge(s["projected"], i * two + (u + 1))
                        nc.vector.scalar_tensor_tensor(img(h, i, u), psKV[u][0:D, 1, 0:N], bo, img(h, i, u), ALU.add, ALU.add).then_inc(s["added"], 1)


def top2(nc, tag, wT, ident, E, mode, x=None, gw=None, gb=None, scores=None):
    gated = scores is None
    with stage(nc, tag, "logits", "chain", "ones", "tri", "shifted", "exped", "weights", "turned", "saved") as (s, sb, ps):
        g = sb("g", [N, B, E]) if gated else scores
        z = sb("z", [N, B, E])
        gt = sb("gt", [N, B, E, E])
        eq = sb("eq", [N, B, E, E])
        tri = sb("tri", [N, E, E])
        st = sb("st", [N, 2, B])
        rank = sb("rank", [N, B, E])
        logits_ps = ps("logits", [N, B, E])
        wT_ps = ps("wT", [E, NC, 512])
        wide = lambda t: t.unsqueeze(2).to_broadcast([N, B, E])
        every = [N, B, E, E]
        n_exp = 2 if mode == "softmax of gates" else 1
        with nc.Block() as block:
            @block.gpsimd
            def _(pool):
                nc.gpsimd.memset(tri[:, :, :], 1.0).then_inc(s["ones"], 1)
                pool.wait_ge(s["ones"], 1)
                nc.gpsimd.affine_select(out=tri[:, :, :], in_=tri[:, :, :], compare_op=ALU.is_ge, fill=0.0, base=-1,
                                        pattern=[[1, E], [-1, E]], channel_multiplier=0).then_inc(s["tri"], 1)

            @block.tensor
            def _(pe):
                if gated:
                    for b in range(B):
                        mm = nc.tensor.matmul(logits_ps[:, b, :], x[:, b * N:(b + 1) * N], gw, start=True, stop=True)
                    mm.then_inc(s["logits"], 1)
                pe.wait_ge(s["weights"], 1)
                for b in range(B):
                    mm = nc.tensor.transpose(wT_ps[:, b // IPC, (b % IPC) * N:(b % IPC + 1) * N], z[:, b, :], ident[0:N, 0:N])
                mm.then_inc(s["turned"], 1)

            @block.scalar
            def _(act):
                for n in range(n_exp):
                    act.wait_ge(s["shifted"], n + 1)
                    if mode != "share" and n == n_exp - 1:
                        nc.scalar.activation(z[:, :, :], z[:, :, :], ACT.Exp).then_inc(s["exped"], 1)
                    else:
                        nc.scalar.activation(g[:, :, :], g[:, :, :], ACT.Exp).then_inc(s["exped"], 1)
                act.wait_ge(s["turned"], 1)
                nc.scalar.activation(wT[:, :].rearrange("e (c t) -> e c t", c=NC), wT_ps[:, :, 0:CH], ACT.Copy).then_inc(s["saved"], 1)

            @block.vector
            def _(dve):
                links = [0]

                def link(ins):
                    links[0] += 1
                    ins.then_inc(s["chain"], 1)
                    dve.wait_ge(s["chain"], links[0])

                V = nc.vector
                if gated:
                    dve.wait_ge(s["logits"], 1)
                    if gb is not None:
                        link(V.tensor_tensor(g[:, :, :], logits_ps[:, :, :], gb.unsqueeze(1).to_broadcast([N, B, E]), ALU.add))
                    else:
                        link(V.tensor_copy(g[:, :, :], logits_ps[:, :, :]))
                    link(V.tensor_reduce(st[:, 0, :], g[:, :, :], X, ALU.max))
                    V.tensor_tensor(g[:, :, :], g[:, :, :], wide(st[:, 0, :]), ALU.subtract).then_inc(s["shifted"], 1)
                    dve.wait_ge(s["exped"], 1)
                    link(V.tensor_reduce(st[:, 0, :], g[:, :, :], X, ALU.add))
                    link(V.reciprocal(st[:, 1, :], st[:, 0, :]))
                    link(V.tensor_tensor(g[:, :, :], g[:, :, :], wide(st[:, 1, :]), ALU.mult))
                dve.wait_ge(s["tri"], 1)
                mine, other = g[:, :, :].unsqueeze(3).to_broadcast(every), g[:, :, :].unsqueeze(2).to_broadcast(every)
                V.tensor_tensor(gt[:, :, :, :], other, mine, ALU.is_gt)
                link(V.tensor_tensor(eq[:, :, :, :], other, mine, ALU.is_equal))
                link(V.tensor_tensor(eq[:, :, :, :], eq[:, :, :, :], tri[:, :, :].unsqueeze(1).to_broadcast(every), ALU.mult))
                link(V.tensor_tensor(gt[:, :, :, :], gt[:, :, :, :], eq[:, :, :, :], ALU.add))
                link(V.tensor_reduce(rank[:, :, :], gt[:, :, :, :], X, ALU.add))
                if mode == "share":
                    link(V.scalar_tensor_tensor(z[:, :, :], rank[:, :, :], 2.0, g[:, :, :], ALU.is_lt, ALU.mult))
                    link(V.tensor_reduce(st[:, 0, :], z[:, :, :], X, ALU.add))
                    link(V.tensor_scalar(st[:, 0, :], st[:, 0, :], 1e-9, None, ALU.add))
                else:
                    link(V.tensor_reduce(st[:, 0, :], g[:, :, :], X, ALU.max))
                    V.tensor_tensor(z[:, :, :], g[:, :, :], wide(st[:, 0, :]), ALU.subtract).then_inc(s["shifted"], 1)
                    dve.wait_ge(s["exped"], n_exp)
                    link(V.scalar_tensor_tensor(z[:, :, :], rank[:, :, :], 2.0, z[:, :, :], ALU.is_lt, ALU.mult))
                    link(V.tensor_reduce(st[:, 0, :], z[:, :, :], X, ALU.add))
                link(V.reciprocal(st[:, 1, :], st[:, 0, :]))
                V.tensor_tensor(z[:, :, :], z[:, :, :], wide(st[:, 1, :]), ALU.mult).then_inc(s["weights"], 1)


KEY = 2048
LOW = 32
HIGH = T // LOW + 1
LC = 46


def chunk(t, i):
    return t[:, i * CH:(i + 1) * CH]


def relu_experts(nc, tag, x, h, wT, pick, W1, b1, W2, b2, W3, sb3, eb3):
    M = len(W1)
    with stage(nc, tag, "first", "first_saved", "second", "second_saved", "weight", "weighted", "sum", "added") as (s, sb, ps):
        h1 = sb("h1", [128, 2, CH])
        h2 = sb("h2", [128, 2, CH])
        hw = sb("hw", [128, 2, CH])
        p1 = [ps(f"p1{k}", [128, 512]) for k in range(2)]
        p2 = [ps(f"p2{k}", [128, 512]) for k in range(2)]
        pw = [ps(f"pw{k}", [128, 512]) for k in range(2)]
        acc = ps("acc", [D, 512])
        n1 = [w.shape[1] for w in W1]
        n2 = [w.shape[1] for w in W2]
        place = [(i, m) for i in range(NC) for m in range(M)]
        gated = lambda i, m: i * (M - 1) + m
        with nc.Block() as block:
            @block.tensor
            def _(pe):
                def first(n):
                    if n >= len(place):
                        return
                    i, m = place[n]
                    if n >= 2:
                        pe.wait_ge(s["first_saved"], n - 1)
                    nc.tensor.matmul(p1[n % 2][0:n1[m], 0:CH], W1[m], chunk(x, i), start=True, stop=True).then_inc(s["first"], 1)

                def last(n):
                    i, m = place[n]
                    if m == 0:
                        if i:
                            pe.wait_ge(s["added"], i)
                        nc.tensor.matmul(acc[:, 0:CH], eb3, chunk(wT, i), start=True, stop=False)
                        pe.wait_ge(s["second_saved"], n + 1)
                    else:
                        pe.wait_ge(s["weighted"], gated(i, m))
                    src = (hw[0:n2[m], gated(i, m) % 2, :] if m else h2[0:n2[m], n % 2, :])
                    mm = nc.tensor.matmul(acc[:, 0:CH], W3[m], src, start=False, stop=(m == M - 1))
                    if m == M - 1:
                        mm.then_inc(s["sum"], 1)

                first(0)
                for n, (i, m) in enumerate(place):
                    first(n + 1)
                    pe.wait_ge(s["first_saved"], n + 1)
                    if n >= 2:
                        pe.wait_ge(s["second_saved"], n - 1)
                    nc.tensor.matmul(p2[n % 2][0:n2[m], 0:CH], W2[m], h1[0:n1[m], n % 2, :], start=True, stop=True).then_inc(s["second"], 1)
                    if m:
                        if gated(i, m) >= 3:
                            pe.wait_ge(s["weighted"], gated(i, m) - 2)
                        nc.tensor.matmul(pw[gated(i, m) % 2][0:n2[m], 0:CH], pick[0:M - 1, m - 1, 0:n2[m]], chunk(wT, i), start=True, stop=True).then_inc(s["weight"], 1)
                    if n:
                        last(n - 1)
                last(len(place) - 1)

            @block.scalar
            def _(act):
                for n, (i, m) in enumerate(place):
                    act.wait_ge(s["first"], n + 1)
                    if n >= 2:
                        act.wait_ge(s["second"], n - 1)
                    nc.scalar.activation(h1[0:n1[m], n % 2, :], p1[n % 2][0:n1[m], 0:CH], ACT.Relu, bias=b1[m]).then_inc(s["first_saved"], 1)
                    act.wait_ge(s["second"], n + 1)
                    if n >= 2 and place[n - 2][1]:
                        act.wait_ge(s["weighted"], gated(*place[n - 2]))
                    nc.scalar.activation(h2[0:n2[m], n % 2, :], p2[n % 2][0:n2[m], 0:CH], ACT.Relu, bias=b2[m]).then_inc(s["second_saved"], 1)

            @block.vector
            def _(dve):
                for n, (i, m) in enumerate(place):
                    if m:
                        k = gated(i, m)
                        dve.wait_ge(s["second_saved"], n + 1)
                        dve.wait_ge(s["weight"], k)
                        nc.vector.tensor_tensor(hw[0:n2[m], k % 2, :], h2[0:n2[m], n % 2, :], pw[k % 2][0:n2[m], 0:CH], ALU.mult).then_inc(s["weighted"], 1)
                    if m == M - 1:
                        dve.wait_ge(s["sum"], i + 1)
                        nc.vector.scalar_tensor_tensor(chunk(h, i), acc[:, 0:CH], sb3, chunk(h, i), ALU.add, ALU.add).then_inc(s["added"], 1)


PK = 16
NKEY = 64
TT = 104
NT = T // TT
TG = 8
HG = TG // 2


def product_keys(nc, tag, x, wq, keys, table, kv, ident, src_ap, dst_ap, key, hist):
    H, G2, SL = 8, 16, slice(None)
    LINKS = 21
    rounds = TT // TG
    early = 8
    late = rounds - early
    L = key.shape[1]
    LP = (NT - 1) * late * LC
    assert LP >= L
    with stage(nc, tag, "q", "q_saved", "iota_i", "consts", "q_tile", "sim", "sim_saved", "chain", "shifted", "exped", "rows_ready",
               "turned", "index_saved", "spread", "staged", "gathered0", "gathered1", "weighed", "kv_saved", "passed",
               "edges_loaded", "digit_chain", "zero", "hot", "hot_used", "hist", "hist_saved") as (s, sb, ps):
        src = sb("src", [128, L], I32)
        dst = sb("dst", [128, L], I32)
        srcf = sb("srcf", [128, L])
        digits = sb("digits", [128, 2, LP], BF16)
        hot_hi = sb("hot_hi", [128, LC, HIGH], BF16)
        hot_lo = sb("hot_lo", [128, LC, LOW], BF16)
        digit = sb("digit", [128, HIGH], BF16)
        zero = sb("zero", [128, HIGH], BF16)
        qT = sb("qT", [128, 4, T])
        qb = sb("qb", [128, 4, TT])
        sim = sb("sim", [TT, G2, NKEY])
        sim2 = sb("sim2", [TT, G2, NKEY])
        top = sb("top", [TT, G2, PK])
        topi = sb("topi", [TT, G2, PK], U32)
        topf = sb("topf", [TT, G2, PK])
        sums = sb("sums", [TT, H, PK * PK])
        sums2 = sb("sums2", [TT, H, PK * PK])
        best = sb("best", [TT, H, PK])
        besti = sb("besti", [TT, H, PK], U32)
        part_u = sb("part_u", [TT, 2, H * PK], U32)
        part = sb("part", [TT, 2, H, PK])
        half_i = sb("half_i", [TT, 2, H, PK])
        row = sb("row", [TT, H, PK])
        wt = sb("wt", [TT, H, PK])
        st = sb("st", [TT, 2, H])
        head0 = sb("head0", [TT, H, PK])
        count = sb("count", [TT, PK])
        own = sb("own", [128, H])
        idxT = sb("idxT", [128, T + TG], U32)
        spread = sb("spread", [128, T, H])
        idx = [sb(f"idx{a}", [128, HG], U32) for a in range(2)]
        got = [sb(f"got{n}", [128, 128]) for n in range(TG)]
        psQ = ps("s", [128, 4, 512])
        psS = psQ[0:TT, :, :]
        psT = ps("t", [128, 2, 256])
        psH = ps("h", [128, 512])[0:HIGH, 0:LOW]
        psG = [ps(f"g{a}", [128, 512]) for a in range(2)]
        full = [TT, H, PK, PK]
        with nc.Block() as block:
            def gather_at(t, g):
                return t * TT + g * TG

            @block.sync
            def _(sp):
                sp.dma_start(src[:, :], src_ap.rearrange("(p l) -> p l", p=128)).then_inc(s["edges_loaded"], 16)
                sp.dma_start(dst[:, :], dst_ap.rearrange("(p l) -> p l", p=128)).then_inc(s["edges_loaded"], 16)

            @block.gpsimd
            def _(pool):
                P = nc.gpsimd
                P.iota(head0[:, :, :], [[NKEY * NKEY, H], [0, PK]], base=0, channel_multiplier=0, allow_small_or_imprecise_dtypes=True)
                P.iota(count[:, :], [[1, PK]], base=0, channel_multiplier=0, allow_small_or_imprecise_dtypes=True)
                P.iota(digit[:, :], [[1, HIGH]], base=0, channel_multiplier=0, allow_small_or_imprecise_dtypes=True)
                P.memset(zero[:, :], 0.0).then_inc(s["zero"], 1)
                P.memset(own[:, :], 1.0).then_inc(s["iota_i"], 1)
                pool.wait_ge(s["iota_i"], 1)
                P.memset(idxT[:, T:T + TG], 0)
                P.affine_select(out=own[:, :], in_=own[:, :], compare_op=ALU.is_ge, fill=0.0, base=0, pattern=[[-PK, H]], channel_multiplier=1).then_inc(s["iota_i"], 1)
                pool.wait_ge(s["iota_i"], 2)
                P.affine_select(out=own[:, :], in_=own[:, :], compare_op=ALU.is_ge, fill=0.0, base=PK - 1, pattern=[[PK, H]], channel_multiplier=-1).then_inc(s["consts"], 1)
                pool.wait_ge(s["consts"], 1)
                with pool.Fori(0, T // TG) as n:
                    for a in range(2):
                        wait_alone(pool, s["staged"], n * 2 + (a + 1), s["passed"])
                        for k in range(HG):
                            P.indirect_dma_start(out=got[a * HG + k][:, :], out_offset=None, in_=table,
                                                 in_offset=bass.IndirectOffsetOnAxis(ap=idx[a][:, k:k + 1], axis=0)).then_inc(s[f"gathered{a}"], 16)

            @block.tensor
            def _(pe):
                M = nc.tensor.matmul
                for j in range(4):
                    for c in range(NC):
                        if j * NC + c >= 4:
                            pe.wait_ge(s["q_saved"], j * NC + c - 3)
                        M(psQ[:, (j * NC + c) % 4, 0:CH], wq[:, j, :], chunk(x, c), start=True, stop=True).then_inc(s["q"], 1)
                pe.wait_ge(s["q_saved"], 4 * NC)

                def score(t):
                    pe.wait_ge(s["q_tile"], t + 1)
                    for f in range(G2):
                        r, j = f % 4, f // 4
                        mm = M(psS[:, r, j * NKEY:(j + 1) * NKEY], qb[32 * r:32 * r + 32, j, :], keys[32 * r:32 * r + 32, j, :], start=True, stop=True)
                    mm.then_inc(s["sim"], 1)

                def turn(t):
                    pe.wait_ge(s["rows_ready"], t + 1)
                    nc.tensor.transpose(psT[:, 0, 0:TT], row[:, :, :].rearrange("n h k -> n (h k)"), ident[0:TT, 0:TT])
                    nc.tensor.transpose(psT[:, 1, 0:TT], wt[:, :, :].rearrange("n h k -> n (h k)"), ident[0:TT, 0:TT]).then_inc(s["turned"], 1)

                def weigh(t, first, steps, count_edges=False):
                    wait_alone(pe, s["spread"], t + 1, s["passed"])
                    with pe.Fori(0, steps) as k_:
                        g = k_ + first
                        for a in range(2):
                            pe.wait_ge(s[f"gathered{a}"], (t * rounds + g) * (16 * HG) + 16 * HG)
                            for k in range(HG):
                                mm = M(psG[a][:, k * H:(k + 1) * H], got[a * HG + k][:, :],
                                       spread[:, bass.ds(gather_at(t, g) + (a * HG + k), 1), :].rearrange("p o h -> p (o h)"), start=True, stop=True)
                            mm.then_inc(s["weighed"], 1)
                        if count_edges:
                            pe.wait_ge(s["hot"], t * late + k_ + 1)
                            for k in range(LC):
                                mm = M(psH, hot_hi[:, k, :], hot_lo[:, k, :], start=False, stop=False, skip_group_check=True)
                            mm.then_inc(s["hot_used"], 1)
                        pe.wait_ge(s["kv_saved"], (t * rounds + g) * 2 + 2)

                pe.wait_ge(s["zero"], 1)
                M(psH, zero[:, :], zero[:, 0:LOW], start=True, stop=False)
                pe.sem_inc(s["hot_used"], 1)
                score(0)
                turn(0)
                with pe.Fori(0, NT - 1) as t:
                    score(t + 1)
                    weigh(t, 0, early)
                    turn(t + 1)
                    weigh(t, early, late, count_edges=True)
                M(psH, zero[:, :], zero[:, 0:LOW], start=False, stop=True).then_inc(s["hist"], 1)
                weigh(NT - 1, 0, rounds)

            @block.scalar
            def _(act):
                C = lambda out, in_: nc.scalar.activation(out, in_, ACT.Copy)
                for j in range(4):
                    for c in range(NC):
                        n = j * NC + c
                        act.wait_ge(s["q"], n + 1)
                        C(chunk(qT[:, j, :], c), psQ[:, n % 4, 0:CH]).then_inc(s["q_saved"], 1)
                act.wait_ge(s["q_saved"], 4 * NC)

                def score(t):
                    C(qb[:, :, :], qT[:, :, bass.ds(t * TT, TT)]).then_inc(s["q_tile"], 1)
                    act.wait_ge(s["sim"], t + 1)
                    C(sim[:, :, :].rearrange("n (j r) k -> n r j k", r=4), psS[:, :, 0:4 * NKEY].rearrange("n r (j k) -> n r j k", j=4)).then_inc(s["sim_saved"], 1)

                def soften(t):
                    act.wait_ge(s["shifted"], t + 1)
                    nc.scalar.activation(wt[:, :, :], wt[:, :, :], ACT.Exp).then_inc(s["exped"], 1)
                    act.wait_ge(s["turned"], t + 1)
                    C(idxT[:, bass.ds(t * TT, TT)], psT[:, 0, 0:TT]).then_inc(s["index_saved"], 1)

                def stage_index(t, g, a):
                    C(idx[a][:, :], idxT[:, bass.ds(gather_at(t, g) + a * HG, HG)]).then_inc(s["staged"], 1)

                def gathers(t, first, steps, tiles):
                    wait_alone(act, s["index_saved"], tiles, s["passed"])
                    with act.Fori(0, steps) as k_:
                        g = k_ + first
                        for a in range(2):
                            act.wait_ge(s["weighed"], (t * rounds + g) * 2 + (a + 1))
                            stage_index(t, g + 1, a)
                            C(kv[:, :, bass.ds(gather_at(t, g) + a * HG, HG)], psG[a][:, 0:HG * H].rearrange("p (n h) -> p h n", h=H)).then_inc(s["kv_saved"], 1)

                score(0)
                soften(0)
                act.wait_ge(s["index_saved"], 1)
                act.wait_ge(s["consts"], 1)
                for a in range(2):
                    stage_index(0, 0, a)
                with act.Fori(0, NT - 1) as t:
                    score(t + 1)
                    gathers(t, 0, early, t + 1)
                    soften(t + 1)
                    gathers(t, early, rounds - early, t + 2)
                gathers(NT - 1, 0, rounds, NT)

            @block.vector
            def _(dve):
                V = nc.vector
                dve.wait_ge(s["consts"], 1)

                def score(t):
                    links = [0]

                    def link(ins):
                        links[0] += 1
                        ins.then_inc(s["chain"], 1)
                        wait_alone(dve, s["chain"], t * LINKS + links[0], s["passed"])

                    def top16(n, val, ind, src, src2):
                        for f in range(n):
                            last = V.max(val[:, f, 0:8], src[:, f, :])
                        link(last)
                        for f in range(n):
                            V.max_index(ind[:, f, 0:8], val[:, f, 0:8], src[:, f, :])
                        for f in range(n):
                            last = V.match_replace(src2[:, f, :], val[:, f, 0:8], src[:, f, :], NEG)
                        link(last)
                        for f in range(n):
                            last = V.max(val[:, f, 8:16], src2[:, f, :])
                        link(last)
                        for f in range(n):
                            last = V.max_index(ind[:, f, 8:16], val[:, f, 8:16], src2[:, f, :])
                        link(last)

                    wait_alone(dve, s["sim_saved"], t + 1, s["passed"])
                    top16(G2, top, topi, sim, sim2)
                    link(V.tensor_copy(topf[:, :, :], topi[:, :, :]))
                    for hd in range(H):
                        last = V.tensor_tensor(sums[:, hd, :].rearrange("n (a b) -> n a b", a=PK), top[:, hd, :].unsqueeze(2).to_broadcast([TT, PK, PK]),
                                               top[:, H + hd, :].unsqueeze(1).to_broadcast([TT, PK, PK]), ALU.add)
                    link(last)
                    top16(H, best, besti, sums, sums2)
                    flat = besti[:, :, :].rearrange("n h k -> n (h k)")
                    V.tensor_scalar(part_u[:, 0, :], flat, 4, None, ALU.logical_shift_right)
                    link(V.tensor_scalar(part_u[:, 1, :], flat, PK - 1, None, ALU.bitwise_and))
                    link(V.tensor_copy(part[:, :, :, :].rearrange("n a h k -> n a (h k)"), part_u[:, :, :]))
                    for a in range(2):
                        eq = sums[:, :, :].rearrange("n h (k m) -> n h k m", k=PK)
                        link(V.tensor_tensor(eq, part[:, a, :, :].unsqueeze(3).to_broadcast(full), count[:, :].unsqueeze(1).unsqueeze(1).to_broadcast(full), ALU.is_equal))
                        link(V.tensor_tensor(eq, eq, topf[:, a * H:(a + 1) * H, :].unsqueeze(2).to_broadcast(full), ALU.mult))
                        link(V.tensor_reduce(half_i[:, a, :, :], eq, X, ALU.add))
                    if not isinstance(t, int) or t:
                        dve.wait_ge(s["turned"], t)
                    link(V.scalar_tensor_tensor(row[:, :, :], half_i[:, 1, :, :], float(NKEY), half_i[:, 0, :, :], ALU.mult, ALU.add))
                    V.tensor_tensor(row[:, :, :], row[:, :, :], head0[:, :, :], ALU.add)
                    V.tensor_tensor(wt[:, :, :], best[:, :, :], best[:, :, 0:1].to_broadcast([TT, H, PK]), ALU.subtract).then_inc(s["shifted"], 1)
                    dve.wait_ge(s["exped"], t + 1)
                    link(V.tensor_reduce(st[:, 0, :], wt[:, :, :], X, ALU.add))
                    link(V.reciprocal(st[:, 1, :], st[:, 0, :]))
                    V.tensor_tensor(wt[:, :, :], wt[:, :, :], st[:, 1, :].unsqueeze(2).to_broadcast([TT, H, PK]), ALU.mult).then_inc(s["rows_ready"], 1)
                    dve.wait_ge(s["index_saved"], t + 1)
                    V.tensor_tensor(spread[:, bass.ds(t * TT, TT), :], psT[:, 1, 0:TT].unsqueeze(2).to_broadcast([128, TT, H]),
                                    own[:, :].unsqueeze(1).to_broadcast([128, TT, H]), ALU.mult).then_inc(s["spread"], 1)
                    assert links[0] <= LINKS, links
                    while links[0] < LINKS:
                        link(V.tensor_copy(st[:, 0, 0:1], st[:, 1, 0:1]))

                def digits_and_keys():
                    links = [0]

                    def link(ins):
                        links[0] += 1
                        ins.then_inc(s["digit_chain"], 1)
                        dve.wait_ge(s["digit_chain"], links[0])

                    hi, lo = digits[:, 0, 0:L], digits[:, 1, 0:L]
                    V.memset(digits[:, :, L:], 2.0 * LOW)
                    dve.wait_ge(s["edges_loaded"], 32)
                    link(V.tensor_copy(srcf[:, :], src[:, :]))
                    link(V.tensor_copy(key[:, :], dst[:, :]))
                    link(V.tensor_scalar(src[:, :], dst[:, :], 5, None, ALU.logical_shift_right))
                    link(V.tensor_copy(hi, src[:, :]))
                    link(V.tensor_scalar(src[:, :], dst[:, :], LOW - 1, None, ALU.bitwise_and))
                    link(V.tensor_copy(lo, src[:, :]))
                    true = src[:, :].bitcast(F32)
                    link(V.tensor_scalar(true, srcf[:, :], float(T - 1), None, ALU.is_lt))
                    link(V.scalar_tensor_tensor(lo, true, 2.0 * LOW, lo, ALU.mult, ALU.add))
                    link(V.scalar_tensor_tensor(true, key[:, :], float(T), true, ALU.is_lt, ALU.mult))
                    link(V.scalar_tensor_tensor(key[:, :], key[:, :], float(KEY), srcf[:, :], ALU.mult, ALU.add))
                    link(V.scalar_tensor_tensor(key[:, :], key[:, :], 1.0, true, ALU.add, ALU.mult))

                score(0)
                digits_and_keys()
                with dve.Fori(0, NT - 1) as t:
                    score(t + 1)
                    with dve.Fori(0, late) as k:
                        wait_alone(dve, s["hot_used"], t * late + k + 1, s["passed"])
                        cols = lambda d: digits[:, d, bass.ds((t * late + k) * LC, LC)]
                        for d, (to, n) in enumerate(((hot_hi, HIGH), (hot_lo, LOW))):
                            last = V.tensor_tensor(to[:, :, :], cols(d).unsqueeze(2).to_broadcast([128, LC, n]),
                                                   digit[:, 0:n].unsqueeze(1).to_broadcast([128, LC, n]), ALU.is_equal)
                        last.then_inc(s["hot"], 1)
                dve.wait_ge(s["hist"], 1)
                V.tensor_copy(hist[:, :], psH).then_inc(s["hist_saved"], 1)



def gate_values(nc, tag, x, h, wg, bg, gate):
    with stage(nc, tag, "made", "saved", "added") as (s, sb, ps):
        made = [ps(f"g{k}", [128, 512]) for k in range(4)]
        with nc.Block() as block:
            @block.tensor
            def _(pe):
                for n in range(2 * NC):
                    if n >= 4:
                        pe.wait_ge(s["saved"], n - 3)
                    nc.tensor.matmul(made[n % 4][:, 0:CH], wg[:, n // NC, :], chunk(x, n % NC), start=True, stop=True).then_inc(s["made"], 1)

            @block.scalar
            def _(act):
                for n in range(2 * NC):
                    act.wait_ge(s["made"], n + 1)
                    nc.scalar.activation(chunk(gate[:, n // NC, :], n % NC), made[n % 4][:, 0:CH], ACT.Sigmoid, bias=bg[:, n // NC:n // NC + 1]).then_inc(s["saved"], 1)

            @block.vector
            def _(dve):
                nc.vector.tensor_tensor(h[:, :], h[:, :], x[:, :], ALU.add).then_inc(s["added"], 1)


def silu_experts(nc, tag, x, h, rest, wT, pick, w1, w3, w2, experts, hid):
    place = [(i, e) for i in range(NC) for e in range(experts)]
    with stage(nc, tag, "weight", "weighted", "up", "silu", "linear", "product", "sum", "rested", "added") as (s, sb, ps):
        xw = sb("xw", [D, 2, CH])
        act_sb = sb("act", [hid, 2, 2, CH])
        hw = sb("hw", [hid, 2, 2, CH])
        p1 = [ps(f"p1{k}", [hid, 2, 512]) for k in range(2)]
        p3 = ps("p3", [hid, 2, 512])
        pw = ps("pw", [D, 512])
        acc = ps("acc", [D, 512])
        with nc.Block() as block:
            @block.tensor
            def _(pe):
                M = nc.tensor.matmul

                def up(n):
                    i, e = place[n]
                    if n:
                        pe.wait_ge(s["weighted"], n)
                    M(pw[:, 0:CH], pick[0:experts, e, 0:D], chunk(wT, i), start=True, stop=True).then_inc(s["weight"], 1)
                    if n >= 2:
                        pe.wait_ge(s["silu"], n - 1)
                    for k in range(2):
                        mm = M(p1[n % 2][:, k, 0:CH], w1[:, e, k, :], chunk(x, i), start=True, stop=True)
                    mm.then_inc(s["up"], 1)

                def down(n):
                    i, e = place[n]
                    pe.wait_ge(s["product"], n + 1)
                    if e == 0 and i:
                        pe.wait_ge(s["added"], i)
                    for k in range(2):
                        mm = M(acc[:, 0:CH], w2[:, e, k, :], hw[:, n % 2, k, :], start=(e == 0 and k == 0), stop=(e == experts - 1 and k == 1))
                    if e == experts - 1:
                        mm.then_inc(s["sum"], 1)

                up(0)
                for n, (i, e) in enumerate(place):
                    if n + 1 < len(place):
                        up(n + 1)
                    pe.wait_ge(s["weighted"], n + 1)
                    if n:
                        pe.wait_ge(s["product"], n)
                    for k in range(2):
                        mm = M(p3[:, k, 0:CH], w3[:, e, k, :], xw[:, n % 2, :], start=True, stop=True)
                    mm.then_inc(s["linear"], 1)
                    if n:
                        down(n - 1)
                down(len(place) - 1)

            @block.scalar
            def _(act):
                for n in range(len(place)):
                    act.wait_ge(s["up"], n + 1)
                    if n >= 2:
                        act.wait_ge(s["product"], n - 1)
                    nc.scalar.activation(act_sb[:, n % 2, :, :], p1[n % 2][:, :, 0:CH], ACT.Silu).then_inc(s["silu"], 1)

            @block.vector
            def _(dve):
                V = nc.vector
                V.tensor_tensor(h[:, :], h[:, :], rest[:, :], ALU.add).then_inc(s["rested"], 1)

                def weight(n):
                    i, e = place[n]
                    dve.wait_ge(s["weight"], n + 1)
                    if n >= 2:
                        dve.wait_ge(s["linear"], n - 1)
                    V.tensor_tensor(xw[:, n % 2, :], chunk(x, i), pw[:, 0:CH], ALU.mult).then_inc(s["weighted"], 1)

                weight(0)
                for n, (i, e) in enumerate(place):
                    if n + 1 < len(place):
                        weight(n + 1)
                    dve.wait_ge(s["silu"], n + 1)
                    dve.wait_ge(s["linear"], n + 1)
                    if n == 0:
                        dve.wait_ge(s["rested"], 1)
                    V.tensor_tensor(hw[:, n % 2, :, :], act_sb[:, n % 2, :, :], p3[:, :, 0:CH], ALU.mult).then_inc(s["product"], 1)
                    if e == experts - 1:
                        dve.wait_ge(s["sum"], i + 1)
                        V.tensor_tensor(chunk(h, i), chunk(h, i), acc[:, 0:CH], ALU.add).then_inc(s["added"], 1)


def gelu_experts(nc, tag, x, h, wT, pick, w1, b1, w2, b2, experts, hid):
    place = [(i, e) for i in range(NC) for e in range(experts)]
    with stage(nc, tag, "weight", "up", "gelu", "weighted", "sum", "added") as (s, sb, ps):
        act_sb = sb("act", [hid, 2, CH])
        hw = sb("hw", [hid, 2, CH])
        p1 = [ps(f"p1{k}", [hid, 512]) for k in range(2)]
        pw = [ps(f"pw{k}", [hid, 512]) for k in range(2)]
        acc = ps("acc", [D, 512])
        with nc.Block() as block:
            @block.tensor
            def _(pe):
                M = nc.tensor.matmul

                def up(n):
                    i, e = place[n]
                    if n >= 2:
                        pe.wait_ge(s["weighted"], n - 1)
                    M(pw[n % 2][:, 0:CH], pick[0:experts, e, 0:hid], chunk(wT, i), start=True, stop=True).then_inc(s["weight"], 1)
                    M(p1[n % 2][:, 0:CH], w1[:, e, :], chunk(x, i), start=True, stop=True).then_inc(s["up"], 1)

                up(0)
                for n, (i, e) in enumerate(place):
                    if n + 1 < len(place):
                        up(n + 1)
                    if e == 0:
                        if i:
                            pe.wait_ge(s["added"], i)
                        M(acc[:, 0:CH], b2, chunk(wT, i), start=True, stop=False)
                    pe.wait_ge(s["weighted"], n + 1)
                    mm = M(acc[:, 0:CH], w2[:, e, :], hw[:, n % 2, :], start=False, stop=(e == experts - 1))
                    if e == experts - 1:
                        mm.then_inc(s["sum"], 1)

            @block.scalar
            def _(act):
                for n, (i, e) in enumerate(place):
                    act.wait_ge(s["up"], n + 1)
                    if n >= 2:
                        act.wait_ge(s["weighted"], n - 1)
                    nc.scalar.activation(act_sb[:, n % 2, :], p1[n % 2][:, 0:CH], ACT.Gelu, bias=b1[:, e:e + 1]).then_inc(s["gelu"], 1)

            @block.vector
            def _(dve):
                for n, (i, e) in enumerate(place):
                    dve.wait_ge(s["gelu"], n + 1)
                    dve.wait_ge(s["weight"], n + 1)
                    nc.vector.tensor_tensor(hw[:, n % 2, :], act_sb[:, n % 2, :], pw[n % 2][:, 0:CH], ALU.mult).then_inc(s["weighted"], 1)
                    if e == experts - 1:
                        dve.wait_ge(s["sum"], i + 1)
                        nc.vector.tensor_tensor(chunk(h, i), chunk(h, i), acc[:, 0:CH], ALU.add).then_inc(s["added"], 1)


ROUND = 8
ROUNDS = 3


def edge_counts(nc, tag, key, hist, ident, countT, absent):
    L = key.shape[1]
    with stage(nc, tag, "chain", "iota", "zeros", "hist_out", "hist_in", "rchain",
               "round_hot", "counted", "added", "flag", "flag_int", "loops", "turned", "made", "passed") as (s, sb, ps):
        place = sb("place", [128, T])
        hot = sb("hot", [128, 2, ROUND, T], BF16)
        top = sb("top", [128, ROUND])
        top_u = sb("top_u", [128, 3, ROUND], U32)
        top_f = sb("top_f", [128, 2, ROUND])
        flag = sb("flag", [128, 1])
        flag_i = sb("flag_i", [128, 1], I32)
        hist_dram = nc.dram_tensor(f"{tag}_hist_dram", (HIGH * LOW,), F32).ap()
        psC = ps("c", [128, 2, 4, 512])
        V = nc.vector
        with nc.Block() as block:
            @block.sync
            def _(sp):
                sp.dma_start(hist_dram.rearrange("(a b) -> a b", b=LOW), hist[:, :]).then_inc(s["hist_out"], 16)
                sp.wait_ge(s["hist_out"], 16)
                sp.wait_ge(s["zeros"], 1)
                sp.dma_start(countT[TT - 1:TT, NT - 1, :], hist_dram[0:T].rearrange("(a n) -> a n", a=1)).then_inc(s["hist_in"], 16)

            @block.gpsimd
            def _(pool):
                P = nc.gpsimd
                P.iota(place[:, :], [[1, T]], base=0, channel_multiplier=0, allow_small_or_imprecise_dtypes=True).then_inc(s["iota"], 1)
                P.memset(countT[:, :, :], 0.0).then_inc(s["zeros"], 1)
                pool.wait_ge(s["flag"], 1)
                P.partition_all_reduce(flag[:, :], flag[:, :], 128, bass.bass_isa.ReduceOp.max).then_inc(s["flag"], 1)

            @block.tensor
            def _(pe):
                M = nc.tensor.matmul
                def round_(r):
                    pe.wait_ge(s["round_hot"], r + 1)
                    for t in range(NT):
                        if t >= 2:
                            pe.wait_ge(s["added"], r * NT + (t - 1))
                        for c in range(NC):
                            for k in range(ROUND):
                                mm = M(psC[0:TT, t % 2, c, 0:CH], hot[:, 0, k, t * TT:(t + 1) * TT], hot[:, 1, k, c * CH:(c + 1) * CH],
                                       start=(k == 0), stop=(k == ROUND - 1))
                        mm.then_inc(s["counted"], 1)
                    pe.wait_ge(s["added"], r * NT + NT)

                with pe.Fori(0, ROUNDS) as r:
                    round_(r)
                pe.wait_ge(s["flag_int"], 1)
                left = pe.value_load(flag_i[0:1, 0:1], min_val=0, max_val=1)
                with pe.If(left > 0):
                    with pe.Fori(ROUNDS, L // ROUND) as r:
                        round_(r)
                for t in range(NT):
                    pe.wait_ge(s["loops"], NT)
                    if t >= 2:
                        pe.wait_ge(s["made"], t - 1)
                    for o in range(NT):
                        mm = nc.tensor.transpose(psC[0:TT, t % 2, o // 4, (o % 4) * TT:(o % 4 + 1) * TT], countT[:, o, t * TT:(t + 1) * TT], ident[0:TT, 0:TT])
                    mm.then_inc(s["turned"], 1)

            @block.vector
            def _(dve):
                links = [0]

                def link(ins):
                    links[0] += 1
                    ins.then_inc(s["chain"], 1)
                    dve.wait_ge(s["chain"], links[0])

                dve.wait_ge(s["iota"], 1)
                RLINKS = 6

                def rlink(r, n, ins):
                    ins.then_inc(s["rchain"], 1)
                    wait_alone(dve, s["rchain"], r * RLINKS + n, s["passed"])

                def round_(r):
                    rlink(r, 1, V.max(top[:, :], key[:, :]))
                    V.match_replace(key[:, :], top[:, :], key[:, :], 0.0)
                    rlink(r, 2, V.tensor_copy(top_u[:, 0, :], top[:, :]))
                    V.tensor_scalar(top_u[:, 1, :], top_u[:, 0, :], KEY - 1, None, ALU.bitwise_and)
                    rlink(r, 3, V.tensor_scalar(top_u[:, 2, :], top_u[:, 0, :], 11, None, ALU.logical_shift_right))
                    rlink(r, 4, V.tensor_copy(top_f[:, :, :], top_u[:, 1:3, :]))
                    rlink(r, 5, V.tensor_scalar(top_f[:, 0, :], top_f[:, 0, :], -1.0, None, ALU.add))
                    for k in range(ROUND):
                        V.tensor_scalar(hot[:, 0, k, :], place[:, :], top_f[:, 0, k:k + 1], None, ALU.is_equal)
                        last = V.tensor_scalar(hot[:, 1, k, :], place[:, :], top_f[:, 1, k:k + 1], None, ALU.is_equal)
                    last.then_inc(s["round_hot"], 1)
                    for t in range(NT):
                        dve.wait_ge(s["counted"], r * NT + (t + 1))
                        V.tensor_tensor(countT[:, t, :].rearrange("p (c n) -> p c n", c=NC), countT[:, t, :].rearrange("p (c n) -> p c n", c=NC),
                                        psC[0:TT, t % 2, :, 0:CH], ALU.add).then_inc(s["added"], 1)
                    rlink(r, 6, V.tensor_copy(top_u[:, 0, 0:1], top_u[:, 1, 0:1]))

                dve.wait_ge(s["zeros"], 1)
                dve.wait_ge(s["hist_in"], 16)
                with dve.Fori(0, ROUNDS) as r:
                    round_(r)
                link(V.tensor_reduce(flag[:, :], key[:, :], X, ALU.max))
                V.tensor_scalar(flag[:, :], flag[:, :], 1.0, None, ALU.min).then_inc(s["flag"], 1)
                dve.wait_ge(s["flag_int"], 1)
                left = dve.value_load(flag_i[0:1, 0:1], min_val=0, max_val=1)
                with dve.If(left > 0):
                    with dve.Fori(ROUNDS, L // ROUND) as r:
                        round_(r)
                for t in range(NT):
                    V.tensor_tensor(countT[:, t, t * TT:(t + 1) * TT], countT[:, t, t * TT:(t + 1) * TT], ident[0:TT, 0:TT], ALU.add).then_inc(s["loops"], 1)
                for t in range(NT):
                    dve.wait_ge(s["turned"], t + 1)
                    for lo, hi in ((0, 8), (8, NT)):
                        last = V.tensor_scalar(absent[:, t, lo * TT:hi * TT].rearrange("p (c n) -> p c n", n=min(4, hi - lo) * TT),
                                               psC[0:TT, t % 2, lo // 4:(hi + 3) // 4, 0:min(4, hi - lo) * TT], 0.5, NEG, ALU.is_lt, ALU.mult)
                    last.then_inc(s["made"], 1)

            @block.scalar
            def _(act):
                act.wait_ge(s["flag"], 2)
                nc.scalar.activation(flag_i[:, :], flag[:, :], ACT.Copy).then_inc(s["flag_int"], 1)


def graph_scores(nc, tag, x, wgat, att, att_col, rows, ident, pick, countT, absent, scores):
    K, E = 4, 4
    W = 32
    two = 2
    with stage(nc, tag, "zeros", "ones", "sel", "made", "saved", "chain", "spread", "maxed", "parts", "turned", "turned_saved",
               "wide", "wide_saved", "copied", "low", "high", "below", "exped", "edges", "summed", "agg", "agg_saved",
               "back", "root", "eps", "passed") as (s, sb, ps):
        hT = sb("hT", [K * E, T])
        hp = sb("hp", [TT, NT, K, W])
        hb = sb("hb", [TT, two, K, W])
        sel = sb("sel", [K * E, K, TT])
        zero = sb("zero", [TT, CH])
        tmp = sb("tmp", [TT, NT, K, E])
        a = sb("a", [TT, 2, NT, K])
        junk = sb("junk", [TT, two, T])
        M = sb("m", [TT, NT, K])
        U = sb("u", [TT, NT, 2 * K])
        UT = sb("ut", [2 * K, T])
        UB = sb("ub", [TT, 2 * K, T])
        z = sb("z", [TT, K, T])
        aggT = sb("aggt", [128, T])
        g = sb("g", [N, B, K * E])
        sq = sb("sq", [N, B, K * E])
        st = sb("st", [N, 4, B])
        den = sb("den", [N, B, K])
        eps_col = sb("eps", [N, 1])
        psA = ps("banks", [128, 2, NC, 512])
        by_chunk = lambda t: t.rearrange("p (c n) -> p c n", c=NC)
        V = nc.vector
        STEP = two * K
        SLOTS = K

        def tile_of(t, n):
            if isinstance(n, int):
                return t[:, n]
            dims = " ".join("bcd"[:len(t.shape) - 2])
            return t[:, bass.ds(n, 1)].rearrange(f"p a {dims} -> p (a {dims[0]}) {dims[1:]}")

        def sweeps(engine, sweep):
            sweep(0, True, False)
            with engine.Fori(1, NT // two - 1) as i:
                sweep(i, False, False)
            sweep(NT // two - 1, False, True)

        with nc.Block() as block:
            @block.gpsimd
            def _(pool):
                P = nc.gpsimd
                P.memset(sel[:, :, :], 1.0).then_inc(s["ones"], 1)
                P.memset(zero[:, :], 0.0).then_inc(s["zeros"], 1)
                P.memset(eps_col[:, :], 1e-5).then_inc(s["eps"], 1)
                P.memset(hp[:, :, :, :], 0.0).then_inc(s["ones"], 1)
                pool.wait_ge(s["ones"], 1)
                P.affine_select(out=sel[:, :, :], in_=sel[:, :, :], compare_op=ALU.is_ge, fill=0.0, base=0,
                                pattern=[[-E, K], [0, TT]], channel_multiplier=1).then_inc(s["ones"], 1)
                pool.wait_ge(s["ones"], 3)
                P.affine_select(out=sel[:, :, :], in_=sel[:, :, :], compare_op=ALU.is_ge, fill=0.0, base=E - 1,
                                pattern=[[E, K], [0, TT]], channel_multiplier=-1).then_inc(s["ones"], 1)
                P.memset(hp[:, :, :, E:E + 1], 1.0).then_inc(s["ones"], 1)
                pool.wait_ge(s["ones"], 5)
                P.tensor_scalar(sel[:, :, :], sel[:, :, :], att_col, None, ALU.mult).then_inc(s["sel"], 1)
                pool.wait_ge(s["parts"], 1)

                def take(t, u):
                    P.tensor_copy(hb[:, u, :, :], tile_of(hp, t)).then_inc(s["copied"], 1)

                def sweep(i, first, last):
                    for n in range(STEP):
                        wait_alone(pool, s["high"], i * STEP + n + 1, s["passed"])
                        P.tensor_scalar(z[:, n % K, :], z[:, n % K, :], 0.0, None, ALU.min).then_inc(s["below"], 1)
                        if n == 0 and not first:
                            wait_alone(pool, s["summed"], i * STEP + SLOTS, s["passed"])
                            take(i * two + 1, 1)
                        if n == K and not last:
                            wait_alone(pool, s["summed"], i * STEP + K + SLOTS, s["passed"])
                            take(i * two + 2, 0)

                take(0, 0)
                take(1, 1)
                sweeps(pool, sweep)

            @block.tensor
            def _(pe):
                MM = nc.tensor.matmul
                for c in range(NC):
                    mm = MM(psA[0:K * E, 0, c, 0:CH], wgat, chunk(x, c), start=True, stop=True)
                mm.then_inc(s["made"], 1)
                for t in range(NT):
                    mm = MM(psA[0:TT, 1, 0, t * K * E:(t + 1) * K * E], x[:, t * TT:(t + 1) * TT], wgat, start=True, stop=True)
                mm.then_inc(s["made"], 1)
                pe.wait_ge(s["saved"], 2)
                pe.wait_ge(s["sel"], 1)
                for k in range(K):
                    if k >= 2:
                        pe.wait_ge(s["maxed"], (k - 1) * NT)
                    for c in range(NC):
                        mm = MM(psA[0:TT, k % 2, c, 0:CH], sel[:, k, :], chunk(hT, c), start=True, stop=True)
                    mm.then_inc(s["spread"], 1)
                pe.wait_ge(s["parts"], 1)
                for t in range(NT):
                    mm = nc.tensor.transpose(psA[0:2 * K, 0, t // 4, (t % 4) * TT:(t % 4 + 1) * TT], U[:, t, :], ident[0:TT, 0:TT])
                mm.then_inc(s["turned"], 1)
                pe.wait_ge(s["turned_saved"], 2)
                for j in range(2 * K):
                    if j >= 2:
                        pe.wait_ge(s["wide_saved"], j - 1)
                    for c in range(NC):
                        mm = MM(psA[0:TT, j % 2, c, 0:CH], pick[0:2 * K, j, 0:TT], chunk(UT, c), start=True, stop=True)
                    mm.then_inc(s["wide"], 1)
                pe.wait_ge(s["wide_saved"], 2 * K)
                for c in range(NC):
                    MM(psA[:, 0, c, 0:CH], zero[:, 0:128], zero[:, :], start=True, stop=False)
                pe.sem_inc(s["summed"], SLOTS)

                def sweep(i, first, last):
                    for n in range(STEP):
                        u, k = divmod(n, K)
                        pe.wait_ge(s["edges"], i * STEP + (n + 1))
                        for c in range(NC):
                            mm = MM(psA[k * W:(k + 1) * W, 0, c, 0:CH], hb[:, u, k, :], z[:, k, c * CH:(c + 1) * CH],
                                    start=False, stop=False, skip_group_check=True, tile_position=(0, k * W))
                        mm.then_inc(s["summed"], 1)

                sweeps(pe, sweep)
                for c in range(NC):
                    mm = MM(psA[:, 0, c, 0:CH], zero[:, 0:128], zero[:, :], start=False, stop=True)
                mm.then_inc(s["agg"], 1)
                pe.wait_ge(s["agg_saved"], 1)
                for b in range(B):
                    mm = nc.tensor.transpose(psA[0:N, 1, b // IPC, (b % IPC) * 128:(b % IPC + 1) * 128], aggT[:, b * N:(b + 1) * N], ident[:, :])
                mm.then_inc(s["back"], 1)

            @block.scalar
            def _(act):
                act.wait_ge(s["made"], 1)
                nc.scalar.copy(by_chunk(hT[:, :]), psA[0:K * E, 0, :, 0:CH]).then_inc(s["saved"], 1)
                act.wait_ge(s["turned"], 1)
                nc.scalar.copy(UT[:, 0:8 * TT].rearrange("p (c n) -> p c n", c=2), psA[0:2 * K, 0, 0:2, 0:4 * TT]).then_inc(s["turned_saved"], 1)
                nc.scalar.copy(UT[:, 8 * TT:T], psA[0:2 * K, 0, 2, 0:2 * TT]).then_inc(s["turned_saved"], 1)
                for j in range(2 * K):
                    act.wait_ge(s["wide"], j + 1)
                    nc.scalar.copy(by_chunk(UB[:, j, :]), psA[0:TT, j % 2, :, 0:CH]).then_inc(s["wide_saved"], 1)
                act.wait_ge(s["wide_saved"], 2 * K)

                def lower(i, n):
                    u, k = n // K % two, n % K
                    if k == 0:
                        act.wait_ge(s["copied"], i * two + (n // K + 1))
                    act.wait_ge(s["summed"], i * STEP + (n + 1))
                    nc.scalar.activation(z[:, k, :], UB[:, K + k, :], ACT.Identity, bias=hb[:, u, k, E + 2:E + 3]).then_inc(s["low"], 1)

                def sweep(i, first, last):
                    for n in range(STEP):
                        act.wait_ge(s["below"], i * STEP + (n + 1))
                        nc.scalar.activation(z[:, n % K, :], z[:, n % K, :], ACT.Exp).then_inc(s["exped"], 1)
                        if not last or n + 3 < STEP:
                            lower(i, n + 3)

                for n in range(3):
                    lower(0, n)
                sweeps(act, sweep)
                act.wait_ge(s["agg"], 1)
                nc.scalar.copy(by_chunk(aggT[:, :]), psA[:, 0, :, 0:CH]).then_inc(s["agg_saved"], 1)
                act.wait_ge(s["eps"], 1)
                act.wait_ge(s["back"], 2)
                nc.scalar.activation(st[:, 2, :], st[:, 1, :], ACT.Sqrt, bias=eps_col[:, 0:1], scale=1.0 / (K * E)).then_inc(s["root"], 1)

            @block.vector
            def _(dve):
                links = [0]

                def link(ins):
                    links[0] += 1
                    ins.then_inc(s["chain"], 1)
                    dve.wait_ge(s["chain"], links[0])

                heads_of = lambda t: t.rearrange("p t (k e) -> p t k e", k=K)
                dve.wait_ge(s["ones"], 5)
                dve.wait_ge(s["made"], 2)
                made = psA[0:TT, 1, 0, 0:NT * K * E].rearrange("p (t k e) -> p t k e", k=K, e=E)
                link(V.tensor_copy(hp[:, :, :, 0:E], made))
                for side in range(2):
                    row = att[:, side, :].rearrange("p (k e) -> p k e", k=K).unsqueeze(1).to_broadcast([TT, NT, K, E])
                    link(V.tensor_tensor(tmp[:, :, :, :], hp[:, :, :, 0:E], row, ALU.mult))
                    link(V.tensor_reduce(a[:, side, :, :], tmp[:, :, :, :], X, ALU.add))
                V.tensor_scalar(hp[:, :, :, E + 1], a[:, 0, :, :], 1.0, None, ALU.mult)
                V.tensor_scalar(hp[:, :, :, E + 2], a[:, 0, :, :], 0.2, None, ALU.mult).then_inc(s["saved"], 1)
                for k in range(K):
                    dve.wait_ge(s["spread"], k + 1)
                    for t in range(NT):
                        n = k * NT + t
                        if n >= two:
                            dve.wait_ge(s["maxed"], n - 1)
                        V.tensor_tensor_reduce(out=by_chunk(junk[:, n % two, :]), in0=by_chunk(absent[:, t, :]), in1=psA[0:TT, k % 2, :, 0:CH],
                                               scale=1.0, scalar=-3.0e38, op0=ALU.add, op1=ALU.max, accum_out=M[:, t, k:k + 1]).then_inc(s["maxed"], 1)
                dve.wait_ge(s["maxed"], K * NT)
                ad = a[:, 1, :, :]
                link(V.tensor_tensor(M[:, :, :], M[:, :, :], ad, ALU.add))
                link(V.scalar_tensor_tensor(M[:, :, :], M[:, :, :], 0.2, M[:, :, :], ALU.mult, ALU.max))
                V.tensor_tensor(U[:, :, 0:K], ad, M[:, :, :], ALU.subtract)
                V.scalar_tensor_tensor(U[:, :, K:2 * K], ad, 0.2, M[:, :, :], ALU.mult, ALU.subtract).then_inc(s["parts"], 1)
                dve.wait_ge(s["wide_saved"], 2 * K)

                def top(i, n):
                    u, k = n // K % two, n % K
                    if k == 0:
                        dve.wait_ge(s["copied"], i * two + (n // K + 1))
                    dve.wait_ge(s["low"], i * STEP + (n + 1))
                    V.scalar_tensor_tensor(z[:, k, :], UB[:, k, :], hb[:, u, k, E + 1:E + 2], z[:, k, :], ALU.add, ALU.max).then_inc(s["high"], 1)

                def sweep(i, first, last):
                    for n in range(STEP):
                        u, k = divmod(n, K)
                        dve.wait_ge(s["exped"], i * STEP + (n + 1))
                        V.tensor_tensor(z[:, k, :], z[:, k, :], tile_of(countT, i * two + u), ALU.mult).then_inc(s["edges"], 1)
                        if not last or n + 2 < STEP:
                            top(i, n + 2)

                for n in range(2):
                    top(0, n)
                sweeps(dve, sweep)
                dve.wait_ge(s["back"], 1)
                agg = psA[0:N, 1, :, :].rearrange("n c (i k w) -> n (c i) k w", k=K, w=W)
                g4 = heads_of(g[:, :, :])
                wide = lambda t: t.unsqueeze(2).to_broadcast([N, B, K * E])
                all_of = lambda r: rows[:, r:r + 1, :].to_broadcast([N, B, K * E])
                link(V.tensor_scalar(den[:, :, :], agg[:, :, :, E], 1e-16, None, ALU.add))
                link(V.reciprocal(den[:, :, :], den[:, :, :]))
                link(V.tensor_tensor(g4, agg[:, :, :, 0:E], den[:, :, :].unsqueeze(3).to_broadcast([N, B, K, E]), ALU.mult))
                link(V.tensor_tensor(g[:, :, :], g[:, :, :], all_of(0), ALU.add))
                link(V.tensor_reduce(st[:, 0, :], g[:, :, :], X, ALU.add))
                link(V.tensor_scalar(st[:, 0, :], st[:, 0, :], 1.0 / (K * E), None, ALU.mult))
                link(V.tensor_tensor(g[:, :, :], g[:, :, :], wide(st[:, 0, :]), ALU.subtract))
                link(V.tensor_tensor(sq[:, :, :], g[:, :, :], g[:, :, :], ALU.mult))
                V.tensor_reduce(st[:, 1, :], sq[:, :, :], X, ALU.add).then_inc(s["back"], 1)
                dve.wait_ge(s["root"], 1)
                link(V.reciprocal(st[:, 3, :], st[:, 2, :]))
                link(V.tensor_tensor(g[:, :, :], g[:, :, :], wide(st[:, 3, :]), ALU.mult))
                link(V.tensor_tensor(g[:, :, :], g[:, :, :], all_of(1), ALU.mult))
                link(V.tensor_tensor(g[:, :, :], g[:, :, :], all_of(2), ALU.add))
                link(V.tensor_reduce(scores[:, :, :], g4.rearrange("n b k e -> n b e k"), X, ALU.add))
                V.tensor_scalar(scores[:, :, :], scores[:, :, :], 1.0 / K, None, ALU.mult)


def pool_tokens(nc, tag, x_dram, h, wq, wk, wv, wo, cols, cls, ident):
    H, L, G, R, PAIRS = 8, 64, 64, 4, B // 2
    IH = 2 * H
    with stage(nc, tag, "loaded_even", "loaded_odd", "ones", "masks", "summed", "sums", "regrouped", "meaned", "q_made", "q_saved", "spread", "qk_made", "qk_saved",
               "qb_made", "qb_saved", "scores", "scored", "maxed", "shifted", "exped", "totals", "inverted", "probs",
               "x_turned", "x_saved", "p_turned", "p_saved", "ctx", "ctx_saved", "v_made", "v_saved", "o_made", "out", "passed") as (s, sb, ps):
        x = sb("x", [128, 2, 4096])
        xr = sb("xr", [128, 2, G, L])
        xT = sb("xt", [128, 2, 8, R, 128])
        q = sb("q", [128, PAIRS, G])
        qp = sb("qp", [128, 2, G])
        qb = sb("qb", [128, 2, 16])
        mask = sb("mask", [128, 32])
        bmask = sb("bmask", [128, 32])
        qm = sb("qm", [128, G, IH])
        A = sb("a", [128, 2, G, 32])
        z = sb("z", [128, 16, L])
        stat = sb("stat", [128, 3, 16])
        pT = sb("pt", [128, 8, R, 2, IH])
        ctx = sb("ctx", [128, PAIRS, H, G])
        v = sb("v", [128, PAIRS * G])
        psC = ps("c", [128, 2, 512])
        psA = ps("ka", [128, 2, 512])
        psS = ps("s", [128, 2, 512])
        psT = [ps(f"t{p}", [128, 512]) for p in range(2)]
        V = nc.vector

        def pipeline(engine, front, mid, back):
            front(0, 0)
            with engine.Fori(0, PAIRS // 2 - 1) as i:
                for u in range(2):
                    mid(i * 2 + u, u)
                    front(i * 2 + (u + 1), 1 - u)
                    back(i * 2 + u, u)
            n = PAIRS - 2
            mid(n, 0)
            front(n + 1, 1)
            back(n, 0)
            mid(n + 1, 1)
            back(n + 1, 1)

        with nc.Block() as block:
            @block.sync
            def _(sp):
                for n in range(PAIRS):
                    if n >= 2:
                        sp.wait_ge(s["regrouped"], (n - 1) * 8)
                    sp.dma_start(x[:, n % 2, :], x_dram[2 * n:2 * n + 2].rearrange("i d w h -> (i d) (w h)")).then_inc(s["loaded_odd" if n % 2 else "loaded_even"], 16)

            @block.gpsimd
            def _(pool):
                P = nc.gpsimd
                P.memset(mask[:, :], 1.0).then_inc(s["ones"], 1)
                P.memset(A[:, :, :, :], 0.0)
                P.memset(pT[:, :, :, :, :], 0.0).then_inc(s["ones"], 1)
                pool.wait_ge(s["ones"], 1)
                P.affine_select(out=mask[:, :], in_=mask[:, :], compare_op=ALU.is_ge, fill=0.0, base=0,
                                pattern=[[-8, 32]], channel_multiplier=1).then_inc(s["ones"], 1)
                pool.wait_ge(s["ones"], 3)
                P.affine_select(out=mask[:, :], in_=mask[:, :], compare_op=ALU.is_ge, fill=0.0, base=7,
                                pattern=[[8, 32]], channel_multiplier=-1).then_inc(s["ones"], 1)
                pool.wait_ge(s["ones"], 4)
                P.tensor_scalar(bmask[:, :], mask[:, :], cols[:, 1:2], None, ALU.mult).then_inc(s["masks"], 1)

                def regroup(i, u):
                    wait_alone(pool, s["loaded_odd" if u else "loaded_even"], i * 16 + 16, s["passed"])
                    for w in range(8):
                        P.tensor_copy(xr[:, u, w * 8:(w + 1) * 8, :].rearrange("p h (a b) -> p h a b", b=8),
                                      x[:, u, w * 512:(w + 1) * 512].rearrange("p (a h b) -> p h a b", a=8, h=8)).then_inc(s["regrouped"], 1)

                regroup(0, 0)
                regroup(0, 1)
                with pool.Fori(1, PAIRS // 2) as i:
                    for u in range(2):
                        wait_alone(pool, s["scores"], i * 2 + (u - 1), s["passed"])
                        regroup(i, u)

            @block.tensor
            def _(pe):
                M = nc.tensor.matmul

                def front(n, u):
                    pe.wait_ge(s["meaned"], n + 1)
                    M(psC[:, 0, 0:G], wq, q_at(n), start=True, stop=True).then_inc(s["q_made"], 1)
                    for w in range(8):
                        pe.wait_ge(s["regrouped"], n * 8 + (w + 1))
                        if isinstance(n, int):
                            if n * 8 + w >= 2:
                                pe.wait_ge(s["x_saved"], n * 8 + w - 1)
                        else:
                            pe.wait_ge(s["x_saved"], n * 8 + w - 1)
                        for r in range(R):
                            g = w * 8 + 2 * r
                            mm = nc.tensor.transpose(psT[w % 2][:, r * 128:(r + 1) * 128], xr[:, u, g:g + 2, :], ident[:, :])
                        mm.then_inc(s["x_turned"], 1)
                    pe.wait_ge(s["q_saved"], n + 1)
                    for r in range(R):
                        mm = M(psC[r * 32:(r + 1) * 32, 0, G:G + 16], bmask[:, :], qp[:, u, :].rearrange("d (w r p) -> d r w p", r=R, p=2)[:, r, :, :],
                               start=True, stop=True, tile_position=(0, r * 32))
                    mm.then_inc(s["qb_made"], 1)
                    pe.wait_ge(s["spread"], n + 1)
                    for c in range(2):
                        mm = M(psA[:, c, :], wk, qm[:, c * 32:(c + 1) * 32, :], start=True, stop=True)
                    mm.then_inc(s["qk_made"], 1)

                def mid(n, u):
                    pe.wait_ge(s["qk_saved"], n + 1)
                    for g in range(G):
                        r, j = g % 8 // 2, g // 8 * 2 + g % 2
                        mm = M(psS[r * 32:(r + 1) * 32, j // 8, (j % 8) * L:(j % 8 + 1) * L], A[:, u, g, :], xr[:, u, g, :],
                               start=True, stop=True, tile_position=(0, r * 32))
                    mm.then_inc(s["scores"], 1)

                def back(n, u):
                    pe.wait_ge(s["probs"], n + 1)
                    pe.wait_ge(s["qk_saved"], later(n))
                    for w in range(8):
                        mm = nc.tensor.transpose(psA[:, w // 4, (w % 4) * 128:(w % 4 + 1) * 128], z[:, 2 * w:2 * w + 2, :], ident[:, :])
                    mm.then_inc(s["p_turned"], 1)
                    pe.wait_ge(s["p_saved"], n + 1)
                    pe.wait_ge(s["qb_saved"], later(n))
                    for w in range(8):
                        for r in range(R):
                            at = (w % 4 * R + r) * 2 * IH
                            mm = M(psC[:, w // 4, at:at + 2 * IH], xT[:, u, w, r, :], pT[:, w, r, :, :], start=True, stop=True)
                    mm.then_inc(s["ctx"], 1)
                    pe.wait_ge(s["ctx_saved"], n + 1)

                later = lambda n: n + 2 if not isinstance(n, int) else min(n + 2, PAIRS)
                q_at = lambda n: q[:, n, :] if isinstance(n, int) else q[:, bass.ds(n, 1), :].rearrange("p a g -> p (a g)")
                pe.wait_ge(s["masks"], 1)
                pipeline(pe, front, mid, back)
                for hd in range(H):
                    mm = M(psT[0][:, :].rearrange("p (n g) -> p n g", g=G), wv[:, hd, :], ctx[:, :, hd, :], start=(hd == 0), stop=(hd == H - 1))
                mm.then_inc(s["v_made"], 1)
                pe.wait_ge(s["v_saved"], 1)
                for i in range(2):
                    M(psC[0:D, i, :], wo[:, i * D:(i + 1) * D], v[:, :], start=True, stop=False)
                    M(psC[0:D, i, :], ident[:, i * D:(i + 1) * D], q[:, :, :], start=False, stop=True).then_inc(s["o_made"], 1)

            @block.scalar
            def _(act):
                def x_save(n, u, ws):
                    for w in ws:
                        act.wait_ge(s["x_turned"], n * 8 + (w + 1))
                        nc.scalar.copy(xT[:, u, w, :, :], psT[w % 2][:, :].rearrange("p (r d) -> p r d", r=R)).then_inc(s["x_saved"], 1)

                def front(n, u):
                    x_save(n, u, range(8) if isinstance(n, int) and n == 0 else range(4, 8))
                    act.wait_ge(s["qk_made"], n + 1)
                    nc.scalar.copy(A[:, u, :, 0:IH], psA[:, :, :].rearrange("p c (g h) -> p (c g) h", h=IH)).then_inc(s["qk_saved"], 1)

                def mid(n, u):
                    if not (isinstance(n, int) and n == PAIRS - 1):
                        x_save(n + 1, 1 - u, range(4))
                    act.wait_ge(s["shifted"], n + 1)
                    nc.scalar.activation(z[:, :, :], z[:, :, :], ACT.Exp, scale=8.0 ** -0.5).then_inc(s["exped"], 1)

                def back(n, u):
                    act.wait_ge(s["p_turned"], n + 1)
                    for p in range(2):
                        half = slice(p * L, (p + 1) * L)
                        last = nc.scalar.copy(pT[half, :, :, p, :], psA[half, :, :].rearrange("l c (w r k) -> l (c w) r k", r=R, k=32)[:, :, :, 0:IH])
                    last.then_inc(s["p_saved"], 1)

                act.wait_ge(s["ones"], 2)
                pipeline(act, front, mid, back)
                act.wait_ge(s["v_made"], 1)
                nc.scalar.activation(v[:, :], psT[0][:, :], ACT.Identity, bias=cols[:, 2:3]).then_inc(s["v_saved"], 1)

            @block.vector
            def _(dve):
                def mean(n, u):
                    dve.wait_ge(s["regrouped"], n * 8 + 8)
                    V.tensor_reduce(q_of(n), xr[:, u, :, :], X, ALU.add).then_inc(s["sums"], 1)
                    dve.wait_ge(s["sums"], n + 1)
                    V.tensor_scalar(q_of(n), q_of(n), 1.0 / L, None, ALU.mult).then_inc(s["meaned"], 1)

                def front(n, u):
                    if isinstance(n, int) and n == 0:
                        mean(n, u)
                    dve.wait_ge(s["q_made"], n + 1)
                    V.tensor_scalar(qp[:, u, :], psC[:, 0, 0:G], cols[:, 0:1], None, ALU.add).then_inc(s["q_saved"], 1)
                    dve.wait_ge(s["q_saved"], n + 1)
                    V.tensor_tensor(qm[:, :, :], qp[:, u, :].unsqueeze(2).to_broadcast([128, G, IH]),
                                    mask[:, 0:IH].unsqueeze(1).to_broadcast([128, G, IH]), ALU.mult).then_inc(s["spread"], 1)
                    dve.wait_ge(s["qb_made"], n + 1)
                    V.tensor_copy(qb[:, u, :], psC[:, 0, G:G + 16]).then_inc(s["qb_saved"], 1)

                wide = lambda t: t.unsqueeze(2).to_broadcast([128, 16, L])

                def mid(n, u):
                    if not (isinstance(n, int) and n == PAIRS - 1):
                        mean(n + 1, 1 - u)
                    dve.wait_ge(s["qb_saved"], n + 1)
                    dve.wait_ge(s["scores"], n + 1)
                    if not (isinstance(n, int) and n == 0):
                        dve.wait_ge(s["p_turned"], n)
                    V.tensor_tensor(z[:, :, :], psS[:, :, :].rearrange("p c (j l) -> p (c j) l", l=L), wide(qb[:, u, :]), ALU.add).then_inc(s["scored"], 1)
                    dve.wait_ge(s["scored"], n + 1)
                    V.tensor_reduce(stat[:, 0, :], z[:, :, :], X, ALU.max).then_inc(s["maxed"], 1)
                    dve.wait_ge(s["maxed"], n + 1)
                    V.tensor_tensor(z[:, :, :], z[:, :, :], wide(stat[:, 0, :]), ALU.subtract).then_inc(s["shifted"], 1)

                def back(n, u):
                    dve.wait_ge(s["exped"], n + 1)
                    V.tensor_reduce(stat[:, 1, :], z[:, :, :], X, ALU.add).then_inc(s["totals"], 1)
                    dve.wait_ge(s["totals"], n + 1)
                    V.reciprocal(stat[:, 2, :], stat[:, 1, :]).then_inc(s["inverted"], 1)
                    dve.wait_ge(s["inverted"], n + 1)
                    V.tensor_tensor(z[:, :, :], z[:, :, :], wide(stat[:, 2, :]), ALU.mult).then_inc(s["probs"], 1)
                    dve.wait_ge(s["ctx"], n + 1)
                    for i in range(2):
                        made = psC[i * 64:(i + 1) * 64, :, :].rearrange("d c (g i h) -> d i h (c g)", i=2, h=H)[:, i, :, :]
                        last = V.tensor_copy(ctx_of(n, i), made)
                    last.then_inc(s["ctx_saved"], 1)

                q_of = lambda n: q[:, n, :] if isinstance(n, int) else q[:, bass.ds(n, 1), :].rearrange("p a g -> p (a g)")
                ctx_of = lambda n, i: (ctx[i * 64:(i + 1) * 64, n, :, :] if isinstance(n, int) else
                                       ctx[i * 64:(i + 1) * 64, bass.ds(n, 1), :, :].rearrange("p a h g -> p (a h) g"))
                dve.wait_ge(s["masks"], 1)
                pipeline(dve, front, mid, back)
                V.tensor_copy(h[:, :].rearrange("d (b n) -> d b n", n=N)[:, :, 0], cls.to_broadcast([D, B])).then_inc(s["out"], 1)
                for i in range(2):
                    dve.wait_ge(s["o_made"], i + 1)
                    V.tensor_scalar(h[:, :].rearrange("d (m i n) -> d i m n", i=2, n=N)[:, i, :, 1:N], psC[0:D, i, :].rearrange("d (m g) -> d m g", g=G),
                                    cols[0:D, 3:4], None, ALU.add).then_inc(s["out"], 1)


def constants(nc, ones, ident, pick, causal, alibi):
    EXPERTS = pick.shape[0]
    with stage(nc, "const", "filled", "cut", "chain") as (s, sb, ps):
        with nc.Block() as block:
            @block.vector
            def _(dve):
                for a in range(2):
                    rows = slice(a * D, (a + 1) * D)
                    nc.vector.memset(ones[rows, a * D:(a + 1) * D], 1.0 / D)
                    nc.vector.memset(ones[rows, (1 - a) * D:(2 - a) * D], 0.0)

            @block.gpsimd
            def _(pool):
                P = nc.gpsimd
                P.memset(ident[:, :], 0.0).then_inc(s["filled"], 1)
                P.memset(pick[:, :, :], 0.0).then_inc(s["filled"], 1)
                P.memset(causal[:, :], 0.0).then_inc(s["filled"], 1)
                P.iota(alibi[:, :, :], [[0, 8], [1, N]], base=0, channel_multiplier=-1, allow_small_or_imprecise_dtypes=True).then_inc(s["filled"], 1)
                pool.wait_ge(s["filled"], 4)
                P.affine_select(out=ident[:, :], in_=ident[:, :], compare_op=ALU.not_equal, fill=1.0, base=0,
                                pattern=[[-1, 128]], channel_multiplier=1).then_inc(s["cut"], 1)
                P.affine_select(out=pick[:, :, :], in_=pick[:, :, :], compare_op=ALU.not_equal, fill=1.0, base=0,
                                pattern=[[-1, EXPERTS], [0, 128]], channel_multiplier=1).then_inc(s["cut"], 1)
                P.affine_select(out=causal[:, :], in_=causal[:, :], compare_op=ALU.is_ge, fill=NEG, base=0,
                                pattern=[[-1, N]], channel_multiplier=1).then_inc(s["cut"], 1)
                for head in range(8):
                    P.tensor_scalar(alibi[:, head, :], alibi[:, head, :], 0.5 ** (head + 1) * 32.0 ** 0.5, None, ALU.mult).then_inc(s["chain"], 1)
                pool.wait_ge(s["chain"], 8)
                P.affine_select(out=alibi[:, :, :], in_=alibi[:, :, :], compare_op=ALU.is_ge, fill=NEG, base=0,
                                pattern=[[0, 8], [-1, N]], channel_multiplier=1).then_inc(s["cut"], 1)
                pool.wait_ge(s["cut"], 4)


def window_bias(nc, window, toeplitz, last):
    WS = toeplitz.shape[0]
    with stage(nc, "window", "filled", "loaded", "scaled") as (s, sb, ps):
        with nc.Block() as block:
            @block.gpsimd
            def _(pool):
                nc.gpsimd.memset(window[:, :], NEG).then_inc(s["filled"], 1)
                pool.wait_ge(s["loaded"], 32)
                nc.gpsimd.tensor_scalar(window[:, :], window[:, :], 8.0 ** 0.5, None, ALU.mult).then_inc(s["scaled"], 1)

            @block.sync
            def _(sp):
                sp.wait_ge(s["filled"], 1)
                sp.dma_start(window[0:WS, 0:WS], toeplitz).then_inc(s["loaded"], 16)
                sp.dma_start(window[WS:N, WS:2 * WS], last).then_inc(s["loaded"], 16)


def load(nc, tag, pairs):
    with stage(nc, tag, "loaded") as (s, sb, ps):
        with nc.Block() as block:
            @block.sync
            def _(sp):
                for to, source in pairs[0::2]:
                    sp.dma_start(to, source).then_inc(s["loaded"], 16)
                sp.wait_ge(s["loaded"], 16 * len(pairs))

            @block.scalar
            def _(act):
                for to, source in pairs[1::2]:
                    act.dma_start(to, source).then_inc(s["loaded"], 16)


def store(nc, h, out):
    with stage(nc, "store", "stored") as (s, sb, ps):
        with nc.Block() as block:
            @block.sync
            def _(sp):
                sp.dma_start(out, h[:, :]).then_inc(s["stored"], 16)
                sp.wait_ge(s["stored"], 16)


def weights(nc, stack, dram, *names):
    to = {n: stack.enter_context(nc.sbuf_tensor(f"w_{n}", list(dram[n].shape), F32)) for n in names}
    load(nc, "load_" + names[0], [(to[n][tuple(slice(None) for _ in dram[n].shape)], dram[n]) for n in names])
    return to


def tower(nc, dram, out):
    E = 4
    with stage(nc, "tower") as (_, sb, _ps), ExitStack() as stack:
        h, x = sb("h", [D, T]), sb("x", [D, T])
        ones, ident = sb("ones", [2 * D, 2 * D]), sb("ident", [128, 128])
        pick = sb("pick", [8, 8, 128])
        causal, window = sb("causal", [N, N]), sb("window", [N, 2 * 64])
        wT = sb("wt", [8, T])
        key, hist = sb("key", [128, dram["f2_src"].shape[0] // 128]), sb("hist", [HIGH, LOW])
        with ExitStack() as early:
            alibi = early.enter_context(nc.sbuf_tensor("alibi", [N, 8, N], F32))
            constants(nc, ones, ident, pick, causal, alibi)
            window_bias(nc, window, dram["a2_toeplitz"], dram["a2_last"])

            with ExitStack() as own:
                w = weights(nc, own, dram, "tok_wq", "tok_wk", "tok_wv", "tok_wo", "tok_cols", "cls")
                pool_tokens(nc, "tok", dram["x"], h, w["tok_wq"][:, :], w["tok_wk"][:, :], w["tok_wv"], w["tok_wo"], w["tok_cols"], w["cls"][:, 0:1], ident)

            w = weights(nc, early, dram, "a0_wq", "a0_wkv", "a0_wo", "a0_bo", "f0_gw", "f0_gb", "f0_sW1", "f0_sW2", "f0_sW3", "f0_sb",
                        "f0_eW1", "f0_eW2", "f0_eW3", "f0_eb1", "f0_eb2", "f0_eb3", "a1_wqk", "a1_wv", "a1_wo", "a1_bo")
            layer_norm(nc, "a0_ln", h, x, ones)
            linear_attention(nc, "a0", x, h, w["a0_wq"], w["a0_wkv"], w["a0_wo"], w["a0_bo"][:, 0:1])
            layer_norm(nc, "f0_ln", h, x, ones)
            top2(nc, "f0_top", wT[0:E], ident, E, "softmax of gates", x=x, gw=w["f0_gw"][:, :], gb=w["f0_gb"][:, :])
            each = lambda name: [w[name][:, e, :] for e in range(E)]
            column = lambda name: [w[name][:, e:e + 1] for e in range(E)]
            relu_experts(nc, "f0", x, h, wT[0:E], pick[0:E], [w["f0_sW1"][:, :]] + each("f0_eW1"), [w["f0_sb"][0:D, 0:1]] + column("f0_eb1"),
                         [w["f0_sW2"][:, :]] + each("f0_eW2"), [w["f0_sb"][:, 1:2]] + column("f0_eb2"),
                         [w["f0_sW3"][:, :]] + each("f0_eW3"), w["f0_sb"][0:D, 2:3], w["f0_eb3"][:, :])
            layer_norm(nc, "a1_ln", h, x, ones)
            attention(nc, "a1", x, h, w["a1_wqk"], w["a1_wv"][:, :], w["a1_wo"], ident, heads=8, hp=32, scale=32.0 ** -0.5,
                      bias=alibi[:, :, :].rearrange("n (b r) c -> n b r c", r=4), bo=w["a1_bo"][:, 0:1])
        with ExitStack() as own:
            w = weights(nc, own, dram, "f1_wqpk", "f1_keys", "f1_wq", "f1_wo")
            layer_norm(nc, "f1_ln", h, x, ones)
            kv = own.enter_context(nc.sbuf_tensor("f1_kv", [128, 8, T], F32))
            product_keys(nc, "f1_keys", x, w["f1_wqpk"], w["f1_keys"], dram["f1_table"], kv, ident, dram["f2_src"], dram["f2_dst"], key, hist)
            attention(nc, "f1", x, h, w["f1_wq"], None, w["f1_wo"], ident, heads=8, hp=64, scale=64.0 ** -0.5, kv=kv,
                      bias=causal[:, :].unsqueeze(1).unsqueeze(1).to_broadcast([N, 2, 4, N]))
        with ExitStack() as own:
            w = weights(nc, own, dram, "a2_wqk", "a2_wv", "a2_wo", "a2_bo", "f2_wgat", "f2_att", "f2_att_col", "f2_rows", "f2_w1", "f2_b1", "f2_w2", "f2_b2")
            layer_norm(nc, "a2_ln", h, x, ones)
            attention(nc, "a2", x, h, w["a2_wqk"], w["a2_wv"][:, :], w["a2_wo"], ident, heads=8, hp=32, scale=8.0 ** -0.5, keys=128,
                      bo=w["a2_bo"][:, 0:1], bias=window[:, :].unsqueeze(1).unsqueeze(1).to_broadcast([N, 2, 4, 128]))
            layer_norm(nc, "f2_ln", h, x, ones)
            scores = own.enter_context(nc.sbuf_tensor("f2_scores", [N, B, E], F32))
            with ExitStack() as graph:
                countT = graph.enter_context(nc.sbuf_tensor("f2_count", [TT, NT, T], F32))
                absent = graph.enter_context(nc.sbuf_tensor("f2_absent", [TT, NT, T], F32))
                edge_counts(nc, "f2_edges", key, hist, ident, countT, absent)
                graph_scores(nc, "f2_gat", x, w["f2_wgat"][:, :], w["f2_att"], w["f2_att_col"][:, 0:1], w["f2_rows"], ident, pick, countT, absent, scores)
            top2(nc, "f2_top", wT[0:E], ident, E, "softmax", scores=scores)
            gelu_experts(nc, "f2", x, h, wT[0:E], pick[0:E], w["f2_w1"], w["f2_b1"], w["f2_w2"], w["f2_b2"][:, :], E, 2 * D)
        with ExitStack() as own:
            w = weights(nc, own, dram, "a3_wqk", "a3_wv", "a3_wo", "a3_wg", "a3_bg", "a3_cols", "f3_wqk", "f3_wv", "f3_wo", "f3_rope", "f3_cols",
                        "f3_router", "f3_w1", "f3_w3", "f3_w2")
            xn = own.enter_context(nc.sbuf_tensor("xn", [D, T], F32))
            gate = own.enter_context(nc.sbuf_tensor("a3_gate", [128, 2, T], F32))
            layer_norm(nc, "a3_ln", h, x, ones)
            layer_norm(nc, "a3_ln2", x, xn, ones, gain=w["a3_cols"][:, 1:2], shift=w["a3_cols"][:, 2:3])
            gate_values(nc, "a3_gate", x, h, w["a3_wg"], w["a3_bg"], gate)
            attention(nc, "a3", xn, h, w["a3_wqk"], w["a3_wv"][:, :], w["a3_wo"], ident, heads=8, hp=32, scale=32.0 ** -0.5,
                      bo=w["a3_cols"][:, 0:1], gate=gate, over_queries=True)
            layer_norm(nc, "f3_ln", h, x, ones)
            layer_norm(nc, "f3_ln1", x, xn, ones, eps=1e-6, center=False, gain=w["f3_cols"][:, 0:1])
            attention(nc, "f3_att", xn, x, w["f3_wqk"], w["f3_wv"][:, :], w["f3_wo"], ident, heads=4, hp=32, scale=16.0 ** -0.5, rope=w["f3_rope"],
                      bias=causal[:, :].unsqueeze(1).unsqueeze(1).to_broadcast([N, 1, 4, N]))
            layer_norm(nc, "f3_ln2", x, xn, ones, eps=1e-6, center=False, gain=w["f3_cols"][:, 1:2])
            top2(nc, "f3_top", wT, ident, 8, "share", x=xn, gw=w["f3_router"][:, :])
            silu_experts(nc, "f3", xn, h, x, wT, pick, w["f3_w1"], w["f3_w3"], w["f3_w2"], 8, 85)
        store(nc, h, out)


def blocks(w):
    z = np.zeros((2, D, 2, D), w.dtype)
    z[0, :, 0], z[1, :, 1] = w, w
    return z.reshape(2 * D, 2 * D)


def padded_heads(w, of, size, swap=False):
    z = np.zeros((w.shape[0], len(of), 32), w.dtype)
    for place, head in enumerate(of):
        part = w[:, head * size:(head + 1) * size]
        z[:, place, :size] = np.roll(part, size // 2, axis=1) if swap else part
    return z.reshape(w.shape[0], -1)


def lay_out(inputs):
    g = {n: np.asarray(a) for n, a in inputs.items()}
    out = {"x": g["x"]}
    t = lambda n: g["L0_tok_" + n]
    wv = np.zeros((8, D, D), np.float32)
    for head in range(8):
        wv[head][:, head * 8:head * 8 + 8] = t("Wv").T[:, head * 8:head * 8 + 8]
    out.update(tok_wq=blocks(t("Wq").T), tok_wk=blocks(t("Wk")), tok_wv=np.stack([blocks(w) for w in wv], 1), tok_wo=blocks(t("Wo").T),
               tok_cols=np.tile(np.stack([t(n) for n in ("bq", "bk", "bv", "bo")], 1), (2, 1)), cls=g["cls_tok"].reshape(D, 1))
    w = g["L0_attn_w_qkv"].T
    out.update(a0_wq=w[:, :512].reshape(D, 4, 128), a0_wkv=w[:, 512:].reshape(D, 16, 64), a0_bo=g["L0_attn_b_out"].reshape(D, 1),
               a0_wo=g["L0_attn_w_out"].T.reshape(4, 128, D).transpose(1, 0, 2))
    t = lambda n: g["L0_ffn_" + n]
    sb = np.zeros((128, 3), np.float32)
    sb[:D, 0], sb[:, 1], sb[:D, 2] = t("sb1"), t("sb2"), t("sb3")
    out.update(f0_gw=t("gW"), f0_gb=np.broadcast_to(t("gb"), (N, 4)), f0_sW1=t("sW1"), f0_sW2=t("sW2"), f0_sW3=t("sW3"), f0_sb=sb,
               f0_eW1=t("eW1").transpose(1, 0, 2), f0_eW2=t("eW2").transpose(1, 0, 2), f0_eW3=t("eW3").transpose(1, 0, 2),
               f0_eb1=t("eb1").T, f0_eb2=t("eb2").T, f0_eb3=t("eb3"))
    t = lambda n: g["L1_attn_" + n]
    out.update(a1_wqk=np.stack([t("Wq")[:, :128], t("Wq")[:, 128:], t("Wk")[:, :128], t("Wk")[:, 128:]], 1), a1_wv=t("Wv"),
               a1_wo=t("Wo").reshape(2, 128, D).transpose(1, 0, 2), a1_bo=t("bo").reshape(D, 1))
    t = lambda n: g["L1_ffn_" + n]
    keys, values = t("keys_table").reshape(8, 4096, D), t("values_table").reshape(8, 4096, D)
    table = np.empty((8, 4096, 2 * D), np.float32)
    table[0::2, :, :D], table[0::2, :, D:] = keys[0::2], values[0::2]
    table[1::2, :, :D], table[1::2, :, D:] = values[1::2], keys[1::2]
    out.update(f1_wqpk=t("Wq_pk").reshape(D, 4, 128), f1_keys=t("pk_keys").transpose(0, 2, 3, 1).reshape(4, 128, 64).transpose(1, 0, 2),
               f1_table=table.reshape(-1, 2 * D), f1_wq=t("Wq").reshape(D, 4, 128), f1_wo=t("Wo").reshape(4, 128, D).transpose(1, 0, 2))
    t = lambda n: g["L2_attn_" + n]
    w = t("w_qkv").T
    first, second = range(0, 4), range(4, 8)
    q, k, v = (w[:, n * D:(n + 1) * D] for n in range(3))
    toeplitz = t("rel_bias")[np.arange(64)[None] - np.arange(64)[:, None] + 63]
    wo = np.zeros((4, 32, 2, D), np.float32)
    wo[:, :8] = t("w_proj").T.reshape(2, 4, 8, D).transpose(1, 2, 0, 3)
    out.update(a2_wqk=np.stack([padded_heads(m, heads, 8) for m in (q, k) for heads in (first, second)], 1), a2_wv=padded_heads(v, range(8), 8),
               a2_wo=wo.reshape(128, 2, D), a2_bo=t("b_proj").reshape(D, 1), a2_toeplitz=toeplitz, a2_last=t("rel_bias")[63:].reshape(1, 64))
    t = lambda n: g["L2_ffn_" + n]
    out.update(f2_wgat=t("W_gat"), f2_att=np.broadcast_to(np.stack([t("att_src").reshape(16), t("att_dst").reshape(16)]), (TT, 2, 16)),
               f2_att_col=t("att_src").reshape(16, 1), f2_rows=np.broadcast_to(np.stack([t("b_gat"), t("ln_gamma"), t("ln_beta")]), (N, 3, 16)),
               f2_w1=t("W1").transpose(1, 0, 2), f2_b1=t("b1").T, f2_w2=t("W2").transpose(1, 0, 2), f2_b2=t("b2"),
               f2_src=t("edge_index")[0], f2_dst=t("edge_index")[1])
    t = lambda n: g["L3_attn_" + n]
    w = t("W_qkv").T
    out.update(a3_wqk=w[:, :512].reshape(D, 4, 128), a3_wv=w[:, 512:], a3_wo=t("W_final").T.reshape(2, 128, D).transpose(1, 0, 2),
               a3_wg=t("W_gate").T.reshape(D, 2, 128), a3_bg=t("b_gate").reshape(2, 128).T,
               a3_cols=np.stack([t("b_final"), t("ln_gamma"), t("ln_beta")], 1))
    t = lambda n: g["L3_ffn_" + n]
    own, shared = range(4), (0, 0, 1, 1)
    q, k, v = t("wq").T, t("wk").T, t("wv").T
    wo = np.zeros((4, 32, D), np.float32)
    wo[:, :16] = t("wo").T.reshape(4, 16, D)
    angle = np.outer(np.arange(N, dtype=np.float32), 1.0 / 10000.0 ** (np.arange(0, 16, 2, dtype=np.float32) / 16))
    rope = np.zeros((4, 32, 2, N), np.float32)
    rope[:, 0:8, 0] = rope[:, 8:16, 0] = np.cos(angle).T
    rope[:, 0:8, 1], rope[:, 8:16, 1] = -np.sin(angle).T, np.sin(angle).T
    out.update(f3_wqk=np.stack([padded_heads(q, own, 16), padded_heads(k, shared, 16), padded_heads(q, own, 16, True), padded_heads(k, shared, 16, True)], 1),
               f3_wv=padded_heads(v, shared, 16), f3_wo=wo.reshape(128, 1, D), f3_rope=rope.reshape(128, 2, N),
               f3_cols=np.stack([t("ln1_w"), t("ln2_w")], 1), f3_router=t("router_w").T,
               f3_w1=t("w1").transpose(2, 0, 1).reshape(D, 8, 2, 85), f3_w3=t("w3").transpose(2, 0, 1).reshape(D, 8, 2, 85),
               f3_w2=t("w2").transpose(2, 0, 1).reshape(2, 85, 8, D).transpose(1, 2, 0, 3))
    return {n: np.ascontiguousarray(a) for n, a in out.items()}


def kernel(**inputs):
    import concourse.bacc as _bacc
    from concourse.bass_utils import run_bass_kernel_spmd as _run

    nc = _bacc.Bacc("TRN2", target_bir_lowering=False, num_devices=1)
    arrays = {f"in_{n}": a for n, a in lay_out(inputs).items()}
    dram = {n[3:]: nc.dram_tensor(n, a.shape, mybir.dt.from_np(a.dtype), kind="ExternalInput").ap() for n, a in arrays.items()}
    out = nc.dram_tensor("tokens_out", (D, T), F32, kind="ExternalOutput").ap()
    tower(nc, dram, out)
    r = _run(nc, [arrays], core_ids=[0])
    return r.results[0]["tokens_out"].T.reshape(B, N, D)
```

```python
from contextlib import ExitStack, contextmanager

import numpy as np
import concourse.bass as bass
from concourse import mybir

F32 = mybir.dt.float32
BF16 = mybir.dt.bfloat16
U32 = mybir.dt.uint32
I32 = mybir.dt.int32
ALU = mybir.AluOpType
ACT = mybir.ActivationFunctionType
X = mybir.AxisListType.X

B, N, D = 16, 65, 64
T = B * N
IPC = 4
CH = IPC * N
NC = T // CH
NEG = -1.0e30


@contextmanager
def stage(nc, tag, *signals):
    sems = {s: nc.alloc_semaphore(f"{tag}_{s}") for s in signals}
    with ExitStack() as stack:
        def sb(name, shape, dt=F32):
            return stack.enter_context(nc.sbuf_tensor(f"{tag}_{name}", shape, dt))

        def ps(name, shape, dt=F32):
            return stack.enter_context(nc.psum_tensor(f"{tag}_{name}", shape, dt))

        yield sems, sb, ps
    nc.clear_and_free_semaphores(list(sems.values()))
    nc.all_engine_barrier()


def wait_alone(engine, signal, value, passed):
    engine.wait_ge(signal, value)
    engine.sem_inc(passed, 1)


def layer_norm(nc, tag, src, dst, ones, eps=1e-5, center=True, gain=None, shift=None):
    with stage(nc, tag, "mean", "centered", "squared", "var", "std", "rstd", "normed", "gained", "eps") as (s, sb, ps):
        mean_ps = ps("mean", [2 * D, 2, 512]) if center else None
        var_ps = ps("var", [2 * D, 2, 512])
        cent = sb("cent", [2 * D, 2, CH])
        sq = sb("sq", [2 * D, 2, CH])
        rstd = sb("rstd", [2 * D, 2, CH])
        std = sb("std", [2 * D, 2, CH])
        eps_col = sb("eps", [2 * D, 1])
        unused = sb("unused", [2 * D, 1])
        tok = lambda t, c: t[:, c * CH:(c + 1) * CH]
        place = [(a, b, 2 * a + b) for b in range(2) for a in range(2)]
        half = lambda t, a, b: t[a * D:(a + 1) * D, b, 0:CH]
        with nc.Block() as block:
            @block.tensor
            def _(pe):
                if center:
                    for a, b, c in place:
                        nc.tensor.matmul(half(mean_ps, a, b), ones[0:D, 0:D], tok(src, c), start=True, stop=True).then_inc(s["mean"], 1)
                for b in range(2):
                    pe.wait_ge(s["squared"], b + 1)
                    nc.tensor.matmul(var_ps[:, b, 0:CH], ones[:, :], sq[:, b, :], start=True, stop=True).then_inc(s["var"], 1)

            @block.gpsimd
            def _(pool):
                nc.gpsimd.memset(eps_col[:, :], eps).then_inc(s["eps"], 1)

            @block.scalar
            def _(act):
                act.wait_ge(s["eps"], 1)
                nc.scalar.activation(unused[:, :], eps_col[:, :], ACT.Sqrt)
                for b in range(2):
                    act.wait_ge(s["var"], b + 1)
                    nc.scalar.activation(std[:, b, :], var_ps[:, b, 0:CH], ACT.Sqrt, bias=eps_col[:, 0:1]).then_inc(s["std"], 1)

            @block.vector
            def _(dve):
                V = nc.vector
                for n, (a, b, c) in enumerate(place):
                    if center:
                        dve.wait_ge(s["mean"], 2 * b + 2)
                        V.tensor_tensor(half(cent, a, b), tok(src, c), half(mean_ps, a, b), ALU.subtract).then_inc(s["centered"], 1)
                    else:
                        V.tensor_copy(half(cent, a, b), tok(src, c)).then_inc(s["centered"], 1)
                    if a == 1:
                        dve.wait_ge(s["centered"], n + 1)
                        V.tensor_tensor(sq[:, b, :], cent[:, b, :], cent[:, b, :], ALU.mult).then_inc(s["squared"], 1)
                for b in range(2):
                    dve.wait_ge(s["std"], b + 1)
                    V.reciprocal(rstd[:, b, :], std[:, b, :]).then_inc(s["rstd"], 1)
                for n, (a, b, c) in enumerate(place):
                    dve.wait_ge(s["rstd"], b + 1)
                    V.tensor_tensor(tok(dst, c), half(cent, a, b), half(rstd, a, b), ALU.mult).then_inc(s["normed"], 1)
                if gain is not None:
                    for n, (a, b, c) in enumerate(place):
                        dve.wait_ge(s["normed"], n + 1)
                        if shift is not None:
                            V.tensor_scalar(tok(dst, c), tok(dst, c), gain, shift, ALU.mult, ALU.add).then_inc(s["gained"], 1)
                        else:
                            V.tensor_scalar(tok(dst, c), tok(dst, c), gain, None, ALU.mult).then_inc(s["gained"], 1)


def attention(nc, tag, x, h, wqk, wv, wo, ident, *, heads, hp, scale, bias=None, bo=None, keys=N,
              kv=None, rope=None, gate=None, over_queries=False):
    per = 128 // hp
    nb = heads // per
    nq = wqk.shape[1]
    banks = heads // 4
    PROJ = 5 * N
    img = lambda t, m: t[:, m * N:(m + 1) * N] if isinstance(m, int) else t[:, bass.ds(m * N, N)]
    imgs = lambda t, m: t[:, :, m * N:(m + 1) * N] if isinstance(m, int) else t[:, :, bass.ds(m * N, N)]
    with stage(nc, tag, "x_copied", "kv_copied", "pads", "qk_made", "qk_saved", "v_made", "v_saved", "scores", "masked", "maxed",
               "shifted", "exped", "summed", "inverted", "probs", "turned", "turned_saved", "summed_v",
               "out_saved", "projected", "added", "roped", "passed") as (s, sb, ps):
        xb = sb("xb", [D, 2, N])
        spread_q = kv is not None
        qx = sb("qx", [128, 2, nb, per if spread_q else 1, N])
        kx = None if spread_q else sb("kx", [128, 2, nb, per, keys])
        vt = sb("vt", [N, 2, heads * hp])
        kvb = sb("kvb", [128, 2, heads, N]) if spread_q else None
        rp = sb("rp", [128, 2, 2, 2, N]) if rope is not None else None
        z = sb("z", [N, 2, heads, keys])
        stat = sb("stat", [N, 2, 3, heads])
        pt = sb("pt", [N, 2, heads, N])
        ot = sb("ot", [128, 2, nb, N])
        psA = [ps(f"a{u}", [128, 512]) for u in range(2)]
        psB = [ps(f"b{u}", [128, 512]) for u in range(2)]
        psS = ps("s", [128, 2, 2, 512])
        at = lambda u, hd, n: psS[0:N, u, hd // 4, hd % 4 * keys:hd % 4 * keys + n]
        all_at = lambda u, n: psS[0:N, u, 0:banks, 0:4 * keys].rearrange("n b (r c) -> n b r c", r=4)[:, :, :, 0:n]
        by_bank = lambda t: t.rearrange("n (b r) c -> n b r c", r=4)

        with nc.Block() as block:
            @block.gpsimd
            def _(pool):
                def take(m, u):
                    nc.gpsimd.tensor_copy(xb[:, u, :], img(x, m)).then_inc(s["x_copied"], 1)
                    if spread_q:
                        nc.gpsimd.tensor_copy(kvb[:, u, :, :], imgs(kv, m)).then_inc(s["kv_copied"], 1)

                nc.gpsimd.memset(qx[:, :, :, :, :] if spread_q else kx[:, :, :, :, :], 0.0).then_inc(s["pads"], 1)
                for u in range(2):
                    take(u, u)
                with pool.Fori(1, B // 2) as i:
                    for u in range(2):
                        wait_alone(pool, s["v_made"], i * 2 + (u - 1), s["passed"])
                        if spread_q:
                            wait_alone(pool, s["scores"], i * 2 + (u - 1), s["passed"])
                        take(i * 2 + u, u)

            @block.tensor
            def _(pe):
                M = nc.tensor.matmul

                def make_qk(m, u):
                    pe.wait_ge(s["x_copied"], m + 1)
                    for j in range(nq):
                        mm = M(psA[u][:, j * N:(j + 1) * N], wqk[:, j, :], xb[:, u, :], start=True, stop=True)
                    mm.then_inc(s["qk_made"], 1)

                def make_v(m, u):
                    if spread_q:
                        pe.wait_ge(s["kv_copied"], m + 1)
                        for hd in range(heads):
                            mm = nc.tensor.transpose(psS[0:N, u, hd // 4, hd % 4 * 128:hd % 4 * 128 + 128], kvb[:, u, hd, :], ident[:, :])
                        mm.then_inc(s["v_made"], 1)
                    else:
                        M(psB[u][0:N, 0:heads * hp], xb[:, u, :], wv, start=True, stop=True).then_inc(s["v_made"], 1)

                def score(m, u):
                    pe.wait_ge(s["qk_saved"], m + 1)
                    if spread_q:
                        pe.wait_ge(s["v_saved"], m + 1)
                        for hd in range(heads):
                            mm = M(at(u, hd, N), qx[:, u, hd // per, hd % per, :], kvb[:, u, hd, :], start=True, stop=True)
                    else:
                        for j in range(nb):
                            mm = M(psS[0:N, u, j, 0:per * keys], qx[:, u, j, 0, :], kx[:, u, j, :, :], start=True, stop=True)
                    mm.then_inc(s["scores"], 1)

                def turn(m, u):
                    pe.wait_ge(s["probs"], m + 1)
                    if not over_queries:
                        for hd in range(heads):
                            mm = nc.tensor.transpose(at(u, hd, N), z[:, u, hd, 0:N], ident[0:N, 0:N])
                        mm.then_inc(s["turned"], 1)

                def finish(m, u, last):
                    if not over_queries:
                        pe.wait_ge(s["turned_saved"], m + 1)
                    pe.wait_ge(s["v_saved"], m + 1)
                    if not last:
                        pe.wait_ge(s["qk_saved"], m + 3)
                    for hd in range(heads):
                        p, j = hp * (hd % per), hd // per
                        probs = z[:, u, hd, 0:N] if over_queries else pt[:, u, hd, :]
                        mm = M(psA[u][p:p + hp, j * N:(j + 1) * N], vt[:, u, hd * hp:(hd + 1) * hp], probs, start=True, stop=True)
                    mm.then_inc(s["summed_v"], 1)
                    pe.wait_ge(s["out_saved"], m + 1)
                    for j in range(nb):
                        mm = M(psA[u][0:D, PROJ:PROJ + N], wo[:, j, :], ot[:, u, j, :], start=(j == 0), stop=(j == nb - 1))
                    mm.then_inc(s["projected"], 1)

                def step(m, u):
                    score(m, u)
                    turn(m - 1, 1 - u)
                    if not isinstance(m, int) or m > 1:
                        pe.wait_ge(s["added"], m - 1)
                    make_qk(m + 1, 1 - u)
                    if spread_q:
                        pe.wait_ge(s["turned_saved"], m)
                    make_v(m + 1, 1 - u)
                    finish(m - 1, 1 - u, False)

                pe.wait_ge(s["pads"], 1)
                make_qk(0, 0)
                make_v(0, 0)
                score(0, 0)
                make_qk(1, 1)
                make_v(1, 1)
                step(1, 1)
                with pe.Fori(1, B // 2 - 1) as i:
                    step(i * 2, 0)
                    step(i * 2 + 1, 1)
                step(B - 2, 0)
                score(B - 1, 1)
                for m in (B - 2, B - 1):
                    turn(m, m % 2)
                    finish(m, m % 2, True)

            @block.scalar
            def _(act):
                C = nc.scalar.copy

                def save_qk(m, u):
                    if rope is None:
                        act.wait_ge(s["qk_made"], m + 1)
                        made = psA[u][:, 0:nq * N].rearrange("p (j n) -> p j n", n=N)
                        if not spread_q:
                            C(qx[:, u, :, 0, :], made[:, 0:nb, :])
                        for r in range(per):
                            rows = slice(r * hp, (r + 1) * hp)
                            to = qx[rows, u, :, r, :] if spread_q else kx[rows, u, :, r, 0:N]
                            last = C(to, made[rows, nq - nb:nq, :])
                        last.then_inc(s["qk_saved"], 1)

                def save_v(m, u):
                    act.wait_ge(s["v_made"], m + 1)
                    if spread_q:
                        v_of = vt[:, u, :].rearrange("n (b r two d) -> n b r two d", b=banks, two=2, d=hp)
                        turned = psS[0:N, u, :, :].rearrange("n b (r two c) -> n b r two c", two=2, c=128)
                        C(v_of[:, :, :, 0, :], turned[:, :, :, 0, hp:2 * hp])
                        C(v_of[:, :, :, 1, :], turned[:, :, :, 1, 0:hp]).then_inc(s["v_saved"], 1)
                    else:
                        C(vt[:, u, :], psB[u][0:N, 0:heads * hp]).then_inc(s["v_saved"], 1)

                def save_turned(m, u):
                    if not over_queries:
                        act.wait_ge(s["turned"], m + 1)
                        C(by_bank(pt[:, u, :, :]), all_at(u, N)).then_inc(s["turned_saved"], 1)

                def exp(m, u):
                    act.wait_ge(s["shifted"], m + 1)
                    nc.scalar.activation(z[:, u, :, :], z[:, u, :, :], ACT.Exp, scale=scale).then_inc(s["exped"], 1)

                def save_out(m, u):
                    if gate is None:
                        act.wait_ge(s["summed_v"], m + 1)
                        C(ot[:, u, :, :], psA[u][:, 0:nb * N].rearrange("p (j n) -> p j n", n=N)).then_inc(s["out_saved"], 1)

                def step(m, u):
                    save_turned(m - 1, 1 - u)
                    save_qk(m + 1, 1 - u)
                    exp(m, u)
                    save_out(m - 1, 1 - u)
                    act.wait_ge(s["summed_v"], m)
                    save_v(m + 1, 1 - u)

                act.wait_ge(s["pads"], 1)
                save_qk(0, 0)
                save_v(0, 0)
                save_qk(1, 1)
                exp(0, 0)
                save_v(1, 1)
                with act.Fori(0, B // 2 - 1) as i:
                    step(i * 2 + 1, 1)
                    step(i * 2 + 2, 0)
                save_turned(B - 2, 0)
                exp(B - 1, 1)
                save_out(B - 2, 0)
                save_turned(B - 1, 1)
                save_out(B - 1, 1)

            @block.vector
            def _(dve):
                V = nc.vector

                def rotate(m, u):
                    if rope is not None:
                        made = psA[u][:, 0:nq * N].rearrange("p (a j n) -> p a j n", a=2, n=N)
                        dve.wait_ge(s["qk_made"], m + 1)
                        for a in range(2):
                            last = V.tensor_tensor(rp[:, u, a, :, :], made[:, a, :, :], rope[:, a:a + 1, :].to_broadcast([128, 2, N]), ALU.mult)
                        last.then_inc(s["roped"], 1)
                        dve.wait_ge(s["roped"], m + 1)
                        V.tensor_tensor(qx[:, u, 0, 0, :], rp[:, u, 0, 0, :], rp[:, u, 1, 0, :], ALU.add)
                        for r in range(per):
                            rows = slice(r * hp, (r + 1) * hp)
                            last = V.tensor_tensor(kx[rows, u, 0, r, 0:N], rp[rows, u, 0, 1, :], rp[rows, u, 1, 1, :], ALU.add)
                        last.then_inc(s["qk_saved"], 1)

                def shift(m, u):
                    dve.wait_ge(s["scores"], m + 1)
                    of, zz = all_at(u, keys), by_bank(z[:, u, :, :])
                    if bias is not None:
                        V.tensor_tensor(zz, of, bias, ALU.add).then_inc(s["masked"], 1)
                        dve.wait_ge(s["masked"], m + 1)
                        of = zz
                    mx = stat[:, u, 0, :].rearrange("n (b r) -> n b r", r=4)
                    V.tensor_reduce(mx, of, X, ALU.max).then_inc(s["maxed"], 1)
                    dve.wait_ge(s["maxed"], m + 1)
                    V.tensor_tensor(zz, of, mx.unsqueeze(3).to_broadcast([N, banks, 4, keys]), ALU.subtract).then_inc(s["shifted"], 1)

                def norm(m, u):
                    dve.wait_ge(s["exped"], m + 1)
                    V.tensor_reduce(stat[:, u, 1, :], z[:, u, :, :], X, ALU.add).then_inc(s["summed"], 1)
                    dve.wait_ge(s["summed"], m + 1)
                    V.reciprocal(stat[:, u, 2, :], stat[:, u, 1, :]).then_inc(s["inverted"], 1)
                    dve.wait_ge(s["inverted"], m + 1)
                    V.tensor_tensor(z[:, u, :, 0:N], z[:, u, :, 0:N], stat[:, u, 2, :].unsqueeze(2).to_broadcast([N, heads, N]), ALU.mult).then_inc(s["probs"], 1)

                def save_gated(m, u):
                    if gate is not None:
                        dve.wait_ge(s["summed_v"], m + 1)
                        V.tensor_tensor(ot[:, u, :, :], psA[u][:, 0:nb * N].rearrange("p (j n) -> p j n", n=N), imgs(gate, m), ALU.mult).then_inc(s["out_saved"], 1)

                def add(m, u):
                    dve.wait_ge(s["projected"], m + 1)
                    mine, made = img(h, m), psA[u][0:D, PROJ:PROJ + N]
                    if bo is not None:
                        V.scalar_tensor_tensor(mine, made, bo, mine, ALU.add, ALU.add).then_inc(s["added"], 1)
                    else:
                        V.tensor_tensor(mine, made, mine, ALU.add).then_inc(s["added"], 1)

                def step(m, u):
                    shift(m, u)
                    rotate(m + 1, 1 - u)
                    save_gated(m - 1, 1 - u)
                    norm(m, u)
                    add(m - 1, 1 - u)

                dve.wait_ge(s["pads"], 1)
                rotate(0, 0)
                shift(0, 0)
                rotate(1, 1)
                norm(0, 0)
                with dve.Fori(0, B // 2 - 1) as i:
                    step(i * 2 + 1, 1)
                    step(i * 2 + 2, 0)
                shift(B - 1, 1)
                norm(B - 1, 1)
                for m in (B - 2, B - 1):
                    save_gated(m, m % 2)
                    add(m, m % 2)


def linear_attention(nc, tag, x, h, wq, wkv, wo, bo):
    H, dh, two, nb = 8, 64, 2, 4
    with stage(nc, tag, "wsum", "wmean", "wcentered", "x_copied", "q_made", "kv_made", "q_saved", "squared", "sums",
               "eps", "root", "inverted", "kv_saved", "dots", "dots_saved", "out", "out_saved", "projected", "added", "passed") as (s, sb, ps):
        wmean = sb("wmean", [D, 2, 2 * H])
        eps_col = sb("eps", [N, 1])
        xb = sb("xb", [D, two, N])
        q = sb("q", [128, two, nb, N])
        sq = sb("sq", [N, two, 2 * H, dh])
        kv = sb("kv", [N, two, 2 * H, dh])
        stat = sb("stat", [N, two, 3, 2 * H])
        dots = sb("dots", [128, two, nb, 128])
        ot = sb("ot", [128, two, nb, N])
        psQ = [ps(f"q{u}", [128, 512]) for u in range(two)]
        psKV = [ps(f"kv{u}", [128, 2, 512]) for u in range(two)]
        psD = [ps(f"d{u}", [128, 512]) for u in range(two)]
        img = lambda t, m: t[:, m * N:(m + 1) * N] if isinstance(m, int) else t[:, bass.ds(m * N, N)]

        def pipeline(engine, step):
            step(0, 0)
            with engine.Fori(1, B // two) as i:
                step(i * two - 1, 1)
                step(i * two, 0)

        with nc.Block() as block:
            @block.gpsimd
            def _(pool):
                nc.gpsimd.memset(eps_col[:, :], 1e-5).then_inc(s["eps"], 1)
                nc.gpsimd.memset(dots[:, :, :, :], 0.0).then_inc(s["eps"], 1)

                def take(m, u):
                    nc.gpsimd.tensor_copy(xb[:, u, :], img(x, m)).then_inc(s["x_copied"], 1)

                def step(m, u):
                    if not isinstance(m, int) or m:
                        wait_alone(pool, s["q_made"], m, s["passed"])
                    take(m + 1, 1 - u)

                take(0, 0)
                pipeline(pool, step)

            @block.tensor
            def _(pe):
                M = nc.tensor.matmul

                def make_kv(m, u):
                    pe.wait_ge(s["x_copied"], m + 1)
                    if not isinstance(m, int) or m > 1:
                        pe.wait_ge(s["added"], m - 1)
                    for part in range(2):
                        mm = M(psKV[u][0:N, part, :], xb[:, u, :], wkv[:, part * H:(part + 1) * H, :], start=True, stop=True)
                    mm.then_inc(s["kv_made"], 1)

                def make_q(m, u):
                    for j in range(nb):
                        mm = M(psQ[u][:, j * N:(j + 1) * N], wq[:, j, :], xb[:, u, :], start=True, stop=True)
                    mm.then_inc(s["q_made"], 1)

                def dot(m, u):
                    pe.wait_ge(s["kv_saved"], m + 1)
                    for hd in range(H):
                        p = dh * (hd % 2)
                        mm = M(psD[u][p:p + dh, (hd // 2) * dh:(hd // 2 + 1) * dh], kv[:, u, hd, :], kv[:, u, H + hd, :], start=True, stop=True)
                    mm.then_inc(s["dots"], 1)

                def finish(m, u):
                    pe.wait_ge(s["q_saved"], m + 1)
                    pe.wait_ge(s["dots_saved"], m * 2 + 2)
                    for j in range(nb):
                        mm = M(psQ[u][:, j * N:(j + 1) * N], dots[:, u, j, :], q[:, u, j, :], start=True, stop=True)
                    mm.then_inc(s["out"], 1)
                    pe.wait_ge(s["out_saved"], m + 1)
                    for j in range(nb):
                        mm = M(psKV[u][0:D, 1, 0:N], wo[:, j, :], ot[:, u, j, :], start=(j == 0), stop=(j == nb - 1))
                    mm.then_inc(s["projected"], 1)

                def step(m, u):
                    make_kv(m + 1, 1 - u)
                    dot(m, u)
                    make_q(m + 1, 1 - u)
                    finish(m, u)

                pe.wait_ge(s["wcentered"], 1)
                make_kv(0, 0)
                make_q(0, 0)
                pipeline(pe, step)
                dot(B - 1, 1)
                finish(B - 1, 1)

            @block.scalar
            def _(act):
                A = nc.scalar.activation

                def square(m, u):
                    act.wait_ge(s["kv_made"], m + 1)
                    A(sq[:, u, :, :], psKV[u][0:N, :, :].rearrange("n a (h d) -> n (a h) d", d=dh), ACT.Square).then_inc(s["squared"], 1)

                def save_q(m, u):
                    act.wait_ge(s["q_made"], m + 1)
                    A(q[:, u, :, :], psQ[u][:, 0:nb * N].rearrange("p (j n) -> p j n", n=N), ACT.Copy).then_inc(s["q_saved"], 1)

                def root(m, u):
                    act.wait_ge(s["sums"], m + 1)
                    A(stat[:, u, 1, :], stat[:, u, 0, :], ACT.Sqrt, bias=eps_col[:, 0:1], scale=1.0 / dh).then_inc(s["root"], 1)

                def save_dots(m, u):
                    act.wait_ge(s["dots"], m + 1)
                    for p in (0, dh):
                        A(dots[p:p + dh, u, :, p:p + dh], psD[u][p:p + dh, 0:nb * dh].rearrange("p (j d) -> p j d", d=dh), ACT.Copy, scale=1.0 / N).then_inc(s["dots_saved"], 1)

                def save_out(m, u):
                    act.wait_ge(s["out"], m + 1)
                    A(ot[:, u, :, :], psQ[u][:, 0:nb * N].rearrange("p (j n) -> p j n", n=N), ACT.Copy).then_inc(s["out_saved"], 1)

                def step(m, u):
                    square(m + 1, 1 - u)
                    save_dots(m, u)
                    root(m + 1, 1 - u)
                    save_q(m + 1, 1 - u)
                    save_out(m, u)

                act.wait_ge(s["eps"], 2)
                square(0, 0)
                root(0, 0)
                save_q(0, 0)
                pipeline(act, step)
                save_dots(B - 1, 1)
                save_out(B - 1, 1)

            @block.vector
            def _(dve):
                V = nc.vector

                def norm(m, u):
                    dve.wait_ge(s["squared"], m + 1)
                    V.tensor_reduce(stat[:, u, 0, :], sq[:, u, :, :], X, ALU.add).then_inc(s["sums"], 1)
                    dve.wait_ge(s["root"], m + 1)
                    V.reciprocal(stat[:, u, 2, :], stat[:, u, 1, :]).then_inc(s["inverted"], 1)
                    dve.wait_ge(s["inverted"], m + 1)
                    V.tensor_tensor(kv[:, u, :, :], psKV[u][0:N, :, :].rearrange("n a (h d) -> n (a h) d", d=dh),
                                    stat[:, u, 2, :].unsqueeze(2).to_broadcast([N, 2 * H, dh]), ALU.mult).then_inc(s["kv_saved"], 1)

                def add(m, u):
                    dve.wait_ge(s["projected"], m + 1)
                    V.scalar_tensor_tensor(img(h, m), psKV[u][0:D, 1, 0:N], bo, img(h, m), ALU.add, ALU.add).then_inc(s["added"], 1)

                def step(m, u):
                    norm(m + 1, 1 - u)
                    add(m, u)

                V.tensor_reduce(wmean[:, 0, :], wkv[:, :, :], X, ALU.add).then_inc(s["wsum"], 1)
                dve.wait_ge(s["wsum"], 1)
                V.tensor_scalar(wmean[:, 1, :], wmean[:, 0, :], 1.0 / dh, None, ALU.mult).then_inc(s["wmean"], 1)
                dve.wait_ge(s["wmean"], 1)
                V.tensor_tensor(wkv[:, :, :], wkv[:, :, :], wmean[:, 1, :].unsqueeze(2).to_broadcast([D, 2 * H, dh]), ALU.subtract).then_inc(s["wcentered"], 1)
                norm(0, 0)
                pipeline(dve, step)
                add(B - 1, 1)


def top2(nc, tag, wT, ident, E, mode, x=None, gw=None, gb=None, scores=None):
    gated = scores is None
    with stage(nc, tag, "logits", "chain", "ones", "tri", "shifted", "exped", "weights", "turned", "saved") as (s, sb, ps):
        g = sb("g", [N, B, E]) if gated else scores
        z = sb("z", [N, B, E])
        gt = sb("gt", [N, B, E, E])
        eq = sb("eq", [N, B, E, E])
        tri = sb("tri", [N, E, E])
        st = sb("st", [N, 2, B])
        rank = sb("rank", [N, B, E])
        logits_ps = ps("logits", [N, B, E])
        wT_ps = ps("wT", [E, NC, 512])
        wide = lambda t: t.unsqueeze(2).to_broadcast([N, B, E])
        every = [N, B, E, E]
        n_exp = 2 if mode == "softmax of gates" else 1
        with nc.Block() as block:
            @block.gpsimd
            def _(pool):
                nc.gpsimd.memset(tri[:, :, :], 1.0).then_inc(s["ones"], 1)
                pool.wait_ge(s["ones"], 1)
                nc.gpsimd.affine_select(out=tri[:, :, :], in_=tri[:, :, :], compare_op=ALU.is_ge, fill=0.0, base=-1,
                                        pattern=[[1, E], [-1, E]], channel_multiplier=0).then_inc(s["tri"], 1)

            @block.tensor
            def _(pe):
                if gated:
                    for b in range(B):
                        mm = nc.tensor.matmul(logits_ps[:, b, :], x[:, b * N:(b + 1) * N], gw, start=True, stop=True)
                    mm.then_inc(s["logits"], 1)
                pe.wait_ge(s["weights"], 1)
                for b in range(B):
                    mm = nc.tensor.transpose(wT_ps[:, b // IPC, (b % IPC) * N:(b % IPC + 1) * N], z[:, b, :], ident[0:N, 0:N])
                mm.then_inc(s["turned"], 1)

            @block.scalar
            def _(act):
                for n in range(n_exp):
                    act.wait_ge(s["shifted"], n + 1)
                    if mode != "share" and n == n_exp - 1:
                        nc.scalar.activation(z[:, :, :], z[:, :, :], ACT.Exp).then_inc(s["exped"], 1)
                    else:
                        nc.scalar.activation(g[:, :, :], g[:, :, :], ACT.Exp).then_inc(s["exped"], 1)
                act.wait_ge(s["turned"], 1)
                nc.scalar.activation(wT[:, :].rearrange("e (c t) -> e c t", c=NC), wT_ps[:, :, 0:CH], ACT.Copy).then_inc(s["saved"], 1)

            @block.vector
            def _(dve):
                links = [0]

                def link(ins):
                    links[0] += 1
                    ins.then_inc(s["chain"], 1)
                    dve.wait_ge(s["chain"], links[0])

                V = nc.vector
                if gated:
                    dve.wait_ge(s["logits"], 1)
                    if gb is not None:
                        link(V.tensor_tensor(g[:, :, :], logits_ps[:, :, :], gb.unsqueeze(1).to_broadcast([N, B, E]), ALU.add))
                    else:
                        link(V.tensor_copy(g[:, :, :], logits_ps[:, :, :]))
                    link(V.tensor_reduce(st[:, 0, :], g[:, :, :], X, ALU.max))
                    V.tensor_tensor(g[:, :, :], g[:, :, :], wide(st[:, 0, :]), ALU.subtract).then_inc(s["shifted"], 1)
                    dve.wait_ge(s["exped"], 1)
                    link(V.tensor_reduce(st[:, 0, :], g[:, :, :], X, ALU.add))
                    link(V.reciprocal(st[:, 1, :], st[:, 0, :]))
                    link(V.tensor_tensor(g[:, :, :], g[:, :, :], wide(st[:, 1, :]), ALU.mult))
                dve.wait_ge(s["tri"], 1)
                mine, other = g[:, :, :].unsqueeze(3).to_broadcast(every), g[:, :, :].unsqueeze(2).to_broadcast(every)
                V.tensor_tensor(gt[:, :, :, :], other, mine, ALU.is_gt)
                link(V.tensor_tensor(eq[:, :, :, :], other, mine, ALU.is_equal))
                link(V.tensor_tensor(eq[:, :, :, :], eq[:, :, :, :], tri[:, :, :].unsqueeze(1).to_broadcast(every), ALU.mult))
                link(V.tensor_tensor(gt[:, :, :, :], gt[:, :, :, :], eq[:, :, :, :], ALU.add))
                link(V.tensor_reduce(rank[:, :, :], gt[:, :, :, :], X, ALU.add))
                if mode == "share":
                    link(V.scalar_tensor_tensor(z[:, :, :], rank[:, :, :], 2.0, g[:, :, :], ALU.is_lt, ALU.mult))
                    link(V.tensor_reduce(st[:, 0, :], z[:, :, :], X, ALU.add))
                    link(V.tensor_scalar(st[:, 0, :], st[:, 0, :], 1e-9, None, ALU.add))
                else:
                    link(V.tensor_reduce(st[:, 0, :], g[:, :, :], X, ALU.max))
                    V.tensor_tensor(z[:, :, :], g[:, :, :], wide(st[:, 0, :]), ALU.subtract).then_inc(s["shifted"], 1)
                    dve.wait_ge(s["exped"], n_exp)
                    link(V.scalar_tensor_tensor(z[:, :, :], rank[:, :, :], 2.0, z[:, :, :], ALU.is_lt, ALU.mult))
                    link(V.tensor_reduce(st[:, 0, :], z[:, :, :], X, ALU.add))
                link(V.reciprocal(st[:, 1, :], st[:, 0, :]))
                V.tensor_tensor(z[:, :, :], z[:, :, :], wide(st[:, 1, :]), ALU.mult).then_inc(s["weights"], 1)


KEY = 2048
LOW = 32
HIGH = T // LOW + 1
LC = 46


def chunk(t, i):
    return t[:, i * CH:(i + 1) * CH]


def relu_experts(nc, tag, x, h, wT, pick, W1, b1, W2, b2, W3, sb3, eb3):
    M = len(W1)
    with stage(nc, tag, "first", "first_saved", "second", "second_saved", "weight", "weighted", "sum", "added") as (s, sb, ps):
        h1 = sb("h1", [128, 2, CH])
        h2 = sb("h2", [128, 2, CH])
        hw = sb("hw", [128, 2, CH])
        p1 = [ps(f"p1{k}", [128, 512]) for k in range(2)]
        p2 = [ps(f"p2{k}", [128, 512]) for k in range(2)]
        pw = [ps(f"pw{k}", [128, 512]) for k in range(2)]
        acc = ps("acc", [D, 512])
        n1 = [w.shape[1] for w in W1]
        n2 = [w.shape[1] for w in W2]
        place = [(i, m) for i in range(NC) for m in range(M)]
        gated = lambda i, m: i * (M - 1) + m
        with nc.Block() as block:
            @block.tensor
            def _(pe):
                def first(n):
                    if n >= len(place):
                        return
                    i, m = place[n]
                    if n >= 2:
                        pe.wait_ge(s["first_saved"], n - 1)
                    nc.tensor.matmul(p1[n % 2][0:n1[m], 0:CH], W1[m], chunk(x, i), start=True, stop=True).then_inc(s["first"], 1)

                def last(n):
                    i, m = place[n]
                    if m == 0:
                        if i:
                            pe.wait_ge(s["added"], i)
                        nc.tensor.matmul(acc[:, 0:CH], eb3, chunk(wT, i), start=True, stop=False)
                        pe.wait_ge(s["second_saved"], n + 1)
                    else:
                        pe.wait_ge(s["weighted"], gated(i, m))
                    src = (hw[0:n2[m], gated(i, m) % 2, :] if m else h2[0:n2[m], n % 2, :])
                    mm = nc.tensor.matmul(acc[:, 0:CH], W3[m], src, start=False, stop=(m == M - 1))
                    if m == M - 1:
                        mm.then_inc(s["sum"], 1)

                first(0)
                for n, (i, m) in enumerate(place):
                    first(n + 1)
                    pe.wait_ge(s["first_saved"], n + 1)
                    if n >= 2:
                        pe.wait_ge(s["second_saved"], n - 1)
                    nc.tensor.matmul(p2[n % 2][0:n2[m], 0:CH], W2[m], h1[0:n1[m], n % 2, :], start=True, stop=True).then_inc(s["second"], 1)
                    if m:
                        if gated(i, m) >= 3:
                            pe.wait_ge(s["weighted"], gated(i, m) - 2)
                        nc.tensor.matmul(pw[gated(i, m) % 2][0:n2[m], 0:CH], pick[0:M - 1, m - 1, 0:n2[m]], chunk(wT, i), start=True, stop=True).then_inc(s["weight"], 1)
                    if n:
                        last(n - 1)
                last(len(place) - 1)

            @block.scalar
            def _(act):
                for n, (i, m) in enumerate(place):
                    act.wait_ge(s["first"], n + 1)
                    if n >= 2:
                        act.wait_ge(s["second"], n - 1)
                    nc.scalar.activation(h1[0:n1[m], n % 2, :], p1[n % 2][0:n1[m], 0:CH], ACT.Relu, bias=b1[m]).then_inc(s["first_saved"], 1)
                    act.wait_ge(s["second"], n + 1)
                    if n >= 2 and place[n - 2][1]:
                        act.wait_ge(s["weighted"], gated(*place[n - 2]))
                    nc.scalar.activation(h2[0:n2[m], n % 2, :], p2[n % 2][0:n2[m], 0:CH], ACT.Relu, bias=b2[m]).then_inc(s["second_saved"], 1)

            @block.vector
            def _(dve):
                for n, (i, m) in enumerate(place):
                    if m:
                        k = gated(i, m)
                        dve.wait_ge(s["second_saved"], n + 1)
                        dve.wait_ge(s["weight"], k)
                        nc.vector.tensor_tensor(hw[0:n2[m], k % 2, :], h2[0:n2[m], n % 2, :], pw[k % 2][0:n2[m], 0:CH], ALU.mult).then_inc(s["weighted"], 1)
                    if m == M - 1:
                        dve.wait_ge(s["sum"], i + 1)
                        nc.vector.scalar_tensor_tensor(chunk(h, i), acc[:, 0:CH], sb3, chunk(h, i), ALU.add, ALU.add).then_inc(s["added"], 1)


PK = 16
NKEY = 64
TT = 104
NT = T // TT
TG = 8
HG = TG // 2


def product_keys(nc, tag, x, wq, keys, table, kv, ident, src_ap, dst_ap, key, hist):
    H, G2, SL = 8, 16, slice(None)
    LINKS = 21
    rounds = TT // TG
    early = 8
    late = rounds - early
    L = key.shape[1]
    LP = (NT - 1) * late * LC
    assert LP >= L
    with stage(nc, tag, "q", "q_saved", "iota_i", "consts", "q_tile", "sim", "sim_saved", "chain", "shifted", "exped", "rows_ready",
               "turned", "index_saved", "spread", "staged", "gathered0", "gathered1", "weighed", "kv_saved", "passed",
               "edges_loaded", "digit_chain", "zero", "hot", "hot_used", "hist", "hist_saved") as (s, sb, ps):
        src = sb("src", [128, L], I32)
        dst = sb("dst", [128, L], I32)
        srcf = sb("srcf", [128, L])
        digits = sb("digits", [128, 2, LP], BF16)
        hot_hi = sb("hot_hi", [128, LC, HIGH], BF16)
        hot_lo = sb("hot_lo", [128, LC, LOW], BF16)
        digit = sb("digit", [128, HIGH], BF16)
        zero = sb("zero", [128, HIGH], BF16)
        qT = sb("qT", [128, 4, T])
        qb = sb("qb", [128, 4, TT])
        sim = sb("sim", [TT, G2, NKEY])
        sim2 = sb("sim2", [TT, G2, NKEY])
        top = sb("top", [TT, G2, PK])
        topi = sb("topi", [TT, G2, PK], U32)
        topf = sb("topf", [TT, G2, PK])
        sums = sb("sums", [TT, H, PK * PK])
        sums2 = sb("sums2", [TT, H, PK * PK])
        best = sb("best", [TT, H, PK])
        besti = sb("besti", [TT, H, PK], U32)
        part_u = sb("part_u", [TT, 2, H * PK], U32)
        part = sb("part", [TT, 2, H, PK])
        half_i = sb("half_i", [TT, 2, H, PK])
        row = sb("row", [TT, H, PK])
        wt = sb("wt", [TT, H, PK])
        st = sb("st", [TT, 2, H])
        head0 = sb("head0", [TT, H, PK])
        count = sb("count", [TT, PK])
        own = sb("own", [128, H])
        idxT = sb("idxT", [128, T + TG], U32)
        spread = sb("spread", [128, T, H])
        idx = [sb(f"idx{a}", [128, HG], U32) for a in range(2)]
        got = [sb(f"got{n}", [128, 128]) for n in range(TG)]
        psQ = ps("s", [128, 4, 512])
        psS = psQ[0:TT, :, :]
        psT = ps("t", [128, 2, 256])
        psH = ps("h", [128, 512])[0:HIGH, 0:LOW]
        psG = [ps(f"g{a}", [128, 512]) for a in range(2)]
        full = [TT, H, PK, PK]
        with nc.Block() as block:
            def gather_at(t, g):
                return t * TT + g * TG

            @block.sync
            def _(sp):
                sp.dma_start(src[:, :], src_ap.rearrange("(p l) -> p l", p=128)).then_inc(s["edges_loaded"], 16)
                sp.dma_start(dst[:, :], dst_ap.rearrange("(p l) -> p l", p=128)).then_inc(s["edges_loaded"], 16)

            @block.gpsimd
            def _(pool):
                P = nc.gpsimd
                P.iota(head0[:, :, :], [[NKEY * NKEY, H], [0, PK]], base=0, channel_multiplier=0, allow_small_or_imprecise_dtypes=True)
                P.iota(count[:, :], [[1, PK]], base=0, channel_multiplier=0, allow_small_or_imprecise_dtypes=True)
                P.iota(digit[:, :], [[1, HIGH]], base=0, channel_multiplier=0, allow_small_or_imprecise_dtypes=True)
                P.memset(zero[:, :], 0.0).then_inc(s["zero"], 1)
                P.memset(own[:, :], 1.0).then_inc(s["iota_i"], 1)
                pool.wait_ge(s["iota_i"], 1)
                P.memset(idxT[:, T:T + TG], 0)
                P.affine_select(out=own[:, :], in_=own[:, :], compare_op=ALU.is_ge, fill=0.0, base=0, pattern=[[-PK, H]], channel_multiplier=1).then_inc(s["iota_i"], 1)
                pool.wait_ge(s["iota_i"], 2)
                P.affine_select(out=own[:, :], in_=own[:, :], compare_op=ALU.is_ge, fill=0.0, base=PK - 1, pattern=[[PK, H]], channel_multiplier=-1).then_inc(s["consts"], 1)
                pool.wait_ge(s["consts"], 1)
                with pool.Fori(0, T // TG) as n:
                    for a in range(2):
                        wait_alone(pool, s["staged"], n * 2 + (a + 1), s["passed"])
                        for k in range(HG):
                            P.indirect_dma_start(out=got[a * HG + k][:, :], out_offset=None, in_=table,
                                                 in_offset=bass.IndirectOffsetOnAxis(ap=idx[a][:, k:k + 1], axis=0)).then_inc(s[f"gathered{a}"], 16)

            @block.tensor
            def _(pe):
                M = nc.tensor.matmul

                def make_q(c):
                    for j in range(4):
                        if c > 1:
                            pe.wait_ge(s["q_saved"], (c - 1) * 4 + j + 1)
                        M(psQ[:, j, 0:CH], wq[:, j, :], chunk(x, c), start=True, stop=True).then_inc(s["q"], 1)

                def score(t):
                    pe.wait_ge(s["q_tile"], t + 1)
                    for f in range(G2):
                        r, j = f % 4, f // 4
                        mm = M(psS[:, r, j * NKEY:(j + 1) * NKEY], qb[32 * r:32 * r + 32, j, :], keys[32 * r:32 * r + 32, j, :], start=True, stop=True)
                    mm.then_inc(s["sim"], 1)

                def turn(t):
                    pe.wait_ge(s["rows_ready"], t + 1)
                    nc.tensor.transpose(psT[:, 0, 0:TT], row[:, :, :].rearrange("n h k -> n (h k)"), ident[0:TT, 0:TT])
                    nc.tensor.transpose(psT[:, 1, 0:TT], wt[:, :, :].rearrange("n h k -> n (h k)"), ident[0:TT, 0:TT]).then_inc(s["turned"], 1)

                def weigh(t, first, steps, count_edges=False):
                    wait_alone(pe, s["spread"], t + 1, s["passed"])
                    with pe.Fori(0, steps) as k_:
                        g = k_ + first
                        for a in range(2):
                            pe.wait_ge(s[f"gathered{a}"], (t * rounds + g) * (16 * HG) + 16 * HG)
                            for k in range(HG):
                                mm = M(psG[a][:, k * H:(k + 1) * H], got[a * HG + k][:, :],
                                       spread[:, bass.ds(gather_at(t, g) + (a * HG + k), 1), :].rearrange("p o h -> p (o h)"), start=True, stop=True)
                            mm.then_inc(s["weighed"], 1)
                        if count_edges:
                            pe.wait_ge(s["hot"], t * late + k_ + 1)
                            for k in range(LC):
                                mm = M(psH, hot_hi[:, k, :], hot_lo[:, k, :], start=False, stop=False, skip_group_check=True)
                            mm.then_inc(s["hot_used"], 1)
                        pe.wait_ge(s["kv_saved"], (t * rounds + g) * 2 + 2)

                pe.wait_ge(s["zero"], 1)
                M(psH, zero[:, :], zero[:, 0:LOW], start=True, stop=False)
                pe.sem_inc(s["hot_used"], 1)
                make_q(0)
                score(0)
                pe.wait_ge(s["sim_saved"], 1)
                for c in range(1, NC):
                    make_q(c)
                pe.wait_ge(s["q_saved"], 4 * NC)
                turn(0)
                with pe.Fori(0, NT - 1) as t:
                    score(t + 1)
                    weigh(t, 0, early)
                    turn(t + 1)
                    weigh(t, early, late, count_edges=True)
                M(psH, zero[:, :], zero[:, 0:LOW], start=False, stop=True).then_inc(s["hist"], 1)
                weigh(NT - 1, 0, rounds)

            @block.scalar
            def _(act):
                C = lambda out, in_: nc.scalar.activation(out, in_, ACT.Copy)

                def save_q(c):
                    for j in range(4):
                        act.wait_ge(s["q"], c * 4 + j + 1)
                        C(chunk(qT[:, j, :], c), psQ[:, j, 0:CH]).then_inc(s["q_saved"], 1)
                    act.wait_ge(s["q_saved"], c * 4 + 4)

                def score(t):
                    C(qb[:, :, :], qT[:, :, bass.ds(t * TT, TT)]).then_inc(s["q_tile"], 1)
                    act.wait_ge(s["sim"], t + 1)
                    C(sim[:, :, :].rearrange("n (j r) k -> n r j k", r=4), psS[:, :, 0:4 * NKEY].rearrange("n r (j k) -> n r j k", j=4)).then_inc(s["sim_saved"], 1)

                def soften(t):
                    act.wait_ge(s["shifted"], t + 1)
                    nc.scalar.activation(wt[:, :, :], wt[:, :, :], ACT.Exp).then_inc(s["exped"], 1)
                    act.wait_ge(s["turned"], t + 1)
                    C(idxT[:, bass.ds(t * TT, TT)], psT[:, 0, 0:TT]).then_inc(s["index_saved"], 1)

                def stage_index(t, g, a):
                    C(idx[a][:, :], idxT[:, bass.ds(gather_at(t, g) + a * HG, HG)]).then_inc(s["staged"], 1)

                def gathers(t, first, steps, tiles):
                    wait_alone(act, s["index_saved"], tiles, s["passed"])
                    with act.Fori(0, steps) as k_:
                        g = k_ + first
                        for a in range(2):
                            act.wait_ge(s["weighed"], (t * rounds + g) * 2 + (a + 1))
                            stage_index(t, g + 1, a)
                            C(kv[:, :, bass.ds(gather_at(t, g) + a * HG, HG)], psG[a][:, 0:HG * H].rearrange("p (n h) -> p h n", h=H)).then_inc(s["kv_saved"], 1)

                save_q(0)
                score(0)
                for c in range(1, NC):
                    save_q(c)
                soften(0)
                act.wait_ge(s["index_saved"], 1)
                act.wait_ge(s["consts"], 1)
                for a in range(2):
                    stage_index(0, 0, a)
                with act.Fori(0, NT - 1) as t:
                    score(t + 1)
                    gathers(t, 0, early, t + 1)
                    soften(t + 1)
                    gathers(t, early, rounds - early, t + 2)
                gathers(NT - 1, 0, rounds, NT)

            @block.vector
            def _(dve):
                V = nc.vector
                dve.wait_ge(s["consts"], 1)

                def score(t):
                    links = [0]

                    def link(ins):
                        links[0] += 1
                        ins.then_inc(s["chain"], 1)
                        wait_alone(dve, s["chain"], t * LINKS + links[0], s["passed"])

                    def top16(n, val, ind, src, src2):
                        for f in range(n):
                            last = V.max(val[:, f, 0:8], src[:, f, :])
                        link(last)
                        for f in range(n):
                            V.max_index(ind[:, f, 0:8], val[:, f, 0:8], src[:, f, :])
                        for f in range(n):
                            last = V.match_replace(src2[:, f, :], val[:, f, 0:8], src[:, f, :], NEG)
                        link(last)
                        for f in range(n):
                            last = V.max(val[:, f, 8:16], src2[:, f, :])
                        link(last)
                        for f in range(n):
                            last = V.max_index(ind[:, f, 8:16], val[:, f, 8:16], src2[:, f, :])
                        link(last)

                    wait_alone(dve, s["sim_saved"], t + 1, s["passed"])
                    top16(G2, top, topi, sim, sim2)
                    link(V.tensor_copy(topf[:, :, :], topi[:, :, :]))
                    for hd in range(H):
                        last = V.tensor_tensor(sums[:, hd, :].rearrange("n (a b) -> n a b", a=PK), top[:, hd, :].unsqueeze(2).to_broadcast([TT, PK, PK]),
                                               top[:, H + hd, :].unsqueeze(1).to_broadcast([TT, PK, PK]), ALU.add)
                    link(last)
                    top16(H, best, besti, sums, sums2)
                    flat = besti[:, :, :].rearrange("n h k -> n (h k)")
                    V.tensor_scalar(part_u[:, 0, :], flat, 4, None, ALU.logical_shift_right)
                    link(V.tensor_scalar(part_u[:, 1, :], flat, PK - 1, None, ALU.bitwise_and))
                    link(V.tensor_copy(part[:, :, :, :].rearrange("n a h k -> n a (h k)"), part_u[:, :, :]))
                    for a in range(2):
                        eq = sums[:, :, :].rearrange("n h (k m) -> n h k m", k=PK)
                        link(V.tensor_tensor(eq, part[:, a, :, :].unsqueeze(3).to_broadcast(full), count[:, :].unsqueeze(1).unsqueeze(1).to_broadcast(full), ALU.is_equal))
                        link(V.tensor_tensor(eq, eq, topf[:, a * H:(a + 1) * H, :].unsqueeze(2).to_broadcast(full), ALU.mult))
                        link(V.tensor_reduce(half_i[:, a, :, :], eq, X, ALU.add))
                    if not isinstance(t, int) or t:
                        dve.wait_ge(s["turned"], t)
                    link(V.scalar_tensor_tensor(row[:, :, :], half_i[:, 1, :, :], float(NKEY), half_i[:, 0, :, :], ALU.mult, ALU.add))
                    V.tensor_tensor(row[:, :, :], row[:, :, :], head0[:, :, :], ALU.add)
                    V.tensor_tensor(wt[:, :, :], best[:, :, :], best[:, :, 0:1].to_broadcast([TT, H, PK]), ALU.subtract).then_inc(s["shifted"], 1)
                    dve.wait_ge(s["exped"], t + 1)
                    link(V.tensor_reduce(st[:, 0, :], wt[:, :, :], X, ALU.add))
                    link(V.reciprocal(st[:, 1, :], st[:, 0, :]))
                    V.tensor_tensor(wt[:, :, :], wt[:, :, :], st[:, 1, :].unsqueeze(2).to_broadcast([TT, H, PK]), ALU.mult).then_inc(s["rows_ready"], 1)
                    dve.wait_ge(s["index_saved"], t + 1)
                    V.tensor_tensor(spread[:, bass.ds(t * TT, TT), :], psT[:, 1, 0:TT].unsqueeze(2).to_broadcast([128, TT, H]),
                                    own[:, :].unsqueeze(1).to_broadcast([128, TT, H]), ALU.mult).then_inc(s["spread"], 1)
                    assert links[0] <= LINKS, links
                    while links[0] < LINKS:
                        link(V.tensor_copy(st[:, 0, 0:1], st[:, 1, 0:1]))

                def digits_and_keys():
                    links = [0]

                    def link(ins):
                        links[0] += 1
                        ins.then_inc(s["digit_chain"], 1)
                        dve.wait_ge(s["digit_chain"], links[0])

                    hi, lo = digits[:, 0, 0:L], digits[:, 1, 0:L]
                    V.memset(digits[:, :, L:], 2.0 * LOW)
                    dve.wait_ge(s["edges_loaded"], 32)
                    link(V.tensor_copy(srcf[:, :], src[:, :]))
                    link(V.tensor_copy(key[:, :], dst[:, :]))
                    link(V.tensor_scalar(src[:, :], dst[:, :], 5, None, ALU.logical_shift_right))
                    link(V.tensor_copy(hi, src[:, :]))
                    link(V.tensor_scalar(src[:, :], dst[:, :], LOW - 1, None, ALU.bitwise_and))
                    link(V.tensor_copy(lo, src[:, :]))
                    true = src[:, :].bitcast(F32)
                    link(V.tensor_scalar(true, srcf[:, :], float(T - 1), None, ALU.is_lt))
                    link(V.scalar_tensor_tensor(lo, true, 2.0 * LOW, lo, ALU.mult, ALU.add))
                    link(V.scalar_tensor_tensor(true, key[:, :], float(T), true, ALU.is_lt, ALU.mult))
                    link(V.scalar_tensor_tensor(key[:, :], key[:, :], float(KEY), srcf[:, :], ALU.mult, ALU.add))
                    link(V.scalar_tensor_tensor(key[:, :], key[:, :], 1.0, true, ALU.add, ALU.mult))

                score(0)
                digits_and_keys()
                with dve.Fori(0, NT - 1) as t:
                    score(t + 1)
                    with dve.Fori(0, late) as k:
                        wait_alone(dve, s["hot_used"], t * late + k + 1, s["passed"])
                        cols = lambda d: digits[:, d, bass.ds((t * late + k) * LC, LC)]
                        for d, (to, n) in enumerate(((hot_hi, HIGH), (hot_lo, LOW))):
                            last = V.tensor_tensor(to[:, :, :], cols(d).unsqueeze(2).to_broadcast([128, LC, n]),
                                                   digit[:, 0:n].unsqueeze(1).to_broadcast([128, LC, n]), ALU.is_equal)
                        last.then_inc(s["hot"], 1)
                dve.wait_ge(s["hist"], 1)
                V.tensor_copy(hist[:, :], psH).then_inc(s["hist_saved"], 1)



def gate_values(nc, tag, x, h, wg, bg, gate):
    with stage(nc, tag, "made", "saved", "added") as (s, sb, ps):
        made = [ps(f"g{k}", [128, 512]) for k in range(4)]
        with nc.Block() as block:
            @block.tensor
            def _(pe):
                for n in range(2 * NC):
                    if n >= 4:
                        pe.wait_ge(s["saved"], n - 3)
                    nc.tensor.matmul(made[n % 4][:, 0:CH], wg[:, n // NC, :], chunk(x, n % NC), start=True, stop=True).then_inc(s["made"], 1)

            @block.scalar
            def _(act):
                for n in range(2 * NC):
                    act.wait_ge(s["made"], n + 1)
                    nc.scalar.activation(chunk(gate[:, n // NC, :], n % NC), made[n % 4][:, 0:CH], ACT.Sigmoid, bias=bg[:, n // NC:n // NC + 1]).then_inc(s["saved"], 1)

            @block.vector
            def _(dve):
                nc.vector.tensor_tensor(h[:, :], h[:, :], x[:, :], ALU.add).then_inc(s["added"], 1)


def silu_experts(nc, tag, x, h, rest, wT, pick, w13, w2, w2_rest):
    experts, last = w2.shape[1], w2_rest.shape[0]
    place = [(i, e) for i in range(NC) for e in range(experts)]
    with stage(nc, tag, "weight", "weighted", "x_copied", "up", "silu", "product", "sum", "rested", "added") as (s, sb, ps):
        xx = sb("xx", [2 * D, 2, CH])
        act_sb = sb("act", [D, 2, 3, CH])
        hw = sb("hw", [2 * D, 2, 2, CH])
        p = [ps(f"p{k}", [2 * D, 3, 512]) for k in range(2)]
        pw = ps("pw", [D, 512])
        acc = ps("acc", [D, 512])
        with nc.Block() as block:
            @block.tensor
            def _(pe):
                M = nc.tensor.matmul

                def weigh(n):
                    i, e = place[n]
                    if n:
                        pe.wait_ge(s["weighted"], n)
                    M(pw[:, 0:CH], pick[0:experts, e, 0:D], chunk(wT, i), start=True, stop=True).then_inc(s["weight"], 1)

                def up(n):
                    i, e = place[n]
                    pe.wait_ge(s["x_copied"], min(2 * i + n % 2 + 1, 2 * NC))
                    pe.wait_ge(s["weighted"], n + 1)
                    if n >= 2:
                        pe.wait_ge(s["product"], 2 * n - 2)
                    for k in range(3):
                        mm = M(p[n % 2][:, k, 0:CH], w13[:, e, k, :], xx[:, n % 2, :], start=True, stop=True)
                    mm.then_inc(s["up"], 1)

                def down(n):
                    i, e = place[n]
                    pe.wait_ge(s["product"], 2 * n + 2)
                    if e == 0 and i:
                        pe.wait_ge(s["added"], i)
                    M(acc[:, 0:CH], w2[:, e, :], hw[:, n % 2, 0, :], start=(e == 0), stop=False)
                    mm = M(acc[:, 0:CH], w2_rest[:, e, :], hw[0:last, n % 2, 1, :], start=False, stop=(e == experts - 1))
                    if e == experts - 1:
                        mm.then_inc(s["sum"], 1)

                weigh(0)
                for n in range(len(place)):
                    if n + 1 < len(place):
                        weigh(n + 1)
                    up(n)
                    if n:
                        down(n - 1)
                down(len(place) - 1)

            @block.scalar
            def _(act):
                for n in range(len(place)):
                    act.wait_ge(s["up"], n + 1)
                    if n >= 2:
                        act.wait_ge(s["product"], 2 * n - 2)
                    nc.scalar.activation(act_sb[:, n % 2, :, :], p[n % 2][0:D, :, 0:CH], ACT.Silu).then_inc(s["silu"], 1)

            @block.vector
            def _(dve):
                V = nc.vector
                V.tensor_tensor(h[:, :], h[:, :], rest[:, :], ALU.add).then_inc(s["rested"], 1)

                def weight(n):
                    i, e = place[n]
                    if n >= 2:
                        dve.wait_ge(s["up"], n - 1)
                    if e < 2:
                        V.tensor_copy(xx[0:D, n % 2, :], chunk(x, i)).then_inc(s["x_copied"], 1)
                    dve.wait_ge(s["weight"], n + 1)
                    V.tensor_tensor(xx[D:2 * D, n % 2, :], chunk(x, i), pw[:, 0:CH], ALU.mult).then_inc(s["weighted"], 1)

                weight(0)
                for n, (i, e) in enumerate(place):
                    if n + 1 < len(place):
                        weight(n + 1)
                    dve.wait_ge(s["silu"], n + 1)
                    linear = p[n % 2][D:2 * D, :, 0:CH]
                    V.tensor_tensor(hw[0:D, n % 2, :, :], act_sb[:, n % 2, 0:2, :], linear[:, 0:2, :], ALU.mult).then_inc(s["product"], 1)
                    V.tensor_tensor(hw[D:2 * D, n % 2, 0, :], act_sb[:, n % 2, 2, :], linear[:, 2, :], ALU.mult).then_inc(s["product"], 1)
                    if e == experts - 1:
                        dve.wait_ge(s["sum"], i + 1)
                        if i == 0:
                            dve.wait_ge(s["rested"], 1)
                        V.tensor_tensor(chunk(h, i), chunk(h, i), acc[:, 0:CH], ALU.add).then_inc(s["added"], 1)


def gelu_experts(nc, tag, x, h, wT, pick, w1, b1, w2, b2, experts, hid):
    place = [(i, e) for i in range(NC) for e in range(experts)]
    with stage(nc, tag, "weight", "up", "gelu", "weighted", "sum", "added") as (s, sb, ps):
        act_sb = sb("act", [hid, 2, CH])
        hw = sb("hw", [hid, 2, CH])
        p1 = [ps(f"p1{k}", [hid, 512]) for k in range(2)]
        pw = [ps(f"pw{k}", [hid, 512]) for k in range(2)]
        acc = ps("acc", [D, 512])
        with nc.Block() as block:
            @block.tensor
            def _(pe):
                M = nc.tensor.matmul

                def up(n):
                    i, e = place[n]
                    if n >= 2:
                        pe.wait_ge(s["weighted"], n - 1)
                    M(pw[n % 2][:, 0:CH], pick[0:experts, e, 0:hid], chunk(wT, i), start=True, stop=True).then_inc(s["weight"], 1)
                    M(p1[n % 2][:, 0:CH], w1[:, e, :], chunk(x, i), start=True, stop=True).then_inc(s["up"], 1)

                up(0)
                for n, (i, e) in enumerate(place):
                    if n + 1 < len(place):
                        up(n + 1)
                    if e == 0:
                        if i:
                            pe.wait_ge(s["added"], i)
                        M(acc[:, 0:CH], b2, chunk(wT, i), start=True, stop=False)
                    pe.wait_ge(s["weighted"], n + 1)
                    mm = M(acc[:, 0:CH], w2[:, e, :], hw[:, n % 2, :], start=False, stop=(e == experts - 1))
                    if e == experts - 1:
                        mm.then_inc(s["sum"], 1)

            @block.scalar
            def _(act):
                for n, (i, e) in enumerate(place):
                    act.wait_ge(s["up"], n + 1)
                    if n >= 2:
                        act.wait_ge(s["weighted"], n - 1)
                    nc.scalar.activation(act_sb[:, n % 2, :], p1[n % 2][:, 0:CH], ACT.Gelu, bias=b1[:, e:e + 1]).then_inc(s["gelu"], 1)

            @block.vector
            def _(dve):
                for n, (i, e) in enumerate(place):
                    dve.wait_ge(s["gelu"], n + 1)
                    dve.wait_ge(s["weight"], n + 1)
                    nc.vector.tensor_tensor(hw[:, n % 2, :], act_sb[:, n % 2, :], pw[n % 2][:, 0:CH], ALU.mult).then_inc(s["weighted"], 1)
                    if e == experts - 1:
                        dve.wait_ge(s["sum"], i + 1)
                        nc.vector.tensor_tensor(chunk(h, i), chunk(h, i), acc[:, 0:CH], ALU.add).then_inc(s["added"], 1)


ROUND = 8
ROUNDS = 3


def edge_counts(nc, tag, key, hist, ident, countT, absent):
    L = key.shape[1]
    with stage(nc, tag, "chain", "iota", "zeros", "hist_out", "hist_in", "rchain",
               "round_hot", "counted", "added", "flag", "flag_int", "loops", "turned", "made", "passed") as (s, sb, ps):
        place = sb("place", [128, T])
        hots = [sb(f"hot{k}", [128, 2, ROUND, T], BF16) for k in range(2)]
        top = sb("top", [128, ROUND])
        top_u = sb("top_u", [128, 3, ROUND], U32)
        top_f = sb("top_f", [128, 2, ROUND])
        flag = sb("flag", [128, 1])
        flag_i = sb("flag_i", [128, 1], I32)
        hist_dram = nc.dram_tensor(f"{tag}_hist_dram", (HIGH * LOW,), F32).ap()
        psC = ps("c", [128, 2, 4, 512])
        V = nc.vector
        with nc.Block() as block:
            @block.sync
            def _(sp):
                sp.dma_start(hist_dram.rearrange("(a b) -> a b", b=LOW), hist[:, :]).then_inc(s["hist_out"], 16)
                sp.wait_ge(s["hist_out"], 16)
                sp.wait_ge(s["zeros"], 1)
                sp.dma_start(countT[TT - 1:TT, NT - 1, :], hist_dram[0:T].rearrange("(a n) -> a n", a=1)).then_inc(s["hist_in"], 16)

            @block.gpsimd
            def _(pool):
                P = nc.gpsimd
                P.iota(place[:, :], [[1, T]], base=0, channel_multiplier=0, allow_small_or_imprecise_dtypes=True).then_inc(s["iota"], 1)
                P.memset(countT[:, :, :], 0.0).then_inc(s["zeros"], 1)
                pool.wait_ge(s["flag"], 1)
                P.partition_all_reduce(flag[:, :], flag[:, :], 128, bass.bass_isa.ReduceOp.max).then_inc(s["flag"], 1)

            @block.tensor
            def _(pe):
                M = nc.tensor.matmul
                def round_(r, hot):
                    pe.wait_ge(s["round_hot"], r + 1)
                    for t in range(NT):
                        if not isinstance(r, int) or r * NT + t >= 2:
                            pe.wait_ge(s["added"], r * NT + t - 1)
                        for c in range(NC):
                            for k in range(ROUND):
                                mm = M(psC[0:TT, t % 2, c, 0:CH], hot[:, 0, k, t * TT:(t + 1) * TT], hot[:, 1, k, c * CH:(c + 1) * CH],
                                       start=(k == 0), stop=(k == ROUND - 1))
                        mm.then_inc(s["counted"], 1)

                for r in range(ROUNDS):
                    round_(r, hots[r % 2])
                pe.wait_ge(s["flag_int"], 1)
                left = pe.value_load(flag_i[0:1, 0:1], min_val=0, max_val=1)
                with pe.If(left > 0):
                    with pe.Fori(ROUNDS, L // ROUND) as r:
                        round_(r, hots[0])
                for t in range(NT):
                    pe.wait_ge(s["loops"], NT)
                    if t >= 2:
                        pe.wait_ge(s["made"], t - 1)
                    for o in range(NT):
                        mm = nc.tensor.transpose(psC[0:TT, t % 2, o // 4, (o % 4) * TT:(o % 4 + 1) * TT], countT[:, o, t * TT:(t + 1) * TT], ident[0:TT, 0:TT])
                    mm.then_inc(s["turned"], 1)

            @block.vector
            def _(dve):
                links = [0]

                def link(ins):
                    links[0] += 1
                    ins.then_inc(s["chain"], 1)
                    dve.wait_ge(s["chain"], links[0])

                dve.wait_ge(s["iota"], 1)
                RLINKS = 5

                def rlink(r, n, ins):
                    ins.then_inc(s["rchain"], 1)
                    wait_alone(dve, s["rchain"], r * RLINKS + n, s["passed"])

                def take(r):
                    rlink(r, 1, V.max(top[:, :], key[:, :]))
                    V.match_replace(key[:, :], top[:, :], key[:, :], 0.0)

                def split(r):
                    rlink(r, 2, V.tensor_copy(top_u[:, 0, :], top[:, :]))
                    V.tensor_scalar(top_u[:, 1, :], top_u[:, 0, :], KEY - 1, None, ALU.bitwise_and)
                    rlink(r, 3, V.tensor_scalar(top_u[:, 2, :], top_u[:, 0, :], 11, None, ALU.logical_shift_right))
                    rlink(r, 4, V.tensor_copy(top_f[:, :, :], top_u[:, 1:3, :]))
                    rlink(r, 5, V.tensor_scalar(top_f[:, 0, :], top_f[:, 0, :], -1.0, None, ALU.add))

                def spread(k, hot):
                    V.tensor_scalar(hot[:, 0, k, :], place[:, :], top_f[:, 0, k:k + 1], None, ALU.is_equal)
                    last = V.tensor_scalar(hot[:, 1, k, :], place[:, :], top_f[:, 1, k:k + 1], None, ALU.is_equal)
                    if k == ROUND - 1:
                        last.then_inc(s["round_hot"], 1)

                def prepare(r, hot):
                    take(r)
                    split(r)
                    for k in range(ROUND):
                        spread(k, hot)

                def add(r, t):
                    dve.wait_ge(s["counted"], r * NT + (t + 1))
                    V.tensor_tensor(countT[:, t, :].rearrange("p (c n) -> p c n", c=NC), countT[:, t, :].rearrange("p (c n) -> p c n", c=NC),
                                    psC[0:TT, t % 2, :, 0:CH], ALU.add).then_inc(s["added"], 1)

                prepare(0, hots[0])
                dve.wait_ge(s["zeros"], 1)
                dve.wait_ge(s["hist_in"], 16)
                for r in range(ROUNDS):
                    for t in range(NT):
                        add(r, t)
                        if r + 1 < ROUNDS:
                            if t == 0:
                                take(r + 1)
                            elif t == 1:
                                split(r + 1)
                            else:
                                spread(t - 2, hots[(r + 1) % 2])
                link(V.tensor_reduce(flag[:, :], key[:, :], X, ALU.max))
                V.tensor_scalar(flag[:, :], flag[:, :], 1.0, None, ALU.min).then_inc(s["flag"], 1)
                dve.wait_ge(s["flag_int"], 1)
                left = dve.value_load(flag_i[0:1, 0:1], min_val=0, max_val=1)
                with dve.If(left > 0):
                    with dve.Fori(ROUNDS, L // ROUND) as r:
                        prepare(r, hots[0])
                        for t in range(NT):
                            add(r, t)
                        wait_alone(dve, s["added"], r * NT + NT, s["passed"])
                dve.wait_ge(s["added"], ROUNDS * NT)
                for t in range(NT):
                    V.tensor_tensor(countT[:, t, t * TT:(t + 1) * TT], countT[:, t, t * TT:(t + 1) * TT], ident[0:TT, 0:TT], ALU.add).then_inc(s["loops"], 1)
                for t in range(NT):
                    dve.wait_ge(s["turned"], t + 1)
                    for lo, hi in ((0, 8), (8, NT)):
                        last = V.tensor_scalar(absent[:, t, lo * TT:hi * TT].rearrange("p (c n) -> p c n", n=min(4, hi - lo) * TT),
                                               psC[0:TT, t % 2, lo // 4:(hi + 3) // 4, 0:min(4, hi - lo) * TT], 0.5, NEG, ALU.is_lt, ALU.mult)
                    last.then_inc(s["made"], 1)

            @block.scalar
            def _(act):
                act.wait_ge(s["flag"], 2)
                nc.scalar.activation(flag_i[:, :], flag[:, :], ACT.Copy).then_inc(s["flag_int"], 1)


def graph_scores(nc, tag, x, wgat, att, att_col, rows, ident, pick, countT, absent, scores):
    K, E = 4, 4
    W = 32
    two = 2
    with stage(nc, tag, "zeros", "ones", "sel", "made", "saved", "chain", "spread", "spread_saved", "maxed", "parts", "turned", "turned_saved",
               "wide", "wide_saved", "copied", "low", "high", "below", "exped", "edges", "summed", "agg", "agg_saved",
               "back", "root", "eps", "passed") as (s, sb, ps):
        hT = sb("hT", [K * E, T])
        hp = sb("hp", [TT, NT, K, W])
        hb = sb("hb", [TT, two, K, W])
        sel = sb("sel", [K * E, K, TT])
        zero = sb("zero", [TT, CH])
        tmp = sb("tmp", [TT, NT, K, E])
        a = sb("a", [TT, 2, NT, K])
        junk = sb("junk", [TT, two, T])
        M = sb("m", [TT, NT, K])
        U = sb("u", [TT, NT, K, 2])
        UT = sb("ut", [2, T])
        UB = sb("ub", [TT, 2 * K, T])
        z = sb("z", [TT, K, T])
        aggT = sb("aggt", [128, T])
        g = sb("g", [N, B, K * E])
        sq = sb("sq", [N, B, K * E])
        st = sb("st", [N, 4, B])
        den = sb("den", [N, B, K])
        eps_col = sb("eps", [N, 1])
        psA = ps("banks", [128, 2, NC, 512])
        by_chunk = lambda t: t.rearrange("p (c n) -> p c n", c=NC)
        V = nc.vector
        STEP = two * K
        SLOTS = K

        def tile_of(t, n):
            if isinstance(n, int):
                return t[:, n]
            dims = " ".join("bcd"[:len(t.shape) - 2])
            return t[:, bass.ds(n, 1)].rearrange(f"p a {dims} -> p (a {dims[0]}) {dims[1:]}")

        def sweeps(engine, sweep):
            sweep(0, True, False)
            with engine.Fori(1, NT // two - 1) as i:
                sweep(i, False, False)
            sweep(NT // two - 1, False, True)

        with nc.Block() as block:
            @block.gpsimd
            def _(pool):
                P = nc.gpsimd
                P.memset(sel[:, :, :], 1.0).then_inc(s["ones"], 1)
                P.memset(zero[:, :], 0.0).then_inc(s["zeros"], 1)
                P.memset(eps_col[:, :], 1e-5).then_inc(s["eps"], 1)
                P.memset(hp[:, :, :, :], 0.0).then_inc(s["ones"], 1)
                pool.wait_ge(s["ones"], 1)
                P.affine_select(out=sel[:, :, :], in_=sel[:, :, :], compare_op=ALU.is_ge, fill=0.0, base=0,
                                pattern=[[-E, K], [0, TT]], channel_multiplier=1).then_inc(s["ones"], 1)
                pool.wait_ge(s["ones"], 3)
                P.affine_select(out=sel[:, :, :], in_=sel[:, :, :], compare_op=ALU.is_ge, fill=0.0, base=E - 1,
                                pattern=[[E, K], [0, TT]], channel_multiplier=-1).then_inc(s["ones"], 1)
                P.memset(hp[:, :, :, E:E + 1], 1.0).then_inc(s["ones"], 1)
                pool.wait_ge(s["ones"], 5)
                P.tensor_scalar(sel[:, :, :], sel[:, :, :], att_col, None, ALU.mult).then_inc(s["sel"], 1)
                pool.wait_ge(s["parts"], 1)

                def take(t, u):
                    P.tensor_copy(hb[:, u, :, :], tile_of(hp, t)).then_inc(s["copied"], 1)

                def sweep(i, first, last):
                    for n in range(STEP):
                        wait_alone(pool, s["high"], i * STEP + n + 1, s["passed"])
                        P.tensor_scalar(z[:, n % K, :], z[:, n % K, :], 0.0, None, ALU.min).then_inc(s["below"], 1)
                        if n == 0 and not first:
                            wait_alone(pool, s["summed"], i * STEP + SLOTS, s["passed"])
                            take(i * two + 1, 1)
                        if n == K and not last:
                            wait_alone(pool, s["summed"], i * STEP + K + SLOTS, s["passed"])
                            take(i * two + 2, 0)

                take(0, 0)
                take(1, 1)
                sweeps(pool, sweep)

            @block.tensor
            def _(pe):
                MM = nc.tensor.matmul
                for c in range(NC):
                    mm = MM(psA[0:K * E, 0, c, 0:CH], wgat, chunk(x, c), start=True, stop=True)
                mm.then_inc(s["made"], 1)
                for t in range(NT):
                    mm = MM(psA[0:TT, 1, 0, t * K * E:(t + 1) * K * E], x[:, t * TT:(t + 1) * TT], wgat, start=True, stop=True)
                mm.then_inc(s["made"], 1)
                pe.wait_ge(s["saved"], 2)
                pe.wait_ge(s["sel"], 1)
                for k in range(K):
                    if k >= 2:
                        pe.wait_ge(s["spread_saved"], k - 1)
                    for c in range(NC):
                        mm = MM(psA[0:TT, k % 2, c, 0:CH], sel[:, k, :], chunk(hT, c), start=True, stop=True)
                    mm.then_inc(s["spread"], 1)
                pe.wait_ge(s["spread_saved"], K)
                for k in range(K):
                    pe.wait_ge(s["parts"], k + 1)
                    if k:
                        pe.wait_ge(s["wide_saved"], 2 * k)
                    for t in range(NT):
                        mm = nc.tensor.transpose(psA[0:2, 0, t // 4, (t % 4) * TT:(t % 4 + 1) * TT], U[:, t, k, :], ident[0:TT, 0:TT])
                    mm.then_inc(s["turned"], 1)
                    pe.wait_ge(s["turned_saved"], 2 * k + 2)
                    for e in range(2):
                        for c in range(NC):
                            mm = MM(psA[0:TT, 1 - e, c, 0:CH], pick[0:2, e, 0:TT], chunk(UT, c), start=True, stop=True)
                        mm.then_inc(s["wide"], 1)
                pe.wait_ge(s["wide_saved"], 2 * K)
                for c in range(NC):
                    MM(psA[:, 0, c, 0:CH], zero[:, 0:128], zero[:, :], start=True, stop=False)
                pe.sem_inc(s["summed"], SLOTS)

                def sweep(i, first, last):
                    for n in range(STEP):
                        u, k = divmod(n, K)
                        pe.wait_ge(s["edges"], i * STEP + (n + 1))
                        for c in range(NC):
                            mm = MM(psA[k * W:(k + 1) * W, 0, c, 0:CH], hb[:, u, k, :], z[:, k, c * CH:(c + 1) * CH],
                                    start=False, stop=False, skip_group_check=True, tile_position=(0, k * W))
                        mm.then_inc(s["summed"], 1)

                sweeps(pe, sweep)
                for c in range(NC):
                    mm = MM(psA[:, 0, c, 0:CH], zero[:, 0:128], zero[:, :], start=False, stop=True)
                mm.then_inc(s["agg"], 1)
                pe.wait_ge(s["agg_saved"], 1)
                for b in range(B):
                    mm = nc.tensor.transpose(psA[0:N, 1, b // IPC, (b % IPC) * 128:(b % IPC + 1) * 128], aggT[:, b * N:(b + 1) * N], ident[:, :])
                mm.then_inc(s["back"], 1)

            @block.scalar
            def _(act):
                act.wait_ge(s["made"], 1)
                nc.scalar.copy(by_chunk(hT[:, :]), psA[0:K * E, 0, :, 0:CH]).then_inc(s["saved"], 1)
                for k in range(K):
                    act.wait_ge(s["spread"], k + 1)
                    nc.scalar.copy(by_chunk(z[:, k, :]), psA[0:TT, k % 2, :, 0:CH]).then_inc(s["spread_saved"], 1)
                for k in range(K):
                    act.wait_ge(s["turned"], k + 1)
                    nc.scalar.copy(UT[:, 0:8 * TT].rearrange("p (c n) -> p c n", c=2), psA[0:2, 0, 0:2, 0:4 * TT]).then_inc(s["turned_saved"], 1)
                    nc.scalar.copy(UT[:, 8 * TT:T], psA[0:2, 0, 2, 0:2 * TT]).then_inc(s["turned_saved"], 1)
                    for e in range(2):
                        act.wait_ge(s["wide"], 2 * k + e + 1)
                        nc.scalar.copy(by_chunk(UB[:, e * K + k, :]), psA[0:TT, 1 - e, :, 0:CH]).then_inc(s["wide_saved"], 1)
                act.wait_ge(s["wide_saved"], 2 * K)

                def lower(i, n):
                    u, k = n // K % two, n % K
                    if k == 0:
                        act.wait_ge(s["copied"], i * two + (n // K + 1))
                    act.wait_ge(s["summed"], i * STEP + (n + 1))
                    nc.scalar.activation(z[:, k, :], UB[:, K + k, :], ACT.Identity, bias=hb[:, u, k, E + 2:E + 3]).then_inc(s["low"], 1)

                def sweep(i, first, last):
                    for n in range(STEP):
                        act.wait_ge(s["below"], i * STEP + (n + 1))
                        nc.scalar.activation(z[:, n % K, :], z[:, n % K, :], ACT.Exp).then_inc(s["exped"], 1)
                        if not last or n + 3 < STEP:
                            lower(i, n + 3)

                for n in range(3):
                    lower(0, n)
                sweeps(act, sweep)
                act.wait_ge(s["agg"], 1)
                nc.scalar.copy(by_chunk(aggT[:, :]), psA[:, 0, :, 0:CH]).then_inc(s["agg_saved"], 1)
                act.wait_ge(s["eps"], 1)
                act.wait_ge(s["back"], 2)
                nc.scalar.activation(st[:, 2, :], st[:, 1, :], ACT.Sqrt, bias=eps_col[:, 0:1], scale=1.0 / (K * E)).then_inc(s["root"], 1)

            @block.vector
            def _(dve):
                links = [0]

                def link(ins):
                    links[0] += 1
                    ins.then_inc(s["chain"], 1)
                    dve.wait_ge(s["chain"], links[0])

                heads_of = lambda t: t.rearrange("p t (k e) -> p t k e", k=K)
                dve.wait_ge(s["ones"], 5)
                dve.wait_ge(s["made"], 2)
                made = psA[0:TT, 1, 0, 0:NT * K * E].rearrange("p (t k e) -> p t k e", k=K, e=E)
                link(V.tensor_copy(hp[:, :, :, 0:E], made))
                for side in range(2):
                    row = att[:, side, :].rearrange("p (k e) -> p k e", k=K).unsqueeze(1).to_broadcast([TT, NT, K, E])
                    link(V.tensor_tensor(tmp[:, :, :, :], hp[:, :, :, 0:E], row, ALU.mult))
                    link(V.tensor_reduce(a[:, side, :, :], tmp[:, :, :, :], X, ALU.add))
                V.tensor_scalar(hp[:, :, :, E + 1], a[:, 0, :, :], 1.0, None, ALU.mult)
                V.tensor_scalar(hp[:, :, :, E + 2], a[:, 0, :, :], 0.2, None, ALU.mult).then_inc(s["saved"], 1)
                for k in range(K):
                    dve.wait_ge(s["spread_saved"], k + 1)
                    for t in range(NT):
                        n = k * NT + t
                        if n >= two:
                            dve.wait_ge(s["maxed"], n - 1)
                        V.tensor_tensor_reduce(out=junk[:, n % two, :], in0=absent[:, t, :], in1=z[:, k, :],
                                               scale=1.0, scalar=-3.0e38, op0=ALU.add, op1=ALU.max, accum_out=M[:, t, k:k + 1]).then_inc(s["maxed"], 1)
                    dve.wait_ge(s["maxed"], (k + 1) * NT)
                    most, ad = M[:, :, k], a[:, 1, :, k]
                    link(V.tensor_tensor(most, most, ad, ALU.add))
                    link(V.scalar_tensor_tensor(most, most, 0.2, most, ALU.mult, ALU.max))
                    V.tensor_tensor(U[:, :, k, 0], ad, most, ALU.subtract)
                    V.scalar_tensor_tensor(U[:, :, k, 1], ad, 0.2, most, ALU.mult, ALU.subtract).then_inc(s["parts"], 1)
                dve.wait_ge(s["wide_saved"], 2 * K)

                def top(i, n):
                    u, k = n // K % two, n % K
                    if k == 0:
                        dve.wait_ge(s["copied"], i * two + (n // K + 1))
                    dve.wait_ge(s["low"], i * STEP + (n + 1))
                    V.scalar_tensor_tensor(z[:, k, :], UB[:, k, :], hb[:, u, k, E + 1:E + 2], z[:, k, :], ALU.add, ALU.max).then_inc(s["high"], 1)

                def sweep(i, first, last):
                    for n in range(STEP):
                        u, k = divmod(n, K)
                        dve.wait_ge(s["exped"], i * STEP + (n + 1))
                        V.tensor_tensor(z[:, k, :], z[:, k, :], tile_of(countT, i * two + u), ALU.mult).then_inc(s["edges"], 1)
                        if not last or n + 2 < STEP:
                            top(i, n + 2)

                for n in range(2):
                    top(0, n)
                sweeps(dve, sweep)
                dve.wait_ge(s["back"], 1)
                agg = psA[0:N, 1, :, :].rearrange("n c (i k w) -> n (c i) k w", k=K, w=W)
                g4 = heads_of(g[:, :, :])
                wide = lambda t: t.unsqueeze(2).to_broadcast([N, B, K * E])
                all_of = lambda r: rows[:, r:r + 1, :].to_broadcast([N, B, K * E])
                link(V.tensor_scalar(den[:, :, :], agg[:, :, :, E], 1e-16, None, ALU.add))
                link(V.reciprocal(den[:, :, :], den[:, :, :]))
                link(V.tensor_tensor(g4, agg[:, :, :, 0:E], den[:, :, :].unsqueeze(3).to_broadcast([N, B, K, E]), ALU.mult))
                link(V.tensor_tensor(g[:, :, :], g[:, :, :], all_of(0), ALU.add))
                link(V.tensor_reduce(st[:, 0, :], g[:, :, :], X, ALU.add))
                link(V.tensor_scalar(st[:, 0, :], st[:, 0, :], 1.0 / (K * E), None, ALU.mult))
                link(V.tensor_tensor(g[:, :, :], g[:, :, :], wide(st[:, 0, :]), ALU.subtract))
                link(V.tensor_tensor(sq[:, :, :], g[:, :, :], g[:, :, :], ALU.mult))
                V.tensor_reduce(st[:, 1, :], sq[:, :, :], X, ALU.add).then_inc(s["back"], 1)
                dve.wait_ge(s["root"], 1)
                link(V.reciprocal(st[:, 3, :], st[:, 2, :]))
                link(V.tensor_tensor(g[:, :, :], g[:, :, :], wide(st[:, 3, :]), ALU.mult))
                link(V.tensor_tensor(g[:, :, :], g[:, :, :], all_of(1), ALU.mult))
                link(V.tensor_tensor(g[:, :, :], g[:, :, :], all_of(2), ALU.add))
                link(V.tensor_reduce(scores[:, :, :], g4.rearrange("n b k e -> n b e k"), X, ALU.add))
                V.tensor_scalar(scores[:, :, :], scores[:, :, :], 1.0 / K, None, ALU.mult)


def first_images(nc, x, x_dram):
    loaded = [nc.alloc_semaphore("images_even"), nc.alloc_semaphore("images_odd")]
    with nc.Block() as block:
        @block.sync
        def _(sp):
            for n in range(2):
                sp.dma_start(x[:, n, :], x_dram[2 * n:2 * n + 2].rearrange("i d w h -> (i d) (w h)")).then_inc(loaded[n], 16)
    return loaded


def pool_tokens(nc, tag, x, x_dram, loaded, h, wq, wk, wv, wo, cols, cls, ident):
    H, L, G, R, PAIRS = 8, 64, 64, 4, B // 2
    IH = 2 * H
    with stage(nc, tag, "ones", "masks", "summed", "sums", "regrouped", "meaned", "q_made", "q_saved", "spread", "qk_made", "qk_saved",
               "qb_made", "qb_saved", "scores", "scored", "maxed", "shifted", "exped", "totals", "inverted", "probs",
               "x_turned", "x_saved", "p_turned", "p_saved", "ctx", "ctx_saved", "v_made", "v_saved", "o_made", "out", "passed") as (s, sb, ps):
        xr = sb("xr", [128, 2, G, L])
        xT = sb("xt", [128, 2, 8, R, 128])
        q = sb("q", [128, PAIRS, G])
        qp = sb("qp", [128, 2, G])
        qb = sb("qb", [128, 2, 16])
        mask = sb("mask", [128, 32])
        bmask = sb("bmask", [128, 32])
        qm = sb("qm", [128, G, IH])
        A = sb("a", [128, 2, G, 32])
        z = sb("z", [128, 16, L])
        stat = sb("stat", [128, 3, 16])
        pT = sb("pt", [128, 8, R, 2, IH])
        ctx = sb("ctx", [128, PAIRS, H, G])
        v = sb("v", [128, PAIRS * G])
        psC = ps("c", [128, 2, 512])
        psA = ps("ka", [128, 2, 512])
        psS = ps("s", [128, 2, 512])
        psT = [ps(f"t{p}", [128, 512]) for p in range(2)]
        V = nc.vector

        def pipeline(engine, front, mid, back):
            front(0, 0)
            with engine.Fori(0, PAIRS // 2 - 1) as i:
                for u in range(2):
                    mid(i * 2 + u, u)
                    front(i * 2 + (u + 1), 1 - u)
                    back(i * 2 + u, u)
            n = PAIRS - 2
            mid(n, 0)
            front(n + 1, 1)
            back(n, 0)
            mid(n + 1, 1)
            back(n + 1, 1)

        with nc.Block() as block:
            @block.sync
            def _(sp):
                for n in range(2, PAIRS):
                    sp.wait_ge(s["regrouped"], (n - 1) * 8)
                    sp.dma_start(x[:, n % 2, :], x_dram[2 * n:2 * n + 2].rearrange("i d w h -> (i d) (w h)")).then_inc(loaded[n % 2], 16)

            @block.gpsimd
            def _(pool):
                P = nc.gpsimd
                P.memset(mask[:, :], 1.0).then_inc(s["ones"], 1)
                P.memset(A[:, :, :, :], 0.0)
                P.memset(pT[:, :, :, :, :], 0.0).then_inc(s["ones"], 1)
                pool.wait_ge(s["ones"], 1)
                P.affine_select(out=mask[:, :], in_=mask[:, :], compare_op=ALU.is_ge, fill=0.0, base=0,
                                pattern=[[-8, 32]], channel_multiplier=1).then_inc(s["ones"], 1)
                pool.wait_ge(s["ones"], 3)
                P.affine_select(out=mask[:, :], in_=mask[:, :], compare_op=ALU.is_ge, fill=0.0, base=7,
                                pattern=[[8, 32]], channel_multiplier=-1).then_inc(s["ones"], 1)
                pool.wait_ge(s["ones"], 4)
                P.tensor_scalar(bmask[:, :], mask[:, :], cols[:, 1:2], None, ALU.mult).then_inc(s["masks"], 1)

                def regroup(i, u):
                    wait_alone(pool, loaded[u], i * 16 + 16, s["passed"])
                    for w in range(8):
                        P.tensor_copy(xr[:, u, w * 8:(w + 1) * 8, :].rearrange("p h (a b) -> p h a b", b=8),
                                      x[:, u, w * 512:(w + 1) * 512].rearrange("p (a h b) -> p h a b", a=8, h=8)).then_inc(s["regrouped"], 1)

                pool.wait_ge(s["regrouped"], 8)
                regroup(0, 1)
                with pool.Fori(1, PAIRS // 2) as i:
                    for u in range(2):
                        wait_alone(pool, s["scores"], i * 2 + (u - 1), s["passed"])
                        regroup(i, u)

            @block.tensor
            def _(pe):
                M = nc.tensor.matmul

                def front(n, u):
                    pe.wait_ge(s["meaned"], n + 1)
                    M(psC[:, 0, 0:G], wq, q_at(n), start=True, stop=True).then_inc(s["q_made"], 1)
                    for w in range(8):
                        pe.wait_ge(s["regrouped"], n * 8 + (w + 1))
                        if isinstance(n, int):
                            if n * 8 + w >= 2:
                                pe.wait_ge(s["x_saved"], n * 8 + w - 1)
                        else:
                            pe.wait_ge(s["x_saved"], n * 8 + w - 1)
                        for r in range(R):
                            g = w * 8 + 2 * r
                            mm = nc.tensor.transpose(psT[w % 2][:, r * 128:(r + 1) * 128], xr[:, u, g:g + 2, :], ident[:, :])
                        mm.then_inc(s["x_turned"], 1)
                    pe.wait_ge(s["q_saved"], n + 1)
                    for r in range(R):
                        mm = M(psC[r * 32:(r + 1) * 32, 0, G:G + 16], bmask[:, :], qp[:, u, :].rearrange("d (w r p) -> d r w p", r=R, p=2)[:, r, :, :],
                               start=True, stop=True, tile_position=(0, r * 32))
                    mm.then_inc(s["qb_made"], 1)
                    pe.wait_ge(s["spread"], n + 1)
                    for c in range(2):
                        mm = M(psA[:, c, :], wk, qm[:, c * 32:(c + 1) * 32, :], start=True, stop=True)
                    mm.then_inc(s["qk_made"], 1)

                def mid(n, u):
                    pe.wait_ge(s["qk_saved"], n + 1)
                    for g in range(G):
                        r, j = g % 8 // 2, g // 8 * 2 + g % 2
                        mm = M(psS[r * 32:(r + 1) * 32, j // 8, (j % 8) * L:(j % 8 + 1) * L], A[:, u, g, :], xr[:, u, g, :],
                               start=True, stop=True, tile_position=(0, r * 32))
                    mm.then_inc(s["scores"], 1)

                def back(n, u):
                    pe.wait_ge(s["probs"], n + 1)
                    pe.wait_ge(s["qk_saved"], later(n))
                    for w in range(8):
                        mm = nc.tensor.transpose(psA[:, w // 4, (w % 4) * 128:(w % 4 + 1) * 128], z[:, 2 * w:2 * w + 2, :], ident[:, :])
                    mm.then_inc(s["p_turned"], 1)
                    pe.wait_ge(s["p_saved"], n + 1)
                    pe.wait_ge(s["qb_saved"], later(n))
                    for w in range(8):
                        for r in range(R):
                            at = (w % 4 * R + r) * 2 * IH
                            mm = M(psC[:, w // 4, at:at + 2 * IH], xT[:, u, w, r, :], pT[:, w, r, :, :], start=True, stop=True)
                    mm.then_inc(s["ctx"], 1)
                    pe.wait_ge(s["ctx_saved"], n + 1)

                later = lambda n: n + 2 if not isinstance(n, int) else min(n + 2, PAIRS)
                q_at = lambda n: q[:, n, :] if isinstance(n, int) else q[:, bass.ds(n, 1), :].rearrange("p a g -> p (a g)")
                pe.wait_ge(s["masks"], 1)
                pipeline(pe, front, mid, back)
                for hd in range(H):
                    mm = M(psT[0][:, :].rearrange("p (n g) -> p n g", g=G), wv[:, hd, :], ctx[:, :, hd, :], start=(hd == 0), stop=(hd == H - 1))
                mm.then_inc(s["v_made"], 1)
                pe.wait_ge(s["v_saved"], 1)
                for i in range(2):
                    M(psC[0:D, i, :], wo[:, i * D:(i + 1) * D], v[:, :], start=True, stop=False)
                    M(psC[0:D, i, :], ident[:, i * D:(i + 1) * D], q[:, :, :], start=False, stop=True).then_inc(s["o_made"], 1)

            @block.scalar
            def _(act):
                def x_save(n, u, ws):
                    for w in ws:
                        act.wait_ge(s["x_turned"], n * 8 + (w + 1))
                        nc.scalar.copy(xT[:, u, w, :, :], psT[w % 2][:, :].rearrange("p (r d) -> p r d", r=R)).then_inc(s["x_saved"], 1)

                def front(n, u):
                    x_save(n, u, range(8) if isinstance(n, int) and n == 0 else range(4, 8))
                    act.wait_ge(s["qk_made"], n + 1)
                    nc.scalar.copy(A[:, u, :, 0:IH], psA[:, :, :].rearrange("p c (g h) -> p (c g) h", h=IH)).then_inc(s["qk_saved"], 1)

                def mid(n, u):
                    if not (isinstance(n, int) and n == PAIRS - 1):
                        x_save(n + 1, 1 - u, range(4))
                    act.wait_ge(s["shifted"], n + 1)
                    nc.scalar.activation(z[:, :, :], z[:, :, :], ACT.Exp, scale=8.0 ** -0.5).then_inc(s["exped"], 1)

                def back(n, u):
                    act.wait_ge(s["p_turned"], n + 1)
                    for p in range(2):
                        half = slice(p * L, (p + 1) * L)
                        last = nc.scalar.copy(pT[half, :, :, p, :], psA[half, :, :].rearrange("l c (w r k) -> l (c w) r k", r=R, k=32)[:, :, :, 0:IH])
                    last.then_inc(s["p_saved"], 1)

                act.wait_ge(loaded[0], 16)
                for w in range(8):
                    nc.scalar.copy(xr[:, 0, w * 8:(w + 1) * 8, :].rearrange("p h (a b) -> p h a b", b=8),
                                   x[:, 0, w * 512:(w + 1) * 512].rearrange("p (a h b) -> p h a b", a=8, h=8)).then_inc(s["regrouped"], 1)
                act.wait_ge(s["ones"], 2)
                pipeline(act, front, mid, back)
                act.wait_ge(s["v_made"], 1)
                nc.scalar.activation(v[:, :], psT[0][:, :], ACT.Identity, bias=cols[:, 2:3]).then_inc(s["v_saved"], 1)

            @block.vector
            def _(dve):
                def mean(n, u):
                    dve.wait_ge(s["regrouped"], n * 8 + 8)
                    V.tensor_reduce(q_of(n), xr[:, u, :, :], X, ALU.add).then_inc(s["sums"], 1)
                    dve.wait_ge(s["sums"], n + 1)
                    V.tensor_scalar(q_of(n), q_of(n), 1.0 / L, None, ALU.mult).then_inc(s["meaned"], 1)

                def front(n, u):
                    if isinstance(n, int) and n == 0:
                        mean(n, u)
                    dve.wait_ge(s["q_made"], n + 1)
                    V.tensor_scalar(qp[:, u, :], psC[:, 0, 0:G], cols[:, 0:1], None, ALU.add).then_inc(s["q_saved"], 1)
                    dve.wait_ge(s["q_saved"], n + 1)
                    V.tensor_tensor(qm[:, :, :], qp[:, u, :].unsqueeze(2).to_broadcast([128, G, IH]),
                                    mask[:, 0:IH].unsqueeze(1).to_broadcast([128, G, IH]), ALU.mult).then_inc(s["spread"], 1)
                    dve.wait_ge(s["qb_made"], n + 1)
                    V.tensor_copy(qb[:, u, :], psC[:, 0, G:G + 16]).then_inc(s["qb_saved"], 1)

                wide = lambda t: t.unsqueeze(2).to_broadcast([128, 16, L])

                def mid(n, u):
                    if not (isinstance(n, int) and n == PAIRS - 1):
                        mean(n + 1, 1 - u)
                    dve.wait_ge(s["qb_saved"], n + 1)
                    dve.wait_ge(s["scores"], n + 1)
                    if not (isinstance(n, int) and n == 0):
                        dve.wait_ge(s["p_turned"], n)
                    V.tensor_tensor(z[:, :, :], psS[:, :, :].rearrange("p c (j l) -> p (c j) l", l=L), wide(qb[:, u, :]), ALU.add).then_inc(s["scored"], 1)
                    dve.wait_ge(s["scored"], n + 1)
                    V.tensor_reduce(stat[:, 0, :], z[:, :, :], X, ALU.max).then_inc(s["maxed"], 1)
                    dve.wait_ge(s["maxed"], n + 1)
                    V.tensor_tensor(z[:, :, :], z[:, :, :], wide(stat[:, 0, :]), ALU.subtract).then_inc(s["shifted"], 1)

                def back(n, u):
                    dve.wait_ge(s["exped"], n + 1)
                    V.tensor_reduce(stat[:, 1, :], z[:, :, :], X, ALU.add).then_inc(s["totals"], 1)
                    dve.wait_ge(s["totals"], n + 1)
                    V.reciprocal(stat[:, 2, :], stat[:, 1, :]).then_inc(s["inverted"], 1)
                    dve.wait_ge(s["inverted"], n + 1)
                    V.tensor_tensor(z[:, :, :], z[:, :, :], wide(stat[:, 2, :]), ALU.mult).then_inc(s["probs"], 1)
                    dve.wait_ge(s["ctx"], n + 1)
                    for i in range(2):
                        made = psC[i * 64:(i + 1) * 64, :, :].rearrange("d c (g i h) -> d i h (c g)", i=2, h=H)[:, i, :, :]
                        last = V.tensor_copy(ctx_of(n, i), made)
                    last.then_inc(s["ctx_saved"], 1)

                q_of = lambda n: q[:, n, :] if isinstance(n, int) else q[:, bass.ds(n, 1), :].rearrange("p a g -> p (a g)")
                ctx_of = lambda n, i: (ctx[i * 64:(i + 1) * 64, n, :, :] if isinstance(n, int) else
                                       ctx[i * 64:(i + 1) * 64, bass.ds(n, 1), :, :].rearrange("p a h g -> p (a h) g"))
                dve.wait_ge(s["masks"], 1)
                pipeline(dve, front, mid, back)
                V.tensor_copy(h[:, :].rearrange("d (b n) -> d b n", n=N)[:, :, 0], cls.to_broadcast([D, B])).then_inc(s["out"], 1)
                for i in range(2):
                    dve.wait_ge(s["o_made"], i + 1)
                    V.tensor_scalar(h[:, :].rearrange("d (m i n) -> d i m n", i=2, n=N)[:, i, :, 1:N], psC[0:D, i, :].rearrange("d (m g) -> d m g", g=G),
                                    cols[0:D, 3:4], None, ALU.add).then_inc(s["out"], 1)


def constants(nc, ones, ident, pick, causal, alibi, window, toeplitz, last):
    WS = toeplitz.shape[0]
    EXPERTS = pick.shape[0]
    with stage(nc, "const", "filled", "cut", "chain", "window_filled", "window_loaded", "window_scaled") as (s, sb, ps):
        with nc.Block() as block:
            @block.vector
            def _(dve):
                for a in range(2):
                    rows = slice(a * D, (a + 1) * D)
                    nc.vector.memset(ones[rows, a * D:(a + 1) * D], 1.0 / D)
                    nc.vector.memset(ones[rows, (1 - a) * D:(2 - a) * D], 0.0)

            @block.gpsimd
            def _(pool):
                P = nc.gpsimd
                P.memset(window[:, :], NEG).then_inc(s["window_filled"], 1)
                P.memset(ident[:, :], 0.0).then_inc(s["filled"], 1)
                P.memset(pick[:, :, :], 0.0).then_inc(s["filled"], 1)
                P.memset(causal[:, :], 0.0).then_inc(s["filled"], 1)
                P.iota(alibi[:, :, :], [[0, 8], [1, N]], base=0, channel_multiplier=-1, allow_small_or_imprecise_dtypes=True).then_inc(s["filled"], 1)
                pool.wait_ge(s["filled"], 4)
                P.affine_select(out=ident[:, :], in_=ident[:, :], compare_op=ALU.not_equal, fill=1.0, base=0,
                                pattern=[[-1, 128]], channel_multiplier=1).then_inc(s["cut"], 1)
                P.affine_select(out=pick[:, :, :], in_=pick[:, :, :], compare_op=ALU.not_equal, fill=1.0, base=0,
                                pattern=[[-1, EXPERTS], [0, 128]], channel_multiplier=1).then_inc(s["cut"], 1)
                P.affine_select(out=causal[:, :], in_=causal[:, :], compare_op=ALU.is_ge, fill=NEG, base=0,
                                pattern=[[-1, N]], channel_multiplier=1).then_inc(s["cut"], 1)
                for head in range(8):
                    P.tensor_scalar(alibi[:, head, :], alibi[:, head, :], 0.5 ** (head + 1) * 32.0 ** 0.5, None, ALU.mult).then_inc(s["chain"], 1)
                pool.wait_ge(s["chain"], 8)
                P.affine_select(out=alibi[:, :, :], in_=alibi[:, :, :], compare_op=ALU.is_ge, fill=NEG, base=0,
                                pattern=[[0, 8], [-1, N]], channel_multiplier=1).then_inc(s["cut"], 1)
                pool.wait_ge(s["cut"], 4)
                pool.wait_ge(s["window_loaded"], 32)
                P.tensor_scalar(window[:, :], window[:, :], 8.0 ** 0.5, None, ALU.mult).then_inc(s["window_scaled"], 1)

            @block.sync
            def _(sp):
                sp.wait_ge(s["window_filled"], 1)
                sp.dma_start(window[0:WS, 0:WS], toeplitz).then_inc(s["window_loaded"], 16)
                sp.dma_start(window[WS:N, WS:2 * WS], last).then_inc(s["window_loaded"], 16)


def store(nc, h, out):
    with stage(nc, "store", "stored") as (s, sb, ps):
        with nc.Block() as block:
            @block.sync
            def _(sp):
                sp.dma_start(out, h[:, :]).then_inc(s["stored"], 16)
                sp.wait_ge(s["stored"], 16)


def room(nc, stack, dram, *names):
    return {n: stack.enter_context(nc.sbuf_tensor(f"w_{n}", list(dram[n].shape), F32)) for n in names}


def fetch(nc, dram, to):
    names = list(to)
    loaded = nc.alloc_semaphore("loaded_" + names[0])
    whole = lambda n: to[n][tuple(slice(None) for _ in dram[n].shape)]
    with nc.Block() as block:
        @block.sync
        def _(sp):
            for n in names[0::2]:
                sp.dma_start(whole(n), dram[n]).then_inc(loaded, 16)

        @block.scalar
        def _(act):
            for n in names[1::2]:
                act.dma_start(whole(n), dram[n]).then_inc(loaded, 16)
    return loaded, 16 * len(names)


def arrived(nc, fetched):
    loaded, count = fetched
    with nc.Block() as block:
        @block.sync
        def _(sp):
            sp.wait_ge(loaded, count)
    nc.clear_and_free_semaphores([loaded])
    nc.all_engine_barrier()


def tower(nc, dram, out):
    E = 4
    with stage(nc, "tower") as (_, sb, _ps), ExitStack() as stack:
        h, x = sb("h", [D, T]), sb("x", [D, T])
        ones, ident = sb("ones", [2 * D, 2 * D]), sb("ident", [128, 128])
        pick = sb("pick", [8, 8, 128])
        causal, window = sb("causal", [N, N]), sb("window", [N, 2 * 64])
        wT = sb("wt", [8, T])
        key, hist = sb("key", [128, dram["f2_src"].shape[0] // 128]), sb("hist", [HIGH, LOW])
        w2 = room(nc, stack, dram, "a2_wqk", "a2_wv", "a2_wo", "a2_bo", "f2_wgat", "f2_att", "f2_att_col", "f2_rows", "f2_w1", "f2_b1", "f2_w2", "f2_b2")
        f1 = stack.enter_context(ExitStack())
        w1 = room(nc, f1, dram, "f1_wqpk", "f1_keys", "f1_wq", "f1_wo")
        with ExitStack() as early:
            alibi = early.enter_context(nc.sbuf_tensor("alibi", [N, 8, N], F32))
            wa = room(nc, early, dram, "a0_wq", "a0_wkv", "a0_wo", "a0_bo")
            with ExitStack() as own:
                w = room(nc, own, dram, "tok_wq", "tok_wk", "tok_wv", "tok_wo", "tok_cols", "cls")
                images = own.enter_context(nc.sbuf_tensor("images", [2 * D, 2, 64 * 64], F32))
                loaded = first_images(nc, images, dram["x"])
                fetched, to_a0 = fetch(nc, dram, w), fetch(nc, dram, wa)
                constants(nc, ones, ident, pick, causal, alibi, window, dram["a2_toeplitz"], dram["a2_last"])
                arrived(nc, fetched)
                pool_tokens(nc, "tok", images, dram["x"], loaded, h, w["tok_wq"][:, :], w["tok_wk"][:, :], w["tok_wv"], w["tok_wo"], w["tok_cols"], w["cls"][:, 0:1], ident)
                nc.clear_and_free_semaphores(loaded)
                nc.all_engine_barrier()
            arrived(nc, to_a0)
            w = room(nc, early, dram, "f0_gw", "f0_gb", "f0_sW1", "f0_sW2", "f0_sW3", "f0_sb", "f0_eW1", "f0_eW2", "f0_eW3",
                     "f0_eb1", "f0_eb2", "f0_eb3", "a1_wqk", "a1_wv", "a1_wo", "a1_bo")
            fetched = fetch(nc, dram, w)
            layer_norm(nc, "a0_ln", h, x, ones)
            linear_attention(nc, "a0", x, h, wa["a0_wq"], wa["a0_wkv"], wa["a0_wo"], wa["a0_bo"][:, 0:1])
            layer_norm(nc, "f0_ln", h, x, ones)
            arrived(nc, fetched)
            top2(nc, "f0_top", wT[0:E], ident, E, "softmax of gates", x=x, gw=w["f0_gw"][:, :], gb=w["f0_gb"][:, :])
            each = lambda name: [w[name][:, e, :] for e in range(E)]
            column = lambda name: [w[name][:, e:e + 1] for e in range(E)]
            relu_experts(nc, "f0", x, h, wT[0:E], pick[0:E], [w["f0_sW1"][:, :]] + each("f0_eW1"), [w["f0_sb"][0:D, 0:1]] + column("f0_eb1"),
                         [w["f0_sW2"][:, :]] + each("f0_eW2"), [w["f0_sb"][:, 1:2]] + column("f0_eb2"),
                         [w["f0_sW3"][:, :]] + each("f0_eW3"), w["f0_sb"][0:D, 2:3], w["f0_eb3"][:, :])
            fetched = fetch(nc, dram, w1)
            layer_norm(nc, "a1_ln", h, x, ones)
            attention(nc, "a1", x, h, w["a1_wqk"], w["a1_wv"][:, :], w["a1_wo"], ident, heads=8, hp=32, scale=32.0 ** -0.5,
                      bias=alibi[:, :, :].rearrange("n (b r) c -> n b r c", r=4), bo=w["a1_bo"][:, 0:1])
            arrived(nc, fetched)
        fetched = fetch(nc, dram, w2)
        layer_norm(nc, "f1_ln", h, x, ones)
        kv = f1.enter_context(nc.sbuf_tensor("f1_kv", [128, 8, T], F32))
        product_keys(nc, "f1_keys", x, w1["f1_wqpk"], w1["f1_keys"], dram["f1_table"], kv, ident, dram["f2_src"], dram["f2_dst"], key, hist)
        attention(nc, "f1", x, h, w1["f1_wq"], None, w1["f1_wo"], ident, heads=8, hp=64, scale=64.0 ** -0.5, kv=kv,
                  bias=causal[:, :].unsqueeze(1).unsqueeze(1).to_broadcast([N, 2, 4, N]))
        f1.close()
        arrived(nc, fetched)
        layer_norm(nc, "a2_ln", h, x, ones)
        attention(nc, "a2", x, h, w2["a2_wqk"], w2["a2_wv"][:, :], w2["a2_wo"], ident, heads=8, hp=32, scale=8.0 ** -0.5, keys=128,
                  bo=w2["a2_bo"][:, 0:1], bias=window[:, :].unsqueeze(1).unsqueeze(1).to_broadcast([N, 2, 4, 128]))
        layer_norm(nc, "f2_ln", h, x, ones)
        scores = stack.enter_context(nc.sbuf_tensor("f2_scores", [N, B, E], F32))
        with ExitStack() as graph:
            countT = graph.enter_context(nc.sbuf_tensor("f2_count", [TT, NT, T], F32))
            absent = graph.enter_context(nc.sbuf_tensor("f2_absent", [TT, NT, T], F32))
            edge_counts(nc, "f2_edges", key, hist, ident, countT, absent)
            graph_scores(nc, "f2_gat", x, w2["f2_wgat"][:, :], w2["f2_att"], w2["f2_att_col"][:, 0:1], w2["f2_rows"], ident, pick, countT, absent, scores)
        w3 = room(nc, stack, dram, "a3_wqk", "a3_wv", "a3_wo", "a3_wg", "a3_bg", "a3_cols", "f3_wqk", "f3_wv", "f3_wo", "f3_rope", "f3_cols",
                  "f3_router", "f3_w13", "f3_w2", "f3_w2_rest")
        fetched = fetch(nc, dram, w3)
        top2(nc, "f2_top", wT[0:E], ident, E, "softmax", scores=scores)
        gelu_experts(nc, "f2", x, h, wT[0:E], pick[0:E], w2["f2_w1"], w2["f2_b1"], w2["f2_w2"], w2["f2_b2"][:, :], E, 2 * D)
        xn = stack.enter_context(nc.sbuf_tensor("xn", [D, T], F32))
        gate = stack.enter_context(nc.sbuf_tensor("gate", [128, 2, T], F32))
        layer_norm(nc, "a3_ln", h, x, ones)
        arrived(nc, fetched)
        layer_norm(nc, "a3_ln2", x, xn, ones, gain=w3["a3_cols"][:, 1:2], shift=w3["a3_cols"][:, 2:3])
        gate_values(nc, "a3_gate", x, h, w3["a3_wg"], w3["a3_bg"], gate)
        attention(nc, "a3", xn, h, w3["a3_wqk"], w3["a3_wv"][:, :], w3["a3_wo"], ident, heads=8, hp=32, scale=32.0 ** -0.5,
                  bo=w3["a3_cols"][:, 0:1], gate=gate, over_queries=True)
        layer_norm(nc, "f3_ln", h, x, ones)
        layer_norm(nc, "f3_ln1", x, xn, ones, eps=1e-6, center=False, gain=w3["f3_cols"][:, 0:1])
        attention(nc, "f3_att", xn, x, w3["f3_wqk"], w3["f3_wv"][:, :], w3["f3_wo"], ident, heads=4, hp=32, scale=16.0 ** -0.5, rope=w3["f3_rope"],
                  bias=causal[:, :].unsqueeze(1).unsqueeze(1).to_broadcast([N, 1, 4, N]))
        layer_norm(nc, "f3_ln2", x, xn, ones, eps=1e-6, center=False, gain=w3["f3_cols"][:, 1:2])
        top2(nc, "f3_top", wT, ident, 8, "share", x=xn, gw=w3["f3_router"][:, :])
        silu_experts(nc, "f3", xn, h, x, wT, pick, w3["f3_w13"], w3["f3_w2"], w3["f3_w2_rest"])
        store(nc, h, out)


def blocks(w):
    z = np.zeros((2, D, 2, D), w.dtype)
    z[0, :, 0], z[1, :, 1] = w, w
    return z.reshape(2 * D, 2 * D)


def padded_heads(w, of, size, swap=False):
    z = np.zeros((w.shape[0], len(of), 32), w.dtype)
    for place, head in enumerate(of):
        part = w[:, head * size:(head + 1) * size]
        z[:, place, :size] = np.roll(part, size // 2, axis=1) if swap else part
    return z.reshape(w.shape[0], -1)


def lay_out(inputs):
    g = {n: np.asarray(a) for n, a in inputs.items()}
    out = {"x": g["x"]}
    t = lambda n: g["L0_tok_" + n]
    wv = np.zeros((8, D, D), np.float32)
    for head in range(8):
        wv[head][:, head * 8:head * 8 + 8] = t("Wv").T[:, head * 8:head * 8 + 8]
    out.update(tok_wq=blocks(t("Wq").T), tok_wk=blocks(t("Wk")), tok_wv=np.stack([blocks(w) for w in wv], 1), tok_wo=blocks(t("Wo").T),
               tok_cols=np.tile(np.stack([t(n) for n in ("bq", "bk", "bv", "bo")], 1), (2, 1)), cls=g["cls_tok"].reshape(D, 1))
    w = g["L0_attn_w_qkv"].T
    out.update(a0_wq=w[:, :512].reshape(D, 4, 128), a0_wkv=w[:, 512:].reshape(D, 16, 64), a0_bo=g["L0_attn_b_out"].reshape(D, 1),
               a0_wo=g["L0_attn_w_out"].T.reshape(4, 128, D).transpose(1, 0, 2))
    t = lambda n: g["L0_ffn_" + n]
    sb = np.zeros((128, 3), np.float32)
    sb[:D, 0], sb[:, 1], sb[:D, 2] = t("sb1"), t("sb2"), t("sb3")
    out.update(f0_gw=t("gW"), f0_gb=np.broadcast_to(t("gb"), (N, 4)), f0_sW1=t("sW1"), f0_sW2=t("sW2"), f0_sW3=t("sW3"), f0_sb=sb,
               f0_eW1=t("eW1").transpose(1, 0, 2), f0_eW2=t("eW2").transpose(1, 0, 2), f0_eW3=t("eW3").transpose(1, 0, 2),
               f0_eb1=t("eb1").T, f0_eb2=t("eb2").T, f0_eb3=t("eb3"))
    t = lambda n: g["L1_attn_" + n]
    out.update(a1_wqk=np.stack([t("Wq")[:, :128], t("Wq")[:, 128:], t("Wk")[:, :128], t("Wk")[:, 128:]], 1), a1_wv=t("Wv"),
               a1_wo=t("Wo").reshape(2, 128, D).transpose(1, 0, 2), a1_bo=t("bo").reshape(D, 1))
    t = lambda n: g["L1_ffn_" + n]
    keys, values = t("keys_table").reshape(8, 4096, D), t("values_table").reshape(8, 4096, D)
    table = np.empty((8, 4096, 2 * D), np.float32)
    table[0::2, :, :D], table[0::2, :, D:] = keys[0::2], values[0::2]
    table[1::2, :, :D], table[1::2, :, D:] = values[1::2], keys[1::2]
    out.update(f1_wqpk=t("Wq_pk").reshape(D, 4, 128), f1_keys=t("pk_keys").transpose(0, 2, 3, 1).reshape(4, 128, 64).transpose(1, 0, 2),
               f1_table=table.reshape(-1, 2 * D), f1_wq=t("Wq").reshape(D, 4, 128), f1_wo=t("Wo").reshape(4, 128, D).transpose(1, 0, 2))
    t = lambda n: g["L2_attn_" + n]
    w = t("w_qkv").T
    first, second = range(0, 4), range(4, 8)
    q, k, v = (w[:, n * D:(n + 1) * D] for n in range(3))
    toeplitz = t("rel_bias")[np.arange(64)[None] - np.arange(64)[:, None] + 63]
    wo = np.zeros((4, 32, 2, D), np.float32)
    wo[:, :8] = t("w_proj").T.reshape(2, 4, 8, D).transpose(1, 2, 0, 3)
    out.update(a2_wqk=np.stack([padded_heads(m, heads, 8) for m in (q, k) for heads in (first, second)], 1), a2_wv=padded_heads(v, range(8), 8),
               a2_wo=wo.reshape(128, 2, D), a2_bo=t("b_proj").reshape(D, 1), a2_toeplitz=toeplitz, a2_last=t("rel_bias")[63:].reshape(1, 64))
    t = lambda n: g["L2_ffn_" + n]
    out.update(f2_wgat=t("W_gat"), f2_att=np.broadcast_to(np.stack([t("att_src").reshape(16), t("att_dst").reshape(16)]), (TT, 2, 16)),
               f2_att_col=t("att_src").reshape(16, 1), f2_rows=np.broadcast_to(np.stack([t("b_gat"), t("ln_gamma"), t("ln_beta")]), (N, 3, 16)),
               f2_w1=t("W1").transpose(1, 0, 2), f2_b1=t("b1").T, f2_w2=t("W2").transpose(1, 0, 2), f2_b2=t("b2"),
               f2_src=t("edge_index")[0], f2_dst=t("edge_index")[1])
    t = lambda n: g["L3_attn_" + n]
    w = t("W_qkv").T
    out.update(a3_wqk=w[:, :512].reshape(D, 4, 128), a3_wv=w[:, 512:], a3_wo=t("W_final").T.reshape(2, 128, D).transpose(1, 0, 2),
               a3_wg=t("W_gate").T.reshape(D, 2, 128), a3_bg=t("b_gate").reshape(2, 128).T,
               a3_cols=np.stack([t("b_final"), t("ln_gamma"), t("ln_beta")], 1))
    t = lambda n: g["L3_ffn_" + n]
    own, shared = range(4), (0, 0, 1, 1)
    q, k, v = t("wq").T, t("wk").T, t("wv").T
    wo = np.zeros((4, 32, D), np.float32)
    wo[:, :16] = t("wo").T.reshape(4, 16, D)
    angle = np.outer(np.arange(N, dtype=np.float32), 1.0 / 10000.0 ** (np.arange(0, 16, 2, dtype=np.float32) / 16))
    rope = np.zeros((4, 32, 2, N), np.float32)
    rope[:, 0:8, 0] = rope[:, 8:16, 0] = np.cos(angle).T
    rope[:, 0:8, 1], rope[:, 8:16, 1] = -np.sin(angle).T, np.sin(angle).T
    w13 = np.zeros((2, D, 8, 3, 2, D), np.float32)
    for half, name in enumerate(("w1", "w3")):
        w = t(name).transpose(2, 0, 1)
        for place, first in enumerate((0, 2 * D, D)):
            part = w[:, :, first:first + D]
            w13[half, :, :, place, half, :part.shape[2]] = part
    w2 = t("w2").transpose(2, 0, 1)
    out.update(f3_wqk=np.stack([padded_heads(q, own, 16), padded_heads(k, shared, 16), padded_heads(q, own, 16, True), padded_heads(k, shared, 16, True)], 1),
               f3_wv=padded_heads(v, shared, 16), f3_wo=wo.reshape(128, 1, D), f3_rope=rope.reshape(128, 2, N),
               f3_cols=np.stack([t("ln1_w"), t("ln2_w")], 1), f3_router=t("router_w").T,
               f3_w13=w13.reshape(2 * D, 8, 3, 2 * D), f3_w2=w2[:2 * D], f3_w2_rest=w2[2 * D:])
    return {n: np.ascontiguousarray(a) for n, a in out.items()}


def kernel(**inputs):
    import concourse.bacc as _bacc
    from concourse.bass_utils import run_bass_kernel_spmd as _run

    nc = _bacc.Bacc("TRN2", target_bir_lowering=False, num_devices=1)
    arrays = {f"in_{n}": a for n, a in lay_out(inputs).items()}
    dram = {n[3:]: nc.dram_tensor(n, a.shape, mybir.dt.from_np(a.dtype), kind="ExternalInput").ap() for n, a in arrays.items()}
    out = nc.dram_tensor("tokens_out", (D, T), F32, kind="ExternalOutput").ap()
    tower(nc, dram, out)
    r = _run(nc, [arrays], core_ids=[0])
    return r.results[0]["tokens_out"].T.reshape(B, N, D)
```
